# Optimizing a Trainium2 kernel written in Bass

```python
import numpy as np
import jax
import jax.numpy as jnp

def _softmax(x, axis=-1):
    return jax.nn.softmax(x, axis=axis)

def _gelu(x):
    return jax.nn.gelu(x, approximate=True)

def _silu(x):
    return jax.nn.silu(x)

def _sigmoid(x):
    return jax.nn.sigmoid(x)

def _layernorm(x, axis=-1, eps=1e-05):
    m = jnp.mean(x, axis=axis, keepdims=True)
    v = jnp.var(x, axis=axis, keepdims=True)
    return (x - m) / jnp.sqrt(v + eps)

def _scatter_add(tgt, idx, src, axis=0):
    return tgt.at[idx].add(src)

def _segment_sum(src, seg, n):
    return jax.ops.segment_sum(src, seg, n)
kernel_name = 'mk_seq_postln_d2_jaxref_r8_61a16f'

def setup_inputs(seed: int=0):
    np.random.seed(seed)
    _w = jnp.asarray

    def _L0_attn_setup():
        import jax, jax.numpy as jnp
        import numpy as np
        CHUNK = 32
        NUM_HEADS = 4
        HEAD_K = 32
        HEAD_V = 32
        EPS = 1e-05

        def l2norm(x, eps=1e-06):
            return x * jax.lax.rsqrt(jnp.sum(x * x, axis=-1, keepdims=True) + eps)

        def causal_depthwise_conv(x, w):
            K = w.shape[1]
            l = x.shape[1]
            xp = jnp.pad(x, ((0, 0), (K - 1, 0), (0, 0)))
            return sum((w[:, k] * xp[:, k:k + l, :] for k in range(K)))

        def delta_rule_chunkwise(q, k, v, beta):
            b, h, l, dk = q.shape
            dv = v.shape[-1]
            c = CHUNK
            n = l // c
            q = l2norm(q)
            k = l2norm(k)
            v = v * beta[..., None]
            k_beta = k * beta[..., None]
            resh = lambda x: x.reshape(b, h, n, c, x.shape[-1])
            q, k, v, k_beta = map(resh, (q, k, v, k_beta))
            tri_strict = jnp.tril(jnp.ones((c, c), dtype=q.dtype), -1)
            attn = -(k_beta @ jnp.swapaxes(k, -1, -2)) * tri_strict

            def body(i, a):
                row = a[..., i, :]
                upd = jnp.einsum('bhnj,bhnjk->bhnk', row, a)
                return a.at[..., i, :].add(upd)
            attn = jax.lax.fori_loop(1, c, body, attn)
            attn = attn + jnp.eye(c, dtype=attn.dtype)
            u = attn @ v
            w = attn @ k_beta
            mask_causal = jnp.tril(jnp.ones((c, c), dtype=q.dtype), 0)
            S0 = jnp.zeros((b, h, dk, dv), dtype=q.dtype)
            to_front = lambda x: jnp.moveaxis(x, 2, 0)

            def step(S, inp):
                q_i, k_i, u_i, w_i = inp
                attn_i = q_i @ jnp.swapaxes(k_i, -1, -2) * mask_causal
                u_new = u_i - w_i @ S
                o_i = q_i @ S + attn_i @ u_new
                S = S + jnp.swapaxes(k_i, -1, -2) @ u_new
                return (S, o_i)
            S, o = jax.lax.scan(step, S0, (to_front(q), to_front(k), to_front(u), to_front(w)))
            o = jnp.moveaxis(o, 0, 2).reshape(b, h, l, dv)
            return (o, S)
        key = jax.random.key(seed)
        ks = jax.random.split(key, 12)
        b, l, d = (4, 512, 128)
        sc = 0.02
        return {'hidden_states': jax.random.normal(ks[0], (b, l, d), jnp.float32), 'Wq': jax.random.normal(ks[1], (128, 128), jnp.float32) * sc, 'Wk': jax.random.normal(ks[2], (128, 128), jnp.float32) * sc, 'Wv': jax.random.normal(ks[3], (128, 128), jnp.float32) * sc, 'conv_q': jax.random.normal(ks[4], (128, 4), jnp.float32) * 0.1, 'conv_k': jax.random.normal(ks[5], (128, 4), jnp.float32) * 0.1, 'conv_v': jax.random.normal(ks[6], (128, 4), jnp.float32) * 0.1, 'Wb': jax.random.normal(ks[7], (4, 128), jnp.float32) * sc, 'Wmix': jax.random.normal(ks[8], (4, 128), jnp.float32) * sc, 'norm_w': jnp.ones((32,), jnp.float32), 'Wo': jax.random.normal(ks[9], (128, 128), jnp.float32) * sc}
    _L0_attn_in = _L0_attn_setup()

    def _L0_ffn_setup():
        import jax, jax.numpy as jnp
        import numpy as np
        B, S, H, E, K = (4, 256, 128, 8, 2)
        key = jax.random.key(seed)
        k0, k1, k2, k3 = jax.random.split(key, 4)
        x = jax.random.normal(k0, (B, S, H), dtype=jnp.float32)
        router_w = jax.random.normal(k1, (E, H), dtype=jnp.float32) * np.float32(1.0 / np.sqrt(H))
        xav1 = np.float32(np.sqrt(2.0 / (2 * H + H)))
        w1 = jax.random.normal(k2, (E, 2 * H, H), dtype=jnp.float32) * xav1
        w2 = jax.random.normal(k3, (E, H, 2 * H), dtype=jnp.float32) * xav1
        return {'x': x, 'router_w': router_w, 'w1': w1, 'w2': w2}
    _L0_ffn_in = _L0_ffn_setup()

    def _L1_attn_setup():
        import math
        import jax, jax.numpy as jnp
        import numpy as np
        C = 8.0
        _MIN_RAD, _MAX_RAD = (0.9, 0.999)

        def block_diag_linear(x, w):
            B, T, D = x.shape
            H, bs, _ = w.shape
            xh = x.reshape(B, T, H, bs)
            return jnp.einsum('bthd,hde->bthe', xh, w).reshape(B, T, D)

        def linear_scan(a, b):

            def op(l, r):
                a1, b1 = l
                a2, b2 = r
                return (a1 * a2, a2 * b1 + b2)
            return jax.lax.associative_scan(op, (a, b), axis=1)[1]

        def _reference_tuple_inner(x, a_param, w_in, w_a):
            gate_x = jax.nn.sigmoid(block_diag_linear(x, w_in))
            gate_a = jax.nn.sigmoid(block_diag_linear(x, w_a))
            log_a = -C * jax.nn.softplus(a_param) * gate_a
            a = jnp.exp(log_a)
            multiplier = jnp.sqrt(1.0 - jnp.exp(2.0 * log_a))
            b = multiplier * (gate_x * x)
            y = linear_scan(a, b)
            h_last = y[:, -1, :]
            return (y, h_last)
        key = jax.random.key(seed)
        k1, k2, k3, k4 = jax.random.split(key, 4)
        B, T, D, H = (4, 512, 128, 8)
        bs = D // H
        x = jax.random.normal(k1, (B, T, D), dtype=jnp.float32)
        std = 1.0 / math.sqrt(bs)
        w_in = jax.random.normal(k2, (H, bs, bs), dtype=jnp.float32) * std
        w_a = jax.random.normal(k3, (H, bs, bs), dtype=jnp.float32) * std
        sp = jax.random.uniform(k4, (D,), dtype=jnp.float32, minval=-math.log(_MAX_RAD) / C, maxval=-math.log(_MIN_RAD) / C)
        a_param = jnp.log(jnp.exp(sp) - 1.0 + 1e-08)
        return {'x': x, 'a_param': a_param, 'w_in': w_in, 'w_a': w_a}
    _L1_attn_in = _L1_attn_setup()

    def _L1_ffn_setup():
        import jax, jax.numpy as jnp
        import numpy as np
        D_IN, D_HID = (128, 512)

        def _ternary(key, shape):
            return jax.random.randint(key, shape, -1, 2).astype(jnp.float32)

        def _tlin(x, w, s):
            return jnp.einsum('bsi,oi->bso', x, w) * s
        key = jax.random.key(seed)
        ks = jax.random.split(key, 12)
        inv = lambda fan: 1.0 / np.sqrt(fan).astype(np.float32)
        return {'x': jax.random.normal(ks[0], (4, 256, D_IN), dtype=jnp.float32), 'w1_w': _ternary(ks[1], (D_HID, D_IN)), 'w1_s': jax.random.uniform(ks[2], (D_HID,), dtype=jnp.float32) * inv(D_IN), 'w2_w': _ternary(ks[3], (D_HID, D_IN)), 'w2_s': jax.random.uniform(ks[4], (D_HID,), dtype=jnp.float32) * inv(D_IN), 'h1_w': _ternary(ks[5], (D_HID, D_HID)), 'h1_s': jax.random.uniform(ks[6], (D_HID,), dtype=jnp.float32) * inv(D_HID), 'h2_w': _ternary(ks[7], (D_HID, D_HID)), 'h2_s': jax.random.uniform(ks[8], (D_HID,), dtype=jnp.float32) * inv(D_HID), 'w3_w': _ternary(ks[9], (D_IN, D_HID)), 'w3_s': jax.random.uniform(ks[10], (D_IN,), dtype=jnp.float32) * inv(D_HID)}
    _L1_ffn_in = _L1_ffn_setup()
    _d = {'L0_attn_hidden_states': _L0_attn_in['hidden_states'], 'L0_attn_Wq': _L0_attn_in['Wq'], 'L0_attn_Wk': _L0_attn_in['Wk'], 'L0_attn_Wv': _L0_attn_in['Wv'], 'L0_attn_conv_q': _L0_attn_in['conv_q'], 'L0_attn_conv_k': _L0_attn_in['conv_k'], 'L0_attn_conv_v': _L0_attn_in['conv_v'], 'L0_attn_Wb': _L0_attn_in['Wb'], 'L0_attn_Wmix': _L0_attn_in['Wmix'], 'L0_attn_norm_w': _L0_attn_in['norm_w'], 'L0_attn_Wo': _L0_attn_in['Wo'], 'L0_ffn_router_w': _L0_ffn_in['router_w'], 'L0_ffn_w1': _L0_ffn_in['w1'], 'L0_ffn_w2': _L0_ffn_in['w2'], 'L1_attn_a_param': _L1_attn_in['a_param'], 'L1_attn_w_in': _L1_attn_in['w_in'], 'L1_attn_w_a': _L1_attn_in['w_a'], 'L1_ffn_w1_w': _L1_ffn_in['w1_w'], 'L1_ffn_w1_s': _L1_ffn_in['w1_s'], 'L1_ffn_w2_w': _L1_ffn_in['w2_w'], 'L1_ffn_w2_s': _L1_ffn_in['w2_s'], 'L1_ffn_h1_w': _L1_ffn_in['h1_w'], 'L1_ffn_h1_s': _L1_ffn_in['h1_s'], 'L1_ffn_h2_w': _L1_ffn_in['h2_w'], 'L1_ffn_h2_s': _L1_ffn_in['h2_s'], 'L1_ffn_w3_w': _L1_ffn_in['w3_w'], 'L1_ffn_w3_s': _L1_ffn_in['w3_s']}
    _x0 = _d['L0_attn_hidden_states']
    _d['L0_attn_hidden_states'] = jax.random.normal(jax.random.fold_in(jax.random.key(seed), 1), (4, 1024, 128), dtype=_x0.dtype)
    del _x0
    return _d

def reference(L0_attn_hidden_states, L0_attn_Wq, L0_attn_Wk, L0_attn_Wv, L0_attn_conv_q, L0_attn_conv_k, L0_attn_conv_v, L0_attn_Wb, L0_attn_Wmix, L0_attn_norm_w, L0_attn_Wo, L0_ffn_router_w, L0_ffn_w1, L0_ffn_w2, L1_attn_a_param, L1_attn_w_in, L1_attn_w_a, L1_ffn_w1_w, L1_ffn_w1_s, L1_ffn_w2_w, L1_ffn_w2_s, L1_ffn_h1_w, L1_ffn_h1_s, L1_ffn_h2_w, L1_ffn_h2_s, L1_ffn_w3_w, L1_ffn_w3_s):

    def _L0_attn_ref(hidden_states, Wq, Wk, Wv, conv_q, conv_k, conv_v, Wb, Wmix, norm_w, Wo):
        import jax, jax.numpy as jnp
        import numpy as np
        CHUNK = 32
        NUM_HEADS = 4
        HEAD_K = 32
        HEAD_V = 32
        EPS = 1e-05

        def l2norm(x, eps=1e-06):
            return x * jax.lax.rsqrt(jnp.sum(x * x, axis=-1, keepdims=True) + eps)

        def causal_depthwise_conv(x, w):
            K = w.shape[1]
            l = x.shape[1]
            xp = jnp.pad(x, ((0, 0), (K - 1, 0), (0, 0)))
            return sum((w[:, k] * xp[:, k:k + l, :] for k in range(K)))

        def delta_rule_chunkwise(q, k, v, beta):
            b, h, l, dk = q.shape
            dv = v.shape[-1]
            c = CHUNK
            n = l // c
            q = l2norm(q)
            k = l2norm(k)
            v = v * beta[..., None]
            k_beta = k * beta[..., None]
            resh = lambda x: x.reshape(b, h, n, c, x.shape[-1])
            q, k, v, k_beta = map(resh, (q, k, v, k_beta))
            tri_strict = jnp.tril(jnp.ones((c, c), dtype=q.dtype), -1)
            attn = -(k_beta @ jnp.swapaxes(k, -1, -2)) * tri_strict

            def body(i, a):
                row = a[..., i, :]
                upd = jnp.einsum('bhnj,bhnjk->bhnk', row, a)
                return a.at[..., i, :].add(upd)
            attn = jax.lax.fori_loop(1, c, body, attn)
            attn = attn + jnp.eye(c, dtype=attn.dtype)
            u = attn @ v
            w = attn @ k_beta
            mask_causal = jnp.tril(jnp.ones((c, c), dtype=q.dtype), 0)
            S0 = jnp.zeros((b, h, dk, dv), dtype=q.dtype)
            to_front = lambda x: jnp.moveaxis(x, 2, 0)

            def step(S, inp):
                q_i, k_i, u_i, w_i = inp
                attn_i = q_i @ jnp.swapaxes(k_i, -1, -2) * mask_causal
                u_new = u_i - w_i @ S
                o_i = q_i @ S + attn_i @ u_new
                S = S + jnp.swapaxes(k_i, -1, -2) @ u_new
                return (S, o_i)
            S, o = jax.lax.scan(step, S0, (to_front(q), to_front(k), to_front(u), to_front(w)))
            o = jnp.moveaxis(o, 0, 2).reshape(b, h, l, dv)
            return (o, S)
        x = hidden_states
        b, l, d = x.shape
        h, dk, dv = (NUM_HEADS, HEAD_K, HEAD_V)
        q = jax.nn.silu(causal_depthwise_conv(x @ Wq.T, conv_q))
        k = jax.nn.silu(causal_depthwise_conv(x @ Wk.T, conv_k))
        v = jax.nn.silu(causal_depthwise_conv(x @ Wv.T, conv_v))
        v_token = v.reshape(b, l, h, dv)
        qh = q.reshape(b, l, h, dk).transpose(0, 2, 1, 3)
        kh = k.reshape(b, l, h, dk).transpose(0, 2, 1, 3)
        vh = v_token.transpose(0, 2, 1, 3)
        beta = jax.nn.sigmoid(x @ Wb.T).transpose(0, 2, 1)
        o, S = delta_rule_chunkwise(qh, kh, vh, beta)
        o = o.transpose(0, 2, 1, 3)
        mix = jax.nn.sigmoid(x @ Wmix.T)[..., None]
        o = mix * o + (1.0 - mix) * v_token
        o = o * jax.lax.rsqrt(jnp.mean(o * o, axis=-1, keepdims=True) + EPS) * norm_w
        o = o.reshape(b, l, h * dv) @ Wo.T
        return o

    def _L0_ffn_ref(x, router_w, w1, w2):
        import jax, jax.numpy as jnp
        import numpy as np
        B, S, H, E, K = (4, 256, 128, 8, 2)
        bsz, seq, hidden = x.shape
        n_experts = w1.shape[0]
        tokens = x.reshape(-1, hidden)
        T = tokens.shape[0]
        logits = tokens @ router_w.T
        topv, topi = jax.lax.top_k(logits, K)
        w = jax.nn.softmax(topv, axis=-1).astype(tokens.dtype)
        gate = jnp.zeros((T, n_experts), tokens.dtype).at[jnp.arange(T)[:, None], topi].add(w)
        out = jnp.zeros_like(tokens)
        for e in range(n_experts):
            h = jax.nn.gelu(tokens @ w1[e].T, approximate=False)
            y = h @ w2[e].T
            out = out + gate[:, e:e + 1] * y
        return out.reshape(bsz, seq, hidden)

    def _L1_attn_ref(x, a_param, w_in, w_a):
        import math
        import jax, jax.numpy as jnp
        import numpy as np
        C = 8.0
        _MIN_RAD, _MAX_RAD = (0.9, 0.999)

        def block_diag_linear(x, w):
            B, T, D = x.shape
            H, bs, _ = w.shape
            xh = x.reshape(B, T, H, bs)
            return jnp.einsum('bthd,hde->bthe', xh, w).reshape(B, T, D)

        def linear_scan(a, b):

            def op(l, r):
                a1, b1 = l
                a2, b2 = r
                return (a1 * a2, a2 * b1 + b2)
            return jax.lax.associative_scan(op, (a, b), axis=1)[1]

        def _reference_tuple_inner(x, a_param, w_in, w_a):
            gate_x = jax.nn.sigmoid(block_diag_linear(x, w_in))
            gate_a = jax.nn.sigmoid(block_diag_linear(x, w_a))
            log_a = -C * jax.nn.softplus(a_param) * gate_a
            a = jnp.exp(log_a)
            multiplier = jnp.sqrt(1.0 - jnp.exp(2.0 * log_a))
            b = multiplier * (gate_x * x)
            y = linear_scan(a, b)
            h_last = y[:, -1, :]
            return (y, h_last)
        return _reference_tuple_inner(x, a_param, w_in, w_a)[0]

    def _L1_ffn_ref(x, w1_w, w1_s, w2_w, w2_s, h1_w, h1_s, h2_w, h2_s, w3_w, w3_s):
        import jax, jax.numpy as jnp
        import numpy as np
        D_IN, D_HID = (128, 512)

        def _ternary(key, shape):
            return jax.random.randint(key, shape, -1, 2).astype(jnp.float32)

        def _tlin(x, w, s):
            return jnp.einsum('bsi,oi->bso', x, w) * s
        h = jax.nn.silu(_tlin(x, w1_w, w1_s)) * _tlin(x, w2_w, w2_s)
        h = jax.nn.gelu(_tlin(h, h1_w, h1_s), approximate=False)
        h = jax.nn.gelu(_tlin(h, h2_w, h2_s), approximate=False)
        return _tlin(h, w3_w, w3_s)
    x = L0_attn_hidden_states
    x = _layernorm(x + _L0_attn_ref(x, L0_attn_Wq, L0_attn_Wk, L0_attn_Wv, L0_attn_conv_q, L0_attn_conv_k, L0_attn_conv_v, L0_attn_Wb, L0_attn_Wmix, L0_attn_norm_w, L0_attn_Wo), axis=-1)
    x = _layernorm(x + _L0_ffn_ref(x, L0_ffn_router_w, L0_ffn_w1, L0_ffn_w2), axis=-1)
    x = _layernorm(x + _L1_attn_ref(x, L1_attn_a_param, L1_attn_w_in, L1_attn_w_a), axis=-1)
    x = _layernorm(x + _L1_ffn_ref(x, L1_ffn_w1_w, L1_ffn_w1_s, L1_ffn_w2_w, L1_ffn_w2_s, L1_ffn_h1_w, L1_ffn_h1_s, L1_ffn_h2_w, L1_ffn_h2_s, L1_ffn_w3_w, L1_ffn_w3_s), axis=-1)
    return x

_drawn_inputs = setup_inputs


def setup_inputs(seed=0):
    import zlib

    import numpy as np

    out = dict(_drawn_inputs(seed))
    spreads = {'L0_attn_norm_w': (1.0, 0.2)}
    factors = {'L1_ffn_w1_w': 8.0,
     'L1_ffn_w1_s': 8.0,
     'L1_ffn_w2_w': 8.0,
     'L1_ffn_w2_s': 8.0,
     'L1_ffn_h1_w': 8.0,
     'L1_ffn_h1_s': 8.0,
     'L1_ffn_h2_w': 8.0,
     'L1_ffn_h2_s': 8.0,
     'L1_ffn_w3_w': 8.0,
     'L1_ffn_w3_s': 8.0}
    for name, (base, spread) in spreads.items():
        noise = np.random.default_rng([zlib.crc32(name.encode()), seed]).standard_normal(out[name].shape)
        drawn = base * np.exp(spread * noise) if base else spread * noise
        out[name] = jnp.asarray(drawn.astype(out[name].dtype))
    for name, factor in factors.items():
        out[name] = (out[name] * factor).astype(out[name].dtype)
    return out
```

```python
from contextlib import ExitStack

import numpy as np
import concourse.bass as bass
import concourse.mybir as mybir
from concourse.alu_op_type import AluOpType as ALU

F32 = mybir.dt.float32
U32 = mybir.dt.uint32
ACT = mybir.ActivationFunctionType
AX = mybir.AxisListType

B, L, D = 4, 1024, 128
NH, DK, C = 4, 32, 32
TOK = 128
NT = L // TOK
W = B * TOK
CN = TOK // C
CT = B * CN
NC = NT * CT
TAPS = 4
HALO = TAPS - 1
E, HID = 8, 256
HC = HID // 128
FF = 512
FC = FF // 128
LN_EPS, RMS_EPS, L2_EPS = 1e-5, 1e-5, 1e-6
SK, SQ, SV, SATT, SKT, SVT = range(6)
NPACK = 6
C_ID, C_MEAN, C_HEAD, C_CAUSAL, C_EYE, C_SEL = 0, 128, 256, 384, 416, 448
N_CONST = C_SEL + E * 128
V_S1, V_S2, V_HS1, V_HS2, V_S3, V_NORM, V_AP = 0, 4, 8, 12, 16, 17, 18
V_EPS, V_L2E, N_VEC = 19, 20, 21


def build(nc, io):
    ctx = ExitStack()
    with ctx:
        def sb(name, shape, dt=F32):
            return ctx.enter_context(nc.sbuf_tensor(name, shape, dt))

        def ps(name):
            return ctx.enter_context(nc.psum_tensor(name, [128, 512], F32))

        def sem(name):
            return ctx.enter_context(nc.semaphore(name))

        cst = sb("cst", [128, N_CONST])
        vec = sb("vec", [128, N_VEC])
        ident = cst[:, C_ID:C_ID + 128]
        mean_w = cst[:, C_MEAN:C_MEAN + 128]
        head_w = cst[:, C_HEAD:C_HEAD + 128]
        causal = cst[:, C_CAUSAL:C_CAUSAL + 32]
        eye = cst[:, C_EYE:C_EYE + 32]
        wqkv = sb("wqkv", [128, 3, 128])
        conv = sb("conv", [128, 3, TAPS, 128])
        wtap = sb("wtap", [128, 3, TAPS, 128])
        wsm = sb("wsm", [128, 5, 128])
        wr = sb("wr", [128, E])
        big = sb("big", [128, 2, 4096])
        apm = big[:, 0, :].rearrange("p (j h i) -> p j h i", j=C, h=NH)
        tpr = big[:, 1, :].rearrange("p (i n) -> p i n", i=C)
        tpm = big[:, 1, :].rearrange("p (i h j) -> p h i j", h=NH, i=C)
        w1 = big[:, 0, 0:E * HID]
        w2 = big[:, 0, E * HID:2 * E * HID]
        kkc = sb("kkc", [128, NC, C])
        beta_tok = sb("beta_tok", [128, NC])
        fw1 = sb("fw1", [128, FF]); fw2 = sb("fw2", [128, FF])
        fh1 = sb("fh1", [128, FC, FF]); fh2 = sb("fh2", [128, FC, FF])
        fw3 = sb("fw3", [128, FC, 128])
        pk = sb("pk", [128, CT, NPACK, C])
        xt = sb("xt", [128, B, TOK + HALO])
        xv = xt[:, :, HALO:HALO + TOK]
        tb = sb("tb", [128, B, CN, C])
        spread = sb("spread", [128, 8, NH, C])
        texp = sb("texp", [128, 2, B, NH, C])
        sexp = sb("sexp", [128, B, NH, DK])
        qpc = sb("qpc", [128, B, 2, C])
        t1 = sb("t1", [128, W]); t2 = sb("t2", [128, W]); t3 = sb("t3", [128, W]); t4 = sb("t4", [128, W])
        t5 = sb("t5", [128, W])
        oT = sb("oT", [128, W])
        x1 = sb("x1", [128, W]); acc = sb("acc", [128, W])
        lg = sb("lg", [128, B, E]); mx = sb("mx", [128, B, 8]); mi = sb("mi", [128, B, 8], U32)
        mf = sb("mf", [128, B, 2]); gw = sb("gw", [128, B, 2]); gt2 = sb("gt2", [128, B, 2, E])
        gate = sb("gate", [128, B, E]); gtT = sb("gtT", [E, W]); iota = sb("iota", [128, E])
        gb = sb("gb", [128, W]); hb = sb("hb", [128, HC, W]); yg = sb("yg", [128, W])
        hst = sb("hst", [128, B])
        spv = sb("spv", [128, 12])
        fa = sb("fa", [128, FC, W]); fb = sb("fb", [128, FC, W])
        tmpv = sb("tmpv", [128, 768]); tmpg = sb("tmpg", [128, 256])
        out_sb = sb("out_sb", [128, W])
        bank = [ps(f"bank{i}") for i in range(8)]

        names = """w_in cst_in wtap_done conv_in x_in x_free pk_stored pk_loaded tb_in fw_in
            qkv_proj beta_proj qkv_act sq_done ss_done rs_act kq_done qn_done kv_tok kexp_done gram_done
            beta_tmp beta_tok_done gram_read v_done bt_ready
            kkt_done kkt_read tinit tv_mul tv_step tg_mul tg_step tt_done tt_read
            texp_ready m2_done wu_ready m4_done qp_step os_done s_ready o_copied s_zero
            mixl_done mix_act mx1 mx2 o_ready osq_done oss_done ors_done og_done wo_done
            r_done lg_ready tk1 tk2 tk3 tk4 tk5 th_done tk6 tk7 gate_ready gtp_done gt_ready
            gbp_done gb_ready up_done h_ready dn_done yg_ready acc_ready moe_y iota_in
            lru_proj lru_t lru_a lru_m lru_l lru_mult lru_gx lru_b lru_scan hst_ready sp_step
            g_done u_done g_act glu_ready h1_done h1_ready h2_done h2_ready w3_done out_stored out_ready""".split()
        S = {n: sem(n) for n in names}
        for n in "1234":
            for k in ("y", "mu", "d", "sq", "var", "rs", "x"):
                S[k + n] = sem(f"ln{n}_{k}")

        START = """beta_proj y1 qkv_act bt_ready rs_act gram_read wu_ready qp_step o_copied s_ready yg_ready h_ready gb_ready g_act glu_ready h1_ready h2_ready qn_done v_done beta_tmp ss_done kq_done dn_done gram_done m2_done acc_ready os_done hst_ready pk_stored out_stored""".split()

        def after(name, n):
            return S[name], n + (1 if name in START else 0)

        block = ctx.enter_context(nc.Block())
        V, A, P, G = nc.vector, nc.scalar, nc.tensor, nc.gpsimd

        def rep(ap, axis, n):
            shape = list(ap.shape)
            shape[axis] = n
            return ap.broadcast_to(shape)

        def heads(n):
            return rep(cst[:, C_HEAD:C_HEAD + 128].rearrange("p (o h c) -> p o h c", o=1, h=NH), 1, n)

        @block.sync
        def _(sp):
            sp.dma_start(cst[:, :], io["cst"]).then_inc(S["cst_in"], 16)
            sp.dma_start(wqkv[:, :, :], io["wqkv"]).then_inc(S["conv_in"], 16)
            sp.dma_start(conv[:, :, :, :], io["conv"]).then_inc(S["conv_in"], 16)
            sp.dma_start(vec[:, :], io["vec"]).then_inc(S["w_in"], 16)
            sp.dma_start(wsm[:, :, :], io["wsm"]).then_inc(S["w_in"], 16)
            with sp.Fori(0, NT) as t:
                sp.wait_ge(*after("beta_proj", t))
                sp.dma_start(xt[:, :, :], io["xh"][:, bass.ds(t * B, B), :]).then_inc(S["x_in"], 16)
                sp.wait_ge(*after("gram_read", 2 * t + 2))
                sp.dma_start(io["pack"][:, bass.ds(t * CT, CT), :, :], pk[:, :, 1:, :]).then_inc(S["pk_stored"], 16)
            sp.dma_start(wr[:, :], io["wr"]).then_inc(S["fw_in"], 16)
            sp.dma_start(fw1[:, :], io["fw1"]).then_inc(S["fw_in"], 16)
            sp.dma_start(fw2[:, :], io["fw2"]).then_inc(S["fw_in"], 16)
            sp.dma_start(fh1[:, :, :], io["fh1"]).then_inc(S["fw_in"], 16)
            sp.dma_start(fh2[:, :, :], io["fh2"]).then_inc(S["fw_in"], 16)
            sp.dma_start(fw3[:, :, :], io["fw3"]).then_inc(S["fw_in"], 16)
            sp.dma_start(iota[:, :], io["iota"]).then_inc(S["fw_in"], 16)
            sp.wait_ge(*after("tt_done", 8))
            sp.wait_ge(*after("tv_step", 31))
            sp.wait_ge(*after("tg_step", 31))
            sp.dma_start(w1, io["w1"]).then_inc(S["fw_in"], 16)
            sp.dma_start(w2, io["w2"]).then_inc(S["fw_in"], 16)
            sp.wait_ge(*after("pk_stored", 16 * NT))
            with sp.Fori(0, NT) as t:
                sp.wait_ge(*after("y1", t))
                sp.dma_start(xt[:, :, :], io["xh"][:, bass.ds(t * B, B), :]).then_inc(S["x_in"], 16)
                sp.dma_start(pk[:, :, 1:, :], io["pack"][:, bass.ds(t * CT, CT), :, :]).then_inc(S["pk_loaded"], 16)
                sp.wait_ge(*after("tt_read", 8))
                sp.dma_start(tb[:, :, :, :].rearrange("p b n c -> p (b n) c"),
                             kkc[:, bass.ds(t * CT, CT), :]).then_inc(S["tb_in"], 16)
                sp.wait_ge(*after("x4", t + 1))
                sp.wait_ge(*after("pk_stored", 16 * NT))
                sp.dma_start(io["out"][bass.ds(t, 1), :, :].rearrange("t p n -> (t p) n"), out_sb[:, :])\
                    .then_inc(S["out_stored"], 16)
            sp.wait_ge(*after("out_stored", 16 * NT))

        @block.tensor
        def _(pe):
            def mm(out, lhsT, rhs, start=True, stop=True, skip=False):
                return P.matmul(out, lhsT, rhs, start=start, stop=stop, skip_group_check=skip)

            xm = xv

            pe.wait_ge(*after("wtap_done", 1))
            pe.wait_ge(*after("w_in", 32))
            with pe.Fori(0, NT) as t:
                pe.wait_ge(*after("x_in", 16 * t + 16))
                for m in range(3):
                    pe.wait_ge(*after("qkv_act", 3 * t))
                    for k in range(TAPS):
                        i = mm(bank[m][:, :].rearrange("p (b n) -> p b n", b=B), wtap[:, m, k, :],
                               xt[:, :, k:k + TOK], start=k == 0, stop=k == TAPS - 1)
                    i.then_inc(S["qkv_proj"], 1)
                pe.wait_ge(*after("bt_ready", t))
                mm(bank[3][:, :].rearrange("p (b n) -> p b n", b=B), wsm[:, 0, :], xm).then_inc(S["beta_proj"], 1)
                for m in range(2):
                    pe.wait_ge(*after("sq_done", 2 * t + m + 1))
                    pe.wait_ge(*after("rs_act", 2 * t))
                    mm(bank[4 + m][:, :], head_w, [t1, t2][m][:, :]).then_inc(S["ss_done"], 1)
                for g in range(2):
                    pe.wait_ge(*after("qn_done", t + 1))
                    pe.wait_ge(*after("kexp_done", 2 * t + g + 1))
                    pe.wait_ge(*after("gram_read", 2 * t))
                    for c in range(8):
                        i = mm(bank[6 + g][:, c * 64:(c + 1) * 64], spread[:, c, :, :].rearrange("p h c -> p (h c)"),
                               pk[:, g * 8 + c, SK:SQ + 1, :].rearrange("p s c -> p (s c)"))
                    i.then_inc(S["gram_done"], 1)
            pe.wait_ge(*after("gram_read", 2 * NT))
            for g in range(8):
                if g >= 2:
                    pe.wait_ge(*after("kkt_read", g - 1))
                for j in range(4):
                    i = P.transpose(bank[g % 2][:, j * 128:(j + 1) * 128], kkc[:, :, 4 * g + j], ident)
                i.then_inc(S["kkt_done"], 1)
            pe.wait_ge(*after("tv_step", 31))
            pe.wait_ge(*after("tg_step", 31))
            pe.wait_ge(*after("kkt_read", 8))
            for g in range(8):
                if g >= 2:
                    pe.wait_ge(*after("tt_read", g - 1))
                for j in range(4):
                    i = P.transpose(bank[g % 2][:, j * 128:(j + 1) * 128],
                                    tpr[:, 4 * g + j, :], ident)
                i.then_inc(S["tt_done"], 1)
            pe.wait_ge(*after("tt_read", 8))
            pe.wait_ge(*after("s_zero", 1))
            pe.wait_ge(*after("fw_in", 16 * 9))

            def norm_products(n, y, sq, t):
                pe.wait_ge(*after("y" + n, t + 1))
                mm(bank[3][:, :], mean_w, y[:, :]).then_inc(S["mu" + n], 1)
                pe.wait_ge(*after("sq" + n, t + 1))
                pe.wait_ge(*after("d" + n, t + 1))
                mm(bank[3][:, :], mean_w, sq[:, :]).then_inc(S["var" + n], 1)

            with pe.Fori(0, NT) as t:
                for n in range(CN):
                    pe.wait_ge(*after("texp_ready", CN * t + n + 1))
                    pe.wait_ge(*after("pk_loaded", 16 * t + 16))
                    pe.wait_ge(*after("wu_ready", CN * t + n))
                    for b in range(B):
                        i = mm(bank[0][:, b * 64:(b + 1) * 64], texp[:, n % 2, b, :, :].rearrange("p h c -> p (h c)"),
                               pk[:, b * CN + n, SKT:SVT + 1, :].rearrange("p s c -> p (s c)"))
                    i.then_inc(S["m2_done"], 1)
                    pe.wait_ge(*after("wu_ready", CN * t + n + 1))
                    pe.wait_ge(*after("qp_step", 2 * (CN * t + n)))
                    for b in range(B):
                        i = mm(bank[1][:, b * 64:(b + 1) * 64], spread[:, 2 * b, :, :].rearrange("p h c -> p (h c)"),
                               pk[:, b * CN + n, SATT:SKT + 1, :].rearrange("p s c -> p (s c)"))
                    i.then_inc(S["m4_done"], 1)
                    pe.wait_ge(*after("o_copied", CN * t + n))
                    for b in range(B):
                        mm(bank[2][:, b * 64:(b + 1) * 64], spread[:, 2 * b + 1, :, :].rearrange("p h c -> p (h c)"),
                           pk[:, b * CN + n, SATT:SKT + 1, :].rearrange("p s c -> p (s c)"),
                           start=b == 0, stop=False, skip=True)
                    pe.wait_ge(*after("qp_step", 2 * (CN * t + n + 1)))
                    pe.wait_ge(*after("s_ready", CN * t + n))
                    for b in range(B):
                        i = mm(bank[2][:, b * 64:(b + 1) * 64], sexp[:, b, :, :].rearrange("p h c -> p (h c)"),
                               qpc[:, b, :, :].rearrange("p s c -> p (s c)"), start=False, stop=b == B - 1, skip=True)
                    i.then_inc(S["os_done"], 1)
                pe.wait_ge(*after("x_in", 16 * NT + 16 * t + 16))
                mm(bank[3][:, :].rearrange("p (b n) -> p b n", b=B), wsm[:, 1, :], xm).then_inc(S["mixl_done"], 1)
                pe.wait_ge(*after("osq_done", t + 1))
                pe.wait_ge(*after("mix_act", t + 1))
                mm(bank[3][:, :], head_w, t2[:, :]).then_inc(S["oss_done"], 1)
                pe.wait_ge(*after("og_done", t + 1))
                mm(bank[3][:, :], wsm[:, 2, :], t3[:, :]).then_inc(S["wo_done"], 1)
                norm_products("1", t1, t2, t)
                pe.wait_ge(*after("x1", t + 1))
                for b in range(B):
                    i = mm(bank[7][:, b * E:(b + 1) * E], x1[:, b * TOK:(b + 1) * TOK], wr[:, :])
                i.then_inc(S["r_done"], 1)

                def down(e):
                    pe.wait_ge(*after("h_ready", HC * E * t + HC * (e + 1)))
                    pe.wait_ge(*after("yg_ready", E * t + e))
                    for c in range(HC):
                        i = mm(bank[6][:, :], w2[:, (e * HC + c) * 128:(e * HC + c + 1) * 128], hb[:, c, :],
                               start=c == 0, stop=c == HC - 1)
                    i.then_inc(S["dn_done"], 1)

                for e in range(E):
                    for c in range(HC):
                        pe.wait_ge(*after("h_ready", HC * (E * t + e)))
                        mm(bank[4 + c][:, :], w1[:, e * HID + c * 128:e * HID + (c + 1) * 128], x1[:, :])\
                            .then_inc(S["up_done"], 1)
                    if e == 0:
                        pe.wait_ge(*after("gate_ready", t + 1))
                        for b in range(B):
                            i = mm(bank[7][0:E, b * TOK:(b + 1) * TOK], gate[:, b, :], ident)
                        i.then_inc(S["gtp_done"], 1)
                        pe.wait_ge(*after("gt_ready", t + 1))
                    pe.wait_ge(*after("gb_ready", E * t + e))
                    mm(bank[7][:, :], cst[0:E, C_SEL + e * 128:C_SEL + (e + 1) * 128], gtT[:, :])\
                        .then_inc(S["gbp_done"], 1)
                    down(e)
                norm_products("2", t1, t2, t)
                pe.wait_ge(*after("x2", t + 1))
                mm(bank[4][:, :], wsm[:, 3, :], x1[:, :]).then_inc(S["lru_proj"], 1)
                mm(bank[5][:, :], wsm[:, 4, :], x1[:, :]).then_inc(S["lru_proj"], 1)
                norm_products("3", t1, t2, t)
                pe.wait_ge(*after("x3", t + 1))
                pe.wait_ge(*after("lru_t", 2 * t + 2))
                for c in range(FC):
                    pe.wait_ge(*after("g_act", FC * t + c))
                    mm(bank[4][:, :], fw1[:, c * 128:(c + 1) * 128], x1[:, :]).then_inc(S["g_done"], 1)
                    pe.wait_ge(*after("glu_ready", FC * t + c))
                    mm(bank[5][:, :], fw2[:, c * 128:(c + 1) * 128], x1[:, :]).then_inc(S["u_done"], 1)
                pe.wait_ge(*after("glu_ready", FC * t + FC))
                for o in range(FC):
                    pe.wait_ge(*after("h1_ready", FC * t + max(o - 1, 0)))
                    for c in range(FC):
                        i = mm(bank[4 + o % 2][:, :], fh1[:, c, o * 128:(o + 1) * 128], fa[:, c, :],
                               start=c == 0, stop=c == FC - 1)
                    i.then_inc(S["h1_done"], 1)
                for o in range(FC):
                    pe.wait_ge(*after("h1_ready", FC * t + FC))
                    pe.wait_ge(*after("h2_ready", FC * t + max(o - 1, 0)))
                    for c in range(FC):
                        i = mm(bank[4 + o % 2][:, :], fh2[:, c, o * 128:(o + 1) * 128], fb[:, c, :],
                               start=c == 0, stop=c == FC - 1)
                    i.then_inc(S["h2_done"], 1)
                pe.wait_ge(*after("h2_ready", FC * t + FC))
                for c in range(FC):
                    i = mm(bank[6][:, :], fw3[:, c, :], fa[:, c, :], start=c == 0, stop=c == FC - 1)
                i.then_inc(S["w3_done"], 1)
                norm_products("4", t1, t2, t)

        @block.scalar
        def _(act):
            eps = vec[:, V_EPS:V_EPS + 1]
            l2e = vec[:, V_L2E:V_L2E + 1]
            act.wait_ge(*after("w_in", 32))
            act.wait_ge(*after("sp_step", 1))
            A.activation(spv[:, 1:2], spv[:, 0:1], ACT.Exp, scale=-1.0).then_inc(S["sp_step"], 1)
            with act.Fori(0, NT) as t:
                dst = [t3, t4, t5]
                for m in range(3):
                    act.wait_ge(*after("qkv_proj", 3 * t + m + 1))
                    if m < 2:
                        act.wait_ge(*after("qn_done", t))
                    else:
                        act.wait_ge(*after("v_done", t))
                    A.activation(dst[m][:, :], bank[m][:, :], ACT.Silu).then_inc(S["qkv_act"], 1)
                act.wait_ge(*after("beta_proj", t + 1))
                act.wait_ge(*after("beta_tmp", t))
                A.activation(gb[:, :], bank[3][:, :], ACT.Tanh, scale=0.5).then_inc(S["bt_ready"], 1)
                for m in range(2):
                    act.wait_ge(*after("qkv_act", 3 * t + m + 1))
                    act.wait_ge(*after("ss_done", 2 * t))
                    A.activation([t1, t2][m][:, :], dst[m][:, :], ACT.Square).then_inc(S["sq_done"], 1)
                for m in range(2):
                    act.wait_ge(*after("ss_done", 2 * t + m + 1))
                    act.wait_ge(*after("kq_done", 2 * t))
                    r = [hb[:, 0, :], hb[:, 1, :]][m]
                    A.activation(r, bank[4 + m][:, :], ACT.Ln, bias=l2e).then_inc(S["rs_act"], 1)
                for m in range(2):
                    r = [hb[:, 0, :], hb[:, 1, :]][m]
                    act.wait_ge(*after("rs_act", 2 * t + m + 1))
                    A.activation(r, r, ACT.Exp, scale=-0.5).then_inc(S["beta_tok_done"], 1)
            for g in range(8):
                act.wait_ge(*after("kkt_done", g + 1))
                A.activation(apm[:, 4 * g:4 * g + 4, :, :].rearrange("p j h i -> p (j h i)"), bank[g % 2][:, :],
                             ACT.Copy).then_inc(S["kkt_read"], 1)

            def norm_act(n, t):
                act.wait_ge(*after("d" + n, t + 1))
                A.activation(t2[:, :], t1[:, :], ACT.Square).then_inc(S["sq" + n], 1)
                act.wait_ge(*after("var" + n, t + 1))
                A.activation(t4[:, :], bank[3][:, :], ACT.Ln, bias=eps).then_inc(S["rs" + n], 1)
                act.wait_ge(*after("rs" + n, 2 * t + 1))
                A.activation(t4[:, :], t4[:, :], ACT.Exp, scale=-0.5).then_inc(S["rs" + n], 1)

            with act.Fori(0, NT) as t:
                act.wait_ge(*after("mixl_done", t + 1))
                A.activation(t4[:, :], bank[3][:, :], ACT.Tanh, scale=0.5).then_inc(S["mix_act"], 1)
                act.wait_ge(*after("o_ready", t + 1))
                A.activation(t2[:, :], t1[:, :], ACT.Square).then_inc(S["osq_done"], 1)
                act.wait_ge(*after("oss_done", t + 1))
                A.activation(t5[:, :], bank[3][:, :], ACT.Ln, scale=1.0 / DK, bias=eps).then_inc(S["ors_done"], 1)
                act.wait_ge(*after("ors_done", 2 * t + 1))
                A.activation(t5[:, :], t5[:, :], ACT.Exp, scale=-0.5).then_inc(S["ors_done"], 1)
                norm_act("1", t)
                act.wait_ge(*after("tk3", t + 1))
                A.activation(gw[:, :, 0], gw[:, :, 1], ACT.Tanh, scale=0.5).then_inc(S["th_done"], 1)
                for e in range(E):
                    for c in range(HC):
                        act.wait_ge(*after("up_done", HC * (E * t + e) + c + 1))
                        act.wait_ge(*after("dn_done", E * t + e))
                        A.activation(hb[:, c, :], bank[4 + c][:, :], ACT.Gelu).then_inc(S["h_ready"], 1)
                    act.wait_ge(*after("gbp_done", E * t + e + 1))
                    act.wait_ge(*after("yg_ready", E * t + e))
                    A.activation(gb[:, :], bank[7][:, :], ACT.Copy).then_inc(S["gb_ready"], 1)
                norm_act("2", t)
                act.wait_ge(*after("lru_proj", 2 * t + 1))
                A.activation(t1[:, :], bank[4][:, :], ACT.Tanh, scale=0.5).then_inc(S["lru_t"], 1)
                act.wait_ge(*after("lru_proj", 2 * t + 2))
                A.activation(t2[:, :], bank[5][:, :], ACT.Tanh, scale=0.5).then_inc(S["lru_t"], 1)
                act.wait_ge(*after("lru_t", 2 * t + 2))
                A.activation(t3[:, :], t2[:, :], ACT.Exp, scale=spv[:, 10:11], bias=spv[:, 10:11]).then_inc(S["lru_a"], 1)
                A.activation(t4[:, :], t2[:, :], ACT.Exp, scale=spv[:, 11:12], bias=spv[:, 11:12]).then_inc(S["lru_a"], 1)
                act.wait_ge(*after("lru_m", t + 1))
                A.activation(t4[:, :], t4[:, :], ACT.Ln, scale=-1.0).then_inc(S["lru_l"], 1)
                act.wait_ge(*after("lru_l", t + 1))
                A.activation(t4[:, :], t4[:, :], ACT.Exp, scale=0.5).then_inc(S["lru_mult"], 1)
                norm_act("3", t)
                for c in range(FC):
                    act.wait_ge(*after("g_done", FC * t + c + 1))
                    act.wait_ge(*after("glu_ready", FC * t + c))
                    A.activation(t2[:, :], bank[4][:, :], ACT.Silu, scale=vec[:, V_S1 + c:V_S1 + c + 1])\
                        .then_inc(S["g_act"], 1)
                for o in range(FC):
                    act.wait_ge(*after("h1_done", FC * t + o + 1))
                    A.activation(fb[:, o, :], bank[4 + o % 2][:, :], ACT.Gelu, scale=vec[:, V_HS1 + o:V_HS1 + o + 1])\
                        .then_inc(S["h1_ready"], 1)
                for o in range(FC):
                    act.wait_ge(*after("h2_done", FC * t + o + 1))
                    act.wait_ge(*after("h1_done", FC * t + FC))
                    A.activation(fa[:, o, :], bank[4 + o % 2][:, :], ACT.Gelu, scale=vec[:, V_HS2 + o:V_HS2 + o + 1])\
                        .then_inc(S["h2_ready"], 1)
                norm_act("4", t)

        @block.gpsimd
        def _(pool):
            for name in START:
                pool.sem_inc(S[name], 1)
            pool.wait_ge(*after("cst_in", 16))
            pool.wait_ge(*after("conv_in", 32))
            for m in range(3):
                for k in range(TAPS):
                    i = G.tensor_tensor(wtap[:, m, k, :], wqkv[:, m, :], conv[:, m, k, :], ALU.mult)
            i.then_inc(S["wtap_done"], 1)
            with pool.Fori(0, NT) as t:
                for g in range(2):
                    pool.wait_ge(*after("qn_done", t + 1))
                    pool.wait_ge(*after("gram_done", 2 * t + g))
                    G.tensor_tensor(spread[:, :, :, :],
                                    rep(pk[:, g * 8:(g + 1) * 8, SK:SK + 1, :], 2, NH),
                                    heads(8), ALU.mult).then_inc(S["kexp_done"], 1)
            pool.wait_ge(*after("kkt_read", 8))
            pool.wait_ge(*after("tinit", 2))
            for j in range(C - 1):
                n, k = C - 1 - j, j + 1
                a = rep(apm[:, j, 3:4, j + 1:C].rearrange("p h (i o) -> p h i o", o=1), 3, k)
                r = rep(tpm[:, 3:4, j:j + 1, 0:k], 2, n)
                m = tmpg[:, 0:n * k].rearrange("p (h i k) -> p h i k", h=1, i=n)
                if j:
                    pool.wait_ge(*after("tg_step", j))
                G.tensor_tensor(m, a, r, ALU.mult).then_inc(S["tg_mul"], 1)
                pool.wait_ge(*after("tg_mul", j + 1))
                o = tpm[:, 3:4, j + 1:C, 0:k]
                G.tensor_tensor(o, o, m, ALU.subtract).then_inc(S["tg_step"], 1)
            with pool.Fori(0, NT) as t:
                for n in range(CN):
                    pool.wait_ge(*after("tb_in", 16 * t + 16))
                    pool.wait_ge(*after("m2_done", CN * t + max(n - 1, 0)))
                    G.tensor_tensor(texp[:, n % 2, :, :, :], rep(tb[:, :, n:n + 1, :], 2, NH), heads(B), ALU.mult)\
                        .then_inc(S["texp_ready"], 1)
                for e in range(E):
                    pool.wait_ge(*after("yg_ready", E * t + e + 1))
                    if e:
                        pool.wait_ge(*after("acc_ready", E * t + e))
                    G.tensor_tensor(acc[:, :], (acc if e else x1)[:, :], yg[:, :], ALU.add).then_inc(S["acc_ready"], 1)

        @block.vector
        def _(dve):
            tt, ts, stt = V.tensor_tensor, V.tensor_scalar, V.scalar_tensor_tensor
            V.memset(big[:, 1, :], 0.0).then_inc(S["tinit"], 1)
            dve.wait_ge(*after("tinit", 1))
            for h in range(NH):
                i = V.memset(big[:, 1, h * C:C * NH * C:NH * C + 1], 1.0)
            i.then_inc(S["tinit"], 1)
            V.memset(sexp[:, :, :, :], 0.0)
            V.memset(hst[:, :], 0.0).then_inc(S["s_zero"], 1)
            dve.wait_ge(*after("w_in", 32))
            n_sp = [0]
            ap = vec[:, V_AP:V_AP + 1]

            def sp_op(i):
                i.then_inc(S["sp_step"], 1)
                n_sp[0] += 1
                dve.wait_ge(*after("sp_step", n_sp[0]))

            col = lambda k: spv[:, k:k + 1]
            stt(col(0), ap, -1.0, ap, ALU.mult, ALU.max).then_inc(S["sp_step"], 1)
            n_sp[0] = 2
            dve.wait_ge(*after("sp_step", 2))
            sp_op(ts(col(2), col(1), 2.0, None, ALU.add))
            sp_op(V.reciprocal(col(3), col(2)))
            sp_op(tt(col(4), col(1), col(3), ALU.mult))
            sp_op(tt(col(5), col(4), col(4), ALU.mult))
            sp_op(ts(col(6), col(5), 1.0 / 17, 1.0 / 15, ALU.mult, ALU.add))
            for k in (13, 11, 9, 7, 5, 3, 1):
                sp_op(tt(col(7), col(6), col(5), ALU.mult))
                sp_op(ts(col(6), col(7), 1.0 / k, None, ALU.add))
            sp_op(tt(col(7), col(6), col(4), ALU.mult))
            sp_op(ts(col(8), ap, 0.0, None, ALU.max))
            sp_op(stt(col(9), col(7), 2.0, col(8), ALU.mult, ALU.add))
            sp_op(ts(col(10), col(9), -4.0, None, ALU.mult))
            sp_op(ts(col(11), col(9), -8.0, None, ALU.mult))
            with dve.Fori(0, NT) as t:
                dve.wait_ge(*after("pk_stored", 16 * t))
                src = [t3, t4]
                for m in range(2):
                    dve.wait_ge(*after("beta_tok_done", 2 * t + m + 1))
                    if m == 0:
                        dve.wait_ge(*after("gram_done", 2 * t))
                    tt(pk[:, :, SK + m, :], src[m][:, :].rearrange("p (c i) -> p c i", c=CT),
                       hb[:, m, :].rearrange("p (c i) -> p c i", c=CT), ALU.mult).then_inc(S["kq_done"], 1)
                dve.wait_ge(*after("kq_done", 2 * t + 2))
                V.transpose(pk[:, :, SKT, :], pk[:, :, SK, :]).then_inc(S["kv_tok"], 1)
                V.memset(tmpv[:, 0:1], 0.0).then_inc(S["qn_done"], 1)
                dve.wait_ge(*after("qkv_act", 3 * t + 3))
                V.transpose(pk[:, :, SVT, :], t5[:, :].rearrange("p (c i) -> p c i", c=CT)).then_inc(S["kv_tok"], 1)
                V.tensor_copy(pk[:, :, SV, :], t5[:, :].rearrange("p (c i) -> p c i", c=CT)).then_inc(S["v_done"], 1)
                dve.wait_ge(*after("bt_ready", t + 1))
                V.transpose(yg[:, :], gb[:, :]).then_inc(S["beta_tmp"], 1)
                dve.wait_ge(*after("beta_tmp", t + 1))
                ts(beta_tok[:, bass.ds(t * CT, CT)], yg[:, 0:W:C], 0.5, 0.5, ALU.mult, ALU.add).then_inc(S["mx1"], 1)
                dve.wait_ge(*after("mx1", t + 1))
                V.tensor_copy(mf[:, 0:1, 0], tmpv[:, 0:1])
                for g in range(2):
                    bk = bank[6 + g][:, :].rearrange("p (c s i) -> p c s i", c=8, s=2)
                    dve.wait_ge(*after("gram_done", 2 * t + g + 1))
                    tt(pk[:, g * 8:(g + 1) * 8, SATT, :], bk[:, :, 1, :],
                       rep(causal.rearrange("p (o i) -> p o i", o=1), 1, 8), ALU.mult)
                    tt(kkc[:, bass.ds(t * CT + g * 8, 8), :], bk[:, :, 0, :],
                       rep(beta_tok[:, bass.ds(t * CT + g * 8, 8)].rearrange("p (c o) -> p c o", o=1), 2, C),
                       ALU.mult).then_inc(S["gram_read"], 1)
            dve.wait_ge(*after("kkt_read", 8))
            for j in range(C - 1):
                n, k = C - 1 - j, j + 1
                a = rep(apm[:, j, 0:3, j + 1:C].rearrange("p h (i o) -> p h i o", o=1), 3, k)
                r = rep(tpm[:, 0:3, j:j + 1, 0:k], 2, n)
                m = tmpv[:, 0:3 * n * k].rearrange("p (h i k) -> p h i k", h=3, i=n)
                if j:
                    dve.wait_ge(*after("tv_step", j))
                tt(m, a, r, ALU.mult).then_inc(S["tv_mul"], 1)
                dve.wait_ge(*after("tv_mul", j + 1))
                o = tpm[:, 0:3, j + 1:C, 0:k]
                tt(o, o, m, ALU.subtract).then_inc(S["tv_step"], 1)
            for g in range(8):
                dve.wait_ge(*after("tt_done", g + 1))
                tt(kkc[:, :, 4 * g:4 * g + 4].rearrange("p c i -> p i c"),
                   bank[g % 2][:, :].rearrange("p (i c) -> p i c", i=4),
                   rep(beta_tok[:, :].rearrange("p (o c) -> p o c", o=1), 1, 4), ALU.mult).then_inc(S["tt_read"], 1)

            def norm_vec(n, t, out):
                dve.wait_ge(*after("mu" + n, t + 1))
                dve.wait_ge(*after("y" + n, t + 1))
                tt(t1[:, :], t1[:, :], bank[3][:, :], ALU.subtract).then_inc(S["d" + n], 1)
                dve.wait_ge(*after("rs" + n, 2 * t + 2))
                dve.wait_ge(*after("d" + n, t + 1))
                tt(out[:, :], t1[:, :], t4[:, :], ALU.mult).then_inc(S["x" + n], 1)

            with dve.Fori(0, NT) as t:
                for n in range(CN):
                    k = CN * t + n
                    dve.wait_ge(*after("m2_done", k + 1))
                    dve.wait_ge(*after("os_done", k))
                    tt(spread[:, :, :, :],
                       rep(bank[0][:, 0:256].rearrange("p (s o c) -> p s o c", s=8, o=1), 2, NH),
                       heads(8), ALU.mult).then_inc(S["wu_ready"], 1)
                    dve.wait_ge(*after("m4_done", k + 1))
                    bk = bank[1][:, 0:256].rearrange("p (b s c) -> p b s c", b=B, s=2)
                    tt(qpc[:, :, 0, :], pk[:, n:CT:CN, SQ, :], bk[:, :, 0, :], ALU.subtract).then_inc(S["qp_step"], 1)
                    tt(qpc[:, :, 1, :], rep(eye.rearrange("p (o c) -> p o c", o=1), 1, B), bk[:, :, 1, :],
                       ALU.subtract).then_inc(S["qp_step"], 1)
                    dve.wait_ge(*after("os_done", k + 1))
                    ob = bank[2][:, 0:256].rearrange("p (b s c) -> p b s c", b=B, s=2)
                    for h in range(NH):
                        i = V.transpose(sexp[32 * h:32 * h + 32, :, h, :], ob[32 * h:32 * h + 32, :, 1, :])
                    i.then_inc(S["s_ready"], 1)
                    V.tensor_copy(oT[:, :].rearrange("p (b n c) -> p b n c", b=B, n=CN)[:, :, n, :], ob[:, :, 0, :])\
                        .then_inc(S["o_copied"], 1)
                vT = pk[:, :, SV, :]
                cc = lambda a: a[:, :].rearrange("p (c i) -> p c i", c=CT)
                dve.wait_ge(*after("o_copied", CN * t + CN))
                tt(cc(t3), cc(oT), vT, ALU.subtract).then_inc(S["mx2"], 1)
                dve.wait_ge(*after("mix_act", t + 1))
                dve.wait_ge(*after("mx2", 2 * t + 1))
                stt(t3[:, :], t4[:, :], 1.0, t3[:, :], ALU.add, ALU.mult).then_inc(S["mx2"], 1)
                dve.wait_ge(*after("mx2", 2 * t + 2))
                stt(cc(t1), cc(t3), 0.5, vT, ALU.mult, ALU.add).then_inc(S["o_ready"], 1)
                dve.wait_ge(*after("ors_done", 2 * t + 2))
                dve.wait_ge(*after("o_ready", t + 1))
                stt(t3[:, :], t1[:, :], vec[:, V_NORM:V_NORM + 1], t5[:, :], ALU.mult, ALU.mult).then_inc(S["og_done"], 1)
                dve.wait_ge(*after("wo_done", t + 1))
                tt(t1[:, :].rearrange("p (b n) -> p b n", b=B), bank[3][:, :].rearrange("p (b n) -> p b n", b=B), xv,
                   ALU.add).then_inc(S["y1"], 1)
                norm_vec("1", t, x1)
                dve.wait_ge(*after("r_done", t + 1))
                V.tensor_copy(lg[:, :, :], bank[7][:, 0:B * E].rearrange("p (b e) -> p b e", b=B)).then_inc(S["lg_ready"], 1)
                dve.wait_ge(*after("lg_ready", t + 1))
                V.memset(mf[:, :, :], 0.0)
                for b in range(B):
                    i = V.max(mx[:, b, :], lg[:, b, :])
                i.then_inc(S["tk1"], 1)
                dve.wait_ge(*after("tk1", t + 1))
                tt(gw[:, :, 1], mx[:, :, 0], mx[:, :, 1], ALU.subtract).then_inc(S["tk3"], 1)
                for b in range(B):
                    i = V.max_index(mi[:, b, :], mx[:, b, :], lg[:, b, :])
                i.then_inc(S["tk2"], 1)
                dve.wait_ge(*after("tk2", t + 1))
                V.tensor_copy(mf[:, :, :], mi[:, :, 0:2]).then_inc(S["tk4"], 1)
                dve.wait_ge(*after("tk4", t + 1))
                for s in range(2):
                    i = tt(gt2[:, :, s, :], rep(iota[:, :].rearrange("p (o e) -> p o e", o=1), 1, B),
                           rep(mf[:, :, s:s + 1], 2, E), ALU.is_equal)
                i.then_inc(S["tk5"], 1)
                dve.wait_ge(*after("th_done", t + 1))
                ts(gw[:, :, 1], gw[:, :, 0], -0.5, 0.5, ALU.mult, ALU.add).then_inc(S["tk6"], 1)
                dve.wait_ge(*after("tk6", 2 * t + 1))
                ts(gw[:, :, 0], gw[:, :, 0], 0.5, 0.5, ALU.mult, ALU.add).then_inc(S["tk6"], 1)
                dve.wait_ge(*after("tk6", 2 * t + 2))
                dve.wait_ge(*after("tk5", t + 1))
                for s in range(2):
                    i = tt(gt2[:, :, s, :], gt2[:, :, s, :], rep(gw[:, :, s:s + 1], 2, E), ALU.mult)
                i.then_inc(S["tk7"], 1)
                dve.wait_ge(*after("tk7", t + 1))
                tt(gate[:, :, :], gt2[:, :, 0, :], gt2[:, :, 1, :], ALU.add).then_inc(S["gate_ready"], 1)
                dve.wait_ge(*after("gtp_done", t + 1))
                V.tensor_copy(gtT[:, :], bank[7][0:E, :]).then_inc(S["gt_ready"], 1)
                for e in range(E):
                    dve.wait_ge(*after("dn_done", E * t + e + 1))
                    dve.wait_ge(*after("gb_ready", E * t + e + 1))
                    dve.wait_ge(*after("acc_ready", E * t + e))
                    tt(yg[:, :], bank[6][:, :], gb[:, :], ALU.mult).then_inc(S["yg_ready"], 1)
                dve.wait_ge(*after("acc_ready", E * t + E))
                V.tensor_copy(t1[:, :], acc[:, :]).then_inc(S["y2"], 1)
                norm_vec("2", t, x1)
                dve.wait_ge(*after("lru_a", 2 * t + 2))
                ts(t4[:, :], t4[:, :], 1.0, -1e-19, ALU.subtract, ALU.min).then_inc(S["lru_m"], 1)
                dve.wait_ge(*after("x2", t + 1))
                stt(t1[:, :], t1[:, :], 1.0, x1[:, :], ALU.add, ALU.mult).then_inc(S["lru_gx"], 1)
                dve.wait_ge(*after("lru_mult", t + 1))
                dve.wait_ge(*after("lru_gx", t + 1))
                stt(t1[:, :], t1[:, :], 0.5, t4[:, :], ALU.mult, ALU.mult).then_inc(S["lru_b"], 1)
                dve.wait_ge(*after("lru_b", t + 1))
                dve.wait_ge(*after("hst_ready", t))
                for b in range(B):
                    c = slice(b * TOK, (b + 1) * TOK)
                    i = V.tensor_tensor_scan(t2[:, c], t3[:, c], t1[:, c], hst[:, b:b + 1], ALU.mult, ALU.add)
                i.then_inc(S["lru_scan"], 1)
                dve.wait_ge(*after("lru_scan", t + 1))
                V.tensor_copy(hst[:, :], t2[:, TOK - 1:W:TOK]).then_inc(S["hst_ready"], 1)
                tt(t1[:, :], t2[:, :], x1[:, :], ALU.add).then_inc(S["y3"], 1)
                norm_vec("3", t, x1)
                for c in range(FC):
                    dve.wait_ge(*after("g_act", FC * t + c + 1))
                    dve.wait_ge(*after("u_done", FC * t + c + 1))
                    stt(fa[:, c, :], bank[5][:, :], vec[:, V_S2 + c:V_S2 + c + 1], t2[:, :], ALU.mult, ALU.mult)\
                        .then_inc(S["glu_ready"], 1)
                dve.wait_ge(*after("w3_done", t + 1))
                dve.wait_ge(*after("x3", t + 1))
                stt(t1[:, :], bank[6][:, :], vec[:, V_S3:V_S3 + 1], x1[:, :], ALU.mult, ALU.add).then_inc(S["y4"], 1)
                dve.wait_ge(*after("out_stored", 16 * t))
                norm_vec("4", t, out_sb)


def _layout(a):
    f = lambda n: np.asarray(a[n], dtype=np.float32)
    T = lambda m: np.ascontiguousarray(m.T)
    x = f("L0_attn_hidden_states")
    xp = np.pad(x, ((0, 0), (HALO, 0), (0, 0)))
    xh = np.stack([xp[b, t * TOK:t * TOK + TOK + HALO].T for t in range(NT) for b in range(B)], axis=1)
    order = ("k", "q", "v")
    wqkv = np.stack([f(f"L0_attn_W{m}").T for m in order], axis=1)
    conv = np.stack([np.broadcast_to(f(f"L0_attn_conv_{m}").T[None], (128, TAPS, 128)) for m in order], axis=1)
    rep = lambda m: np.repeat(m, DK, axis=0).T

    def blocks(w):
        out = np.zeros((128, 128), np.float32)
        s = w.shape[1]
        for h in range(w.shape[0]):
            out[h * s:(h + 1) * s, h * s:(h + 1) * s] = w[h]
        return out

    wsm = np.stack([rep(f("L0_attn_Wb")), rep(f("L0_attn_Wmix")), f("L0_attn_Wo").T,
                    blocks(f("L1_attn_w_in")), blocks(f("L1_attn_w_a"))], axis=1)
    p = np.arange(128)
    cst = np.zeros((128, N_CONST), np.float32)
    cst[:, C_ID:C_ID + 128] = np.eye(128)
    cst[:, C_MEAN:C_MEAN + 128] = 1.0 / D
    cst[:, C_HEAD:C_HEAD + 128] = (p[:, None] // DK) == (p[None] // DK)
    cst[:, C_CAUSAL:C_CAUSAL + 32] = np.arange(32)[None] >= (p[:, None] % 32)
    cst[:, C_EYE:C_EYE + 32] = np.arange(32)[None] == (p[:, None] % 32)
    for e in range(E):
        cst[e, C_SEL + e * 128:C_SEL + (e + 1) * 128] = 1.0
    vec = np.zeros((128, N_VEC), np.float32)
    cols = lambda v: v.reshape(-1, 128).T
    vec[:, V_S1:V_S1 + FC] = cols(f("L1_ffn_w1_s"))
    vec[:, V_S2:V_S2 + FC] = cols(f("L1_ffn_w2_s"))
    vec[:, V_HS1:V_HS1 + FC] = cols(f("L1_ffn_h1_s"))
    vec[:, V_HS2:V_HS2 + FC] = cols(f("L1_ffn_h2_s"))
    vec[:, V_S3:V_S3 + 1] = cols(f("L1_ffn_w3_s"))
    vec[:, V_NORM] = np.tile(f("L0_attn_norm_w"), NH)
    vec[:, V_AP] = f("L1_attn_a_param")
    vec[:, V_EPS] = LN_EPS
    vec[:, V_L2E] = L2_EPS
    w1 = f("L0_ffn_w1").transpose(2, 0, 1).reshape(128, E * HID)
    w2 = f("L0_ffn_w2").reshape(E, 128, HC, 128).transpose(3, 0, 2, 1).reshape(128, E * HC * 128)
    kc = lambda w: w.T.reshape(FC, 128, -1).transpose(1, 0, 2)
    ins = dict(xh=xh, wqkv=wqkv, conv=conv, wsm=wsm, cst=cst, vec=vec, wr=f("L0_ffn_router_w").T, w1=w1, w2=w2,
               fw1=f("L1_ffn_w1_w").T, fw2=f("L1_ffn_w2_w").T, fh1=kc(f("L1_ffn_h1_w")), fh2=kc(f("L1_ffn_h2_w")),
               fw3=kc(f("L1_ffn_w3_w")), iota=np.broadcast_to(np.arange(E, dtype=np.float32), (128, E)))
    return {n: np.ascontiguousarray(v) for n, v in ins.items()}


def program(nc, ins):
    io = {n: nc.dram_tensor(f"in_{n}", v.shape, F32, kind="ExternalInput").ap() for n, v in ins.items()}
    io["out"] = nc.dram_tensor("out_0", (NT, 128, W), F32, kind="ExternalOutput").ap()
    io["pack"] = nc.dram_tensor("pack", (128, NC, NPACK - 1, C), F32, kind="Internal").ap()
    build(nc, io)


def kernel(**inputs):
    import concourse.bacc as bacc
    from concourse.bass_utils import run_bass_kernel_spmd

    ins = _layout(inputs)
    nc = bacc.Bacc("TRN2", target_bir_lowering=False, num_devices=1)
    program(nc, ins)
    r = run_bass_kernel_spmd(nc, [{f"in_{n}": v for n, v in ins.items()}], core_ids=[0])
    out = r.results[0]["out_0"]
    return out.reshape(NT, 128, B, TOK).transpose(2, 0, 3, 1).reshape(B, L, D)
```

```python
from contextlib import ExitStack

import numpy as np
import concourse.bass as bass
import concourse.mybir as mybir
from concourse.alu_op_type import AluOpType as ALU

F32 = mybir.dt.float32
F32R = mybir.dt.float32r
U32 = mybir.dt.uint32
ACT = mybir.ActivationFunctionType
AX = mybir.AxisListType

B, L, D = 4, 1024, 128
NH, DK, C = 4, 32, 32
TOK = 128
NT = L // TOK
W = B * TOK
CN = TOK // C
CT = B * CN
NC = NT * CT
TAPS = 4
HALO = TAPS - 1
E, HID = 8, 256
HC = HID // 128
FF = 512
FC = FF // 128
LN_EPS, RMS_EPS, L2_EPS = 1e-5, 1e-5, 1e-6
WF = 2 * FF + 2 * FC * FF + FC * 128
WM = 2 * E * HID
WCH = WF // NT
SK, SQ, SV, SATT, SKT, SVT = range(6)
NPACK = 6
C_ID, C_MEAN, C_HEAD, C_CAUSAL, C_EYE, C_SEL = 0, 128, 256, 384, 416, 448
N_CONST = C_SEL + E
V_S1, V_S2, V_HS1, V_HS2, V_S3, V_NORM, V_AP = 0, 4, 8, 12, 16, 17, 18
V_EPS, V_L2E, N_VEC = 19, 20, 21


def build(nc, io):
    ctx = ExitStack()
    with ctx:
        top = [(nc.sbuf_base + 63) // 64 * 64]

        def cols(shape):
            n = 4
            for d in shape[1:]:
                n *= d
            return (n + 31) // 32 * 32

        def over(name, shape, dt, at):
            return nc.alloc_sbuf_tensor_at(name, shape, dt, offset=at)

        def sb(name, shape, dt=F32):
            at = top[0]
            top[0] += cols(shape)
            return over(name, shape, dt, at)

        def ps(name):
            return ctx.enter_context(nc.psum_tensor(name, [128, 512], F32))

        def sem(name):
            return ctx.enter_context(nc.semaphore(name))

        cst = sb("cst", [128, N_CONST])
        vec = sb("vec", [128, N_VEC])
        ident = cst[:, C_ID:C_ID + 128]
        mean_w = cst[:, C_MEAN:C_MEAN + 128]
        head_w = cst[:, C_HEAD:C_HEAD + 128]
        causal = cst[:, C_CAUSAL:C_CAUSAL + 32]
        eye = cst[:, C_EYE:C_EYE + 32]
        sel = sb("sel", [40, E], F32R)
        wsm = sb("wsm", [128, 5, 128])
        wr = sb("wr", [128, E])
        beta_tok = sb("beta_tok", [128, NC])
        lg = sb("lg", [128, B, E]); mx = sb("mx", [128, B, 8]); mi = sb("mi", [128, B, 8], U32)
        mf = sb("mf", [128, B, 2]); gw = sb("gw", [128, B, 2]); gt2 = sb("gt2", [128, B, 2, E])
        gate = sb("gate", [128, B, E]); iota = sb("iota", [128, E])
        hst = sb("hst", [128, B])
        spv = sb("spv", [128, 12])
        gtT = sb("gtT", [64, W], F32R)
        x1 = sb("x1", [128, W]); x1h = sb("x1h", [128, W], F32R); x1l = sb("x1l", [128, W], F32R)
        x2 = sb("x2", [128, W])
        x3 = sb("x3", [128, W]); x3h = sb("x3h", [128, W], F32R); x3l = sb("x3l", [128, W], F32R)
        acc = sb("acc", [128, W])
        gb = sb("gb", [128, 2, W]); yg = sb("yg", [128, 2, W]); hf = sb("hf", [128, 2, W])
        a1, a2, a3, a4, a5, oT = (sb(n, [128, W]) for n in ("a1", "a2", "a3", "a4", "a5", "oT"))
        temps = top[0]
        m1, m2, m3, m4 = (sb(n, [128, W]) for n in ("m1", "m2", "m3", "m4"))
        f1, f2, f3 = (sb(n, [128, W]) for n in ("f1", "f2", "f3"))
        pk = sb("pk", [128, CT, NPACK, C])
        xt = sb("xt", [128, B, TOK + HALO])
        xv = xt[:, :, HALO:HALO + TOK]
        xth = sb("xth", [128, B, TOK + HALO], F32R); xtl = sb("xtl", [128, B, TOK + HALO], F32R)
        tb = sb("tb", [128, B, CN, C])
        texp = sb("texp", [128, B, NH, C])
        spread = sb("spread", [128, 8, NH, C])
        sexp = sb("sexp", [128, B, NH, DK])
        qpc = sb("qpc", [128, B, 2, C])
        ws = sb("ws", [128, WCH])
        at_fa = top[0]
        fah = sb("fah", [128, FC, W], F32R); fal = sb("fal", [128, FC, W], F32R)
        at_fb = top[0]
        fbh = sb("fbh", [128, FC, W], F32R); fbl = sb("fbl", [128, FC, W], F32R)
        at_wm = top[0]
        wmh = sb("wmh", [128, WM], F32R); wml = sb("wml", [128, WM], F32R)
        wfh = sb("wfh", [128, WF], F32R); wfl = sb("wfl", [128, WF], F32R)
        assert top[0] <= nc.sbuf_usable_end, top[0]
        wqkv = over("wqkv", [128, 3, 128], F32, temps)
        conv = over("conv", [128, 3, TAPS, 128], F32, temps + 2048)
        tmpv = over("tmpv", [128, 768], F32, temps)
        tmpg = over("tmpg", [128, 256], F32, temps + 4096)
        wtap = over("wtap", [128, 3, TAPS, 128], F32, at_wm)
        wtaph = over("wtaph", [128, 3, TAPS, 128], F32R, at_fa)
        wtapl = over("wtapl", [128, 3, TAPS, 128], F32R, at_fa + 6144)
        stg = over("stg", [128, WM], F32, at_fa)
        kkc = over("kkc", [128, NC, C], F32, at_fb)
        big = over("big", [128, 2, 4096], F32, at_wm)
        apm = big[:, 0, :].rearrange("p (j h i) -> p j h i", j=C, h=NH)
        tpr = big[:, 1, :].rearrange("p (i n) -> p i n", i=C)
        tpm = big[:, 1, :].rearrange("p (i h j) -> p h i j", h=NH, i=C)
        bank = [ps(f"bank{i}") for i in range(8)]
        t1, t2, t3, t4, t5 = a1, a2, a3, a4, a5

        O_G, O_U, O_H1, O_H2, O_W3 = 0, FF, 2 * FF, 2 * FF + FC * FF, 2 * FF + 2 * FC * FF
        O_UP, O_DN = 0, E * HID

        names = """w_in cst_in conv_in x_in pk_stored pk_loaded tb_in fw_in ws_in ws_hi ws_lo wm_in wm_hi wm_lo tt_stored
            wtap_f wtap_hi wtap_done xt_hi xt_ready
            beta_proj qkv_proj qkv_act sq_done ss_done rs_ln rs_act kq_done qn_done kv_tok kexp_done gram_done
            bt_ready beta_tmp beta_tok_done gram_read v_done
            kkt_done kkt_read tinit tv_mul tv_step tg_mul tg_step tt_done tt_read s_zero sp_step
            texp_ready m2_done wu_ready m4_done qp_step os_done s_ready o_copied
            mixl_done mix_act mix_o o_ready osq_done oss_done ors_done og_done wo_done x1_hi
            r_done lg_ready tk1 tk2 tk3 tk4 tk5 th_done tk6 tk7 gate_ready gtp_done gt_hi gt_ready
            gbp_done gb_ready up_done gelu_done hi1 lo0 lo1 dn_done yg_ready acc_ready
            lru_proj lru_t lru_a lru_m lru_l lru_mult lru_gx lru_b lru_scan hst_ready x3_hi x3_ready
            g_done u_done g_act glu_f glu_hi fa_ready h1_done h1_act h1_hi fb_ready h2_done h2_act h2_hi f2_ready
            w3_done out_stored""".split()
        S = {n: sem(n) for n in names}
        for n in "1234":
            for k in ("y", "mu", "d", "sq", "var", "rs", "x"):
                S[k + n] = sem(f"ln{n}_{k}")
        START = """beta_proj qkv_proj qkv_act sq_done ss_done rs_ln rs_act kq_done qn_done gram_done bt_ready beta_tmp
            gram_read v_done kexp_done ws_lo m2_done wu_ready qp_step os_done s_ready o_copied x1 y2 y4
            dn_done lo0 lo1 gelu_done yg_ready acc_ready gb_ready w3_done gt_ready rs3 d3 d1 lg_ready mix_act
            hst_ready out_stored pk_stored fa_ready h1_done h2_done fb_ready x4 o_ready y1 rs4 d4 x3_ready
            g_act glu_f""".split()

        def after(name, n):
            return S[name], n + (1 if name in START else 0)

        block = ctx.enter_context(nc.Block())
        V, A, P, G = nc.vector, nc.scalar, nc.tensor, nc.gpsimd

        def rep(ap, axis, n):
            shape = list(ap.shape)
            shape[axis] = n
            return ap.broadcast_to(shape)

        def heads(n):
            return rep(cst[:, C_HEAD:C_HEAD + 128].rearrange("p (o h c) -> p o h c", o=1, h=NH), 1, n)

        def f32(ap):
            return ap.bitcast(F32)

        def by_seq(ap):
            return ap.rearrange("p (b n) -> p b n", b=B)

        def by_chunk(ap):
            return ap.rearrange("p (c i) -> p c i", c=CT)

        def schedule(eng, dense, tails):
            dense(None, 0, None)
            tails(None, None, 0)
            dense(0, 1, None)
            tails(None, 0, 1)
            dense(1, 2, None)
            with eng.Fori(1, NT - 2) as t:
                tails(t - 1, t, t + 1)
                dense(t + 1, t + 2, t - 1)
            tails(NT - 3, NT - 2, NT - 1)
            dense(NT - 1, None, NT - 3)
            tails(NT - 2, NT - 1, None)
            dense(None, None, NT - 2)
            tails(NT - 1, None, None)
            dense(None, None, NT - 1)

        @block.sync
        def _(sp):
            def load_x(t):
                sp.dma_start(xt[:, :, :], io["xh"][:, bass.ds(t * B, B), :]).then_inc(S["x_in"], 16)

            def load_tile(t):
                sp.wait_ge(*after("y1", t))
                load_x(t)
                sp.wait_ge(*after("o_ready", t))
                sp.dma_start(pk[:, :, 1:, :], io["pack"][:, bass.ds(t * CT, CT), :, :]).then_inc(S["pk_loaded"], 16)
                sp.dma_start(tb[:, :, :, :].rearrange("p b n c -> p (b n) c"),
                             io["tt"][:, bass.ds(t * CT, CT), :]).then_inc(S["tb_in"], 16)

            def store_out(t):
                sp.wait_ge(*after("x4", t + 1))
                sp.dma_start(io["out"][:, bass.ds(t * W, W)], f1[:, :]).then_inc(S["out_stored"], 16)

            sp.dma_start(cst[:, :], io["cst"]).then_inc(S["cst_in"], 16)
            sp.dma_start(wqkv[:, :, :], io["wqkv"]).then_inc(S["conv_in"], 16)
            sp.dma_start(conv[:, :, :, :], io["conv"]).then_inc(S["conv_in"], 16)
            sp.dma_start(vec[:, :], io["vec"]).then_inc(S["w_in"], 16)
            sp.dma_start(wsm[:, :, :], io["wsm"]).then_inc(S["w_in"], 16)
            sp.dma_start(wr[:, :], io["wr"]).then_inc(S["fw_in"], 16)
            sp.dma_start(iota[:, :], io["iota"]).then_inc(S["fw_in"], 16)
            load_x(0)
            with sp.Fori(0, NT) as t:
                sp.wait_ge(*after("ws_lo", t))
                sp.dma_start(ws[:, :], io["wf"][:, bass.ds(t * WCH, WCH)]).then_inc(S["ws_in"], 16)
                sp.wait_ge(*after("beta_proj", t + 1))
                sp.wait_ge(S["xt_ready"], t + 1)
                sp.dma_start(xt[:, :, :], io["xh"][:, bass.ds((t + 1) * B, B), :]).then_inc(S["x_in"], 16)
                sp.wait_ge(*after("gram_read", 2 * t + 2))
                sp.dma_start(io["pack"][:, bass.ds(t * CT, CT), :, :], pk[:, :, 1:, :]).then_inc(S["pk_stored"], 16)
            sp.wait_ge(*after("qkv_proj", 3 * NT))
            sp.dma_start(stg[:, :], io["wm"]).then_inc(S["wm_in"], 16)
            sp.wait_ge(S["tt_read"], 8)
            sp.dma_start(io["tt"], kkc[:, :, :]).then_inc(S["tt_stored"], 16)
            sp.wait_ge(S["tt_stored"], 16)
            sp.wait_ge(*after("pk_stored", 16 * NT))

            def dense(m, a, l):
                if l is not None:
                    store_out(l)

            def tails(f, m, a):
                if a is not None and (not isinstance(a, int) or a < NT - 1):
                    load_tile(a + 1)

            load_tile(0)
            schedule(sp, dense, tails)
            sp.wait_ge(*after("out_stored", 16 * NT))

        @block.tensor
        def _(pe):
            def mm(out, lhsT, rhs, start=True, stop=True, skip=False):
                return P.matmul(out, lhsT, rhs, start=start, stop=stop, skip_group_check=skip)

            def mm3(out, wh, wl, xh, xl, start=True, stop=True):
                mm(out, wh, xl, start=start, stop=False)
                mm(out, wl, xh, start=False, stop=False)
                return mm(out, wh, xh, start=False, stop=stop)

            def flat(ap):
                return ap.rearrange("p h c -> p (h c)")

            def project(t):
                pe.wait_ge(S["x_in"], 16 * t + 16)
                pe.wait_ge(*after("bt_ready", t))
                mm(by_seq(bank[3][:, :]), wsm[:, 0, :], xv).then_inc(S["beta_proj"], 1)
                pe.wait_ge(S["xt_ready"], t + 1)
                for m in range(3):
                    pe.wait_ge(*after("qkv_act", 3 * t + m))
                    for k in range(TAPS):
                        i = mm3(by_seq(bank[m][:, :]), wtaph[:, m, k, :], wtapl[:, m, k, :],
                                xth[:, :, k:k + TOK], xtl[:, :, k:k + TOK], start=k == 0, stop=k == TAPS - 1)
                    i.then_inc(S["qkv_proj"], 1)

            def squares(t):
                for m in range(2):
                    pe.wait_ge(*after("sq_done", 2 * t + m + 1))
                    pe.wait_ge(*after("rs_ln", 2 * t))
                    mm(bank[4 + m][:, :], head_w, [t1, t2][m][:, :]).then_inc(S["ss_done"], 1)

            def gram(t):
                for g in range(2):
                    pe.wait_ge(*after("qn_done", t + 1))
                    pe.wait_ge(*after("kexp_done", 2 * t + g + 1))
                    pe.wait_ge(*after("gram_read", 2 * t))
                    for c in range(8):
                        i = mm(bank[6 + g][:, c * 64:(c + 1) * 64], flat(spread[:, c, :, :]),
                               flat(pk[:, g * 8 + c, SK:SQ + 1, :]))
                    i.then_inc(S["gram_done"], 1)

            pe.wait_ge(S["w_in"], 32)
            pe.wait_ge(S["wtap_done"], 1)
            project(0)
            with pe.Fori(0, NT - 1) as t:
                squares(t)
                project(t + 1)
                gram(t)
            squares(NT - 1)
            gram(NT - 1)
            pe.wait_ge(*after("gram_read", 2 * NT))
            for g in range(8):
                if g >= 2:
                    pe.wait_ge(S["kkt_read"], g - 1)
                for j in range(4):
                    i = P.transpose(bank[g % 2][:, j * 128:(j + 1) * 128], kkc[:, :, 4 * g + j], ident)
                i.then_inc(S["kkt_done"], 1)
            pe.wait_ge(S["tv_step"], C - 1)
            pe.wait_ge(S["tg_step"], C - 1)
            pe.wait_ge(S["kkt_read"], 8)
            for g in range(8):
                if g >= 2:
                    pe.wait_ge(S["tt_read"], g - 1)
                for j in range(4):
                    i = P.transpose(bank[g % 2][:, j * 128:(j + 1) * 128], tpr[:, 4 * g + j, :], ident)
                i.then_inc(S["tt_done"], 1)
            pe.wait_ge(S["tt_read"], 8)
            pe.wait_ge(S["s_zero"], 1)
            pe.wait_ge(S["fw_in"], 32)
            pe.wait_ge(S["wm_lo"], 2)
            pe.wait_ge(*after("ws_lo", NT))

            def mean_product(n, t, src, bk):
                pe.wait_ge(*after("y" + n, t + 1))
                mm(bank[bk][:, :], mean_w, src[:, :]).then_inc(S["mu" + n], 1)

            def var_product(n, t, src, bk):
                pe.wait_ge(S["sq" + n], t + 1)
                mm(bank[bk][:, :], mean_w, src[:, :]).then_inc(S["var" + n], 1)

            def delta_wu(t, n):
                pe.wait_ge(S["texp_ready"], CN * t + n + 1)
                pe.wait_ge(S["pk_loaded"], 16 * t + 16)
                pe.wait_ge(*after("wu_ready", CN * t + n))
                for b in range(B):
                    i = mm(bank[0][:, b * 64:(b + 1) * 64], flat(texp[:, b, :, :]),
                           flat(pk[:, b * CN + n, SKT:SVT + 1, :]))
                i.then_inc(S["m2_done"], 1)

            def delta_attn(t, n):
                k = CN * t + n
                pe.wait_ge(*after("wu_ready", k + 1))
                pe.wait_ge(*after("qp_step", 2 * k))
                for b in range(B):
                    i = mm(bank[1][:, b * 64:(b + 1) * 64], flat(spread[:, 2 * b, :, :]),
                           flat(pk[:, b * CN + n, SATT:SKT + 1, :]))
                i.then_inc(S["m4_done"], 1)
                pe.wait_ge(*after("o_copied", k))
                for b in range(B):
                    mm(bank[2][:, b * 64:(b + 1) * 64], flat(spread[:, 2 * b + 1, :, :]),
                       flat(pk[:, b * CN + n, SATT:SKT + 1, :]), start=b == 0, stop=False, skip=True)

            def delta_state(t, n):
                k = CN * t + n
                pe.wait_ge(*after("qp_step", 2 * k + 2))
                pe.wait_ge(*after("s_ready", k))
                for b in range(B):
                    i = mm(bank[2][:, b * 64:(b + 1) * 64], flat(sexp[:, b, :, :]),
                           flat(qpc[:, b, :, :]), start=False, stop=b == B - 1, skip=True)
                i.then_inc(S["os_done"], 1)

            def up(t, e):
                pe.wait_ge(*after("x1", t + 1))
                pe.wait_ge(*after("gelu_done", 3 * (E * t + e)))
                for c in range(HC):
                    o = O_UP + e * HID + c * 128
                    mm3(bank[4 + c][:, :], wmh[:, o:o + 128], wml[:, o:o + 128], x1h[:, :], x1l[:, :])\
                        .then_inc(S["up_done"], 1)

            def gate_rows(t, e):
                pe.wait_ge(*after("gt_ready", t + 1))
                pe.wait_ge(*after("gb_ready", E * t + e))
                mm(bank[7][:, :], sel[0:40, e:e + 1].broadcast_to([40, 128]), gtT[0:40, :]).then_inc(S["gbp_done"], 1)

            def down(t, e):
                pe.wait_ge(*after("lo0", E * t + e + 1))
                pe.wait_ge(*after("yg_ready", E * t + e))
                for c in range(HC):
                    if c == 1:
                        pe.wait_ge(*after("lo1", E * t + e + 1))
                    o, s = O_DN + (e * HC + c) * 128, (e % 2) * HC + c
                    i = mm3(bank[6][:, :], wmh[:, o:o + 128], wml[:, o:o + 128], fah[:, s, :], fal[:, s, :],
                            start=c == 0, stop=c == HC - 1)
                i.then_inc(S["dn_done"], 1)

            def dense(m, a, l):
                if l is not None and m is None:
                    mean_product("4", l, f1, 3)
                    var_product("4", l, f2, 3)
                if a is not None:
                    pe.wait_ge(*after("lg_ready", a))
                    pe.wait_ge(*after("gt_ready", a))
                for e in range(E):
                    if m is not None:
                        if e == 0:
                            if l is not None:
                                pe.wait_ge(*after("y4", l + 1))
                            pe.wait_ge(*after("gt_ready", m + 1))
                        up(m, e)
                        gate_rows(m, e)
                    if a is not None and e % 2 == 0:
                        delta_wu(a, e // 2)
                    if a is not None and e % 2 == 1:
                        delta_state(a, e // 2)
                    if l is not None and m is not None and e == 1:
                        mean_product("4", l, f1, 3)
                    if l is not None and m is not None and e == 3:
                        var_product("4", l, f2, 3)
                    if a is not None and e == 5:
                        pe.wait_ge(S["x_in"], 16 * (NT + 1) + 16 * a + 16)
                        if l is not None:
                            pe.wait_ge(*after("rs4", 2 * l + 1))
                        mm(by_seq(bank[3][:, :]), wsm[:, 1, :], xv).then_inc(S["mixl_done"], 1)
                    if m is not None and e:
                        down(m, e - 1)
                    if a is not None and e % 2 == 0:
                        delta_attn(a, e // 2)
                if m is not None:
                    down(m, E - 1)

            def glu(f, c):
                o = 4 + 2 * (c % 2)
                pe.wait_ge(*after("g_act", FC * f + max(c - 1, 0)))
                g, u = O_G + c * 128, O_U + c * 128
                mm3(bank[o][:, :], wfh[:, g:g + 128], wfl[:, g:g + 128], x3h[:, :], x3l[:, :]).then_inc(S["g_done"], 1)
                pe.wait_ge(*after("glu_f", FC * f + max(c - 1, 0)))
                mm3(bank[o + 1][:, :], wfh[:, u:u + 128], wfl[:, u:u + 128], x3h[:, :], x3l[:, :]).then_inc(S["u_done"], 1)

            def hidden(f, o, base, xh, xl, ready, done):
                for c in range(FC):
                    if o == 0:
                        pe.wait_ge(*(after(ready, FC * f + c + 1)))
                    w = base + c * FF + o * 128
                    i = mm3(bank[4 + o][:, :], wfh[:, w:w + 128], wfl[:, w:w + 128], xh[:, c, :], xl[:, c, :],
                            start=c == 0, stop=c == FC - 1)
                i.then_inc(S[done], 1)

            def tails(f, m, a):
                if f is not None:
                    pe.wait_ge(*after("x3_ready", f + 1))
                    pe.wait_ge(*after("y4", f))
                    last = f + 2 if f is not m and m is not None else NT
                    pe.wait_ge(*after("gelu_done", 3 * E * last))
                    glu(f, 0)
                if m is not None:
                    mean_product("2", m, m1, 0)
                if f is not None:
                    pe.wait_ge(*after("gb_ready", E * last))
                    pe.wait_ge(*after("yg_ready", E * last))
                    glu(f, 1)
                if a is not None:
                    pe.wait_ge(S["osq_done"], a + 1)
                    pe.wait_ge(*after("o_copied", CN * a + CN))
                    mm(bank[2][:, :], head_w, a2[:, :]).then_inc(S["oss_done"], 1)
                if f is not None:
                    glu(f, 2)
                if m is not None:
                    var_product("2", m, m2, 1)
                if f is not None:
                    glu(f, 3)
                    pe.wait_ge(*after("g_act", FC * f + FC - 1))
                    hidden(f, 0, O_H1, fah, fal, "fa_ready", "h1_done")
                    pe.wait_ge(*after("g_act", FC * f + FC))
                if a is not None:
                    pe.wait_ge(S["og_done"], a + 1)
                    mm(bank[3][:, :], wsm[:, 2, :], a3[:, :]).then_inc(S["wo_done"], 1)
                if m is not None:
                    pe.wait_ge(S["x2"], m + 1)
                    mm(bank[0][:, :], wsm[:, 3, :], x2[:, :]).then_inc(S["lru_proj"], 1)
                    mm(bank[1][:, :], wsm[:, 4, :], x2[:, :]).then_inc(S["lru_proj"], 1)
                if f is not None:
                    hidden(f, 1, O_H1, fah, fal, "fa_ready", "h1_done")
                if a is not None:
                    pe.wait_ge(S["ors_done"], 2 * a + 2)
                    mean_product("1", a, a1, 2)
                if f is not None:
                    hidden(f, 2, O_H1, fah, fal, "fa_ready", "h1_done")
                if a is not None:
                    var_product("1", a, a2, 3)
                if f is not None:
                    hidden(f, 3, O_H1, fah, fal, "fa_ready", "h1_done")
                if m is not None:
                    pe.wait_ge(S["lru_t"], 2 * m + 2)
                    mean_product("3", m, m1, 0)
                if f is not None:
                    hidden(f, 0, O_H2, fbh, fbl, "fb_ready", "h2_done")
                if a is not None:
                    pe.wait_ge(*after("x1", a + 1))
                    for b in range(B):
                        i = mm(bank[2][:, b * E:(b + 1) * E], x1[:, b * TOK:(b + 1) * TOK], wr[:, :])
                    i.then_inc(S["r_done"], 1)
                if m is not None:
                    var_product("3", m, m2, 1)
                if f is not None:
                    hidden(f, 1, O_H2, fbh, fbl, "fb_ready", "h2_done")
                    hidden(f, 2, O_H2, fbh, fbl, "fb_ready", "h2_done")
                if a is not None:
                    pe.wait_ge(S["gate_ready"], a + 1)
                    for b in range(B):
                        i = mm(bank[3][0:E, b * TOK:(b + 1) * TOK], gate[:, b, :], ident)
                    i.then_inc(S["gtp_done"], 1)
                if f is not None:
                    hidden(f, 3, O_H2, fbh, fbl, "fb_ready", "h2_done")
                    for c in range(FC):
                        pe.wait_ge(S["f2_ready"], FC * f + c + 1)
                        w = O_W3 + c * 128
                        i = mm3(bank[4][:, :], wfh[:, w:w + 128], wfl[:, w:w + 128], fah[:, c, :], fal[:, c, :],
                                start=c == 0, stop=c == FC - 1)
                    i.then_inc(S["w3_done"], 1)
                if m is not None:
                    pe.wait_ge(*after("d3", m + 1))
                    pe.wait_ge(*after("rs3", 2 * m + 1))

            schedule(pe, dense, tails)

        @block.scalar
        def _(act):
            eps = vec[:, V_EPS:V_EPS + 1]
            l2e = vec[:, V_L2E:V_L2E + 1]
            act.wait_ge(S["w_in"], 32)
            act.wait_ge(S["sp_step"], 1)
            A.activation(spv[:, 1:2], spv[:, 0:1], ACT.Exp, scale=-1.0).then_inc(S["sp_step"], 1)
            act.wait_ge(S["wtap_f"], 1)
            A.activation(wtaph[:, :, :, :], wtap[:, :, :, :], ACT.Copy).then_inc(S["wtap_hi"], 1)
            with act.Fori(0, NT) as t:
                dst = [t3, t4, t5]
                for m in range(3):
                    act.wait_ge(*after("qkv_proj", 3 * t + m + 1))
                    act.wait_ge(*after("qn_done", t) if m < 2 else after("v_done", t))
                    A.activation(dst[m][:, :], bank[m][:, :], ACT.Silu).then_inc(S["qkv_act"], 1)
                    if m < 2:
                        act.wait_ge(*after("qkv_act", 3 * t + m + 1))
                        act.wait_ge(*after("ss_done", 2 * t))
                        A.activation([t1, t2][m][:, :], dst[m][:, :], ACT.Square).then_inc(S["sq_done"], 1)
                act.wait_ge(*after("beta_proj", t + 1))
                act.wait_ge(*after("beta_tmp", t))
                A.activation(gb[:, 0, :], bank[3][:, :], ACT.Tanh, scale=0.5).then_inc(S["bt_ready"], 1)
                act.wait_ge(S["ws_in"], 16 * t + 16)
                A.activation(wfh[:, bass.ds(t * WCH, WCH)], ws[:, :], ACT.Copy).then_inc(S["ws_hi"], 1)
                for m in range(2):
                    act.wait_ge(*after("ss_done", 2 * t + m + 1))
                    act.wait_ge(*after("kq_done", 2 * t))
                    A.activation(hf[:, m, :], bank[4 + m][:, :], ACT.Ln, bias=l2e).then_inc(S["rs_ln"], 1)
                for m in range(2):
                    act.wait_ge(*after("rs_ln", 2 * t + m + 1))
                    A.activation(hf[:, m, :], hf[:, m, :], ACT.Exp, scale=-0.5).then_inc(S["rs_act"], 1)
            for g in range(8):
                act.wait_ge(S["kkt_done"], g + 1)
                A.activation(apm[:, 4 * g:4 * g + 4, :, :].rearrange("p j h i -> p (j h i)"), bank[g % 2][:, :],
                             ACT.Copy).then_inc(S["kkt_read"], 1)
            act.wait_ge(S["wm_in"], 16)
            act.wait_ge(S["tt_done"], 8)
            for g in range(2):
                c = slice(g * WM // 2, (g + 1) * WM // 2)
                A.activation(wmh[:, c], stg[:, c], ACT.Copy).then_inc(S["wm_hi"], 1)

            def square(n, t, src, dst):
                act.wait_ge(*after("d" + n, t + 1) if n in "134" else (S["d" + n], t + 1))
                A.activation(dst[:, :], src[:, :], ACT.Square).then_inc(S["sq" + n], 1)

            def rstd_ln(n, t, bk, dst):
                act.wait_ge(S["var" + n], t + 1)
                A.activation(dst[:, :], bank[bk][:, :], ACT.Ln, bias=eps).then_inc(S["rs" + n], 1)

            def rstd_exp(n, t, dst):
                act.wait_ge(*after("rs" + n, 2 * t + 1) if n in "34" else (S["rs" + n], 2 * t + 1))
                A.activation(dst[:, :], dst[:, :], ACT.Exp, scale=-0.5).then_inc(S["rs" + n], 1)

            def dense(m, a, l):
                if m is None and l is not None:
                    square("4", l, f1, f2)
                    rstd_ln("4", l, 3, f3)
                    rstd_exp("4", l, f3)
                if m is None and a is not None:
                    act.wait_ge(S["mixl_done"], a + 1)
                    A.activation(a4[:, :], bank[3][:, :], ACT.Tanh, scale=0.5).then_inc(S["mix_act"], 1)
                if m is None:
                    return
                for e in range(E):
                    k = E * m + e
                    s = (e % 2) * HC
                    act.wait_ge(S["up_done"], HC * k + 1)
                    act.wait_ge(*after("lo0", k))
                    A.activation(hf[:, 0, :], bank[4][:, :], ACT.Gelu).then_inc(S["gelu_done"], 1)
                    act.wait_ge(*after("dn_done", E * m + max(e - 1, 0)))
                    A.activation(fah[:, s, :], bank[4][:, :], ACT.Gelu).then_inc(S["gelu_done"], 1)
                    act.wait_ge(S["up_done"], HC * k + 2)
                    act.wait_ge(*after("lo1", k))
                    A.activation(hf[:, 1, :], bank[5][:, :], ACT.Gelu).then_inc(S["gelu_done"], 1)
                    act.wait_ge(S["gbp_done"], k + 1)
                    act.wait_ge(*after("yg_ready", E * m + max(e - 1, 0)))
                    A.activation(gb[:, e % 2, :], bank[7][:, :], ACT.Copy).then_inc(S["gb_ready"], 1)
                    if l is not None and e == 2:
                        square("4", l, f1, f2)
                    if l is not None and e == 4:
                        rstd_ln("4", l, 3, f3)
                        rstd_exp("4", l, f3)
                    if a is not None and e == 6:
                        act.wait_ge(S["mixl_done"], a + 1)
                        act.wait_ge(*after("x1", a))
                        A.activation(a4[:, :], bank[3][:, :], ACT.Tanh, scale=0.5).then_inc(S["mix_act"], 1)

            def silu(f, c):
                act.wait_ge(S["g_done"], FC * f + c + 1)
                act.wait_ge(*after("glu_f", FC * f + max(c - 1, 0)))
                A.activation(gb[:, c % 2, :], bank[4 + 2 * (c % 2)][:, :], ACT.Silu,
                             scale=vec[:, V_S1 + c:V_S1 + c + 1]).then_inc(S["g_act"], 1)

            def gelu(f, o, done, acted, v, free, n):
                act.wait_ge(S[done], FC * f + o + 1 + (1 if done in START else 0))
                act.wait_ge(*after(free, n))
                A.activation(hf[:, o % 2, :], bank[4 + o][:, :], ACT.Gelu, scale=vec[:, v + o:v + o + 1])\
                    .then_inc(S[acted], 1)

            def gelu1(f, o):
                if o < 2:
                    gelu(f, o, "h1_done", "h1_act", V_HS1, "fa_ready", FC * f + 3 + o)
                else:
                    gelu(f, o, "h1_done", "h1_act", V_HS1, "fb_ready", FC * f + o - 1)

            def gelu2(f, o):
                if o < 2:
                    gelu(f, o, "h2_done", "h2_act", V_HS2, "fb_ready", FC * f + 3 + o)
                else:
                    gelu(f, o, "h2_done", "h2_act", V_HS2, "f2_ready", FC * f + o - 1)

            def tails(f, m, a):
                F_, M_, A_ = f is not None, m is not None, a is not None
                if F_:
                    act.wait_ge(*after("yg_ready", E * (f + 2 if M_ else NT)))
                    silu(f, 0)
                if A_:
                    act.wait_ge(*after("o_ready", a + 1))
                    A.activation(a2[:, :], a1[:, :], ACT.Square).then_inc(S["osq_done"], 1)
                if F_:
                    silu(f, 1)
                if M_:
                    square("2", m, m1, m2)
                if F_:
                    silu(f, 2)
                    silu(f, 3)
                if A_:
                    act.wait_ge(S["oss_done"], a + 1)
                    A.activation(a5[:, :], bank[2][:, :], ACT.Ln, scale=1.0 / DK, bias=eps).then_inc(S["ors_done"], 1)
                    act.wait_ge(S["ors_done"], 2 * a + 1)
                    A.activation(a5[:, :], a5[:, :], ACT.Exp, scale=-0.5).then_inc(S["ors_done"], 1)
                if M_:
                    rstd_ln("2", m, 1, m3)
                    rstd_exp("2", m, m3)
                if F_:
                    gelu1(f, 0)
                if M_:
                    act.wait_ge(S["x2"], m + 1)
                    act.wait_ge(S["lru_proj"], 2 * m + 1)
                    A.activation(m1[:, :], bank[0][:, :], ACT.Tanh, scale=0.5).then_inc(S["lru_t"], 1)
                    act.wait_ge(S["lru_proj"], 2 * m + 2)
                    A.activation(m2[:, :], bank[1][:, :], ACT.Tanh, scale=0.5).then_inc(S["lru_t"], 1)
                    act.wait_ge(S["lru_t"], 2 * m + 2)
                    A.activation(m4[:, :], m2[:, :], ACT.Exp, scale=spv[:, 11:12], bias=spv[:, 11:12])\
                        .then_inc(S["lru_a"], 1)
                    A.activation(m3[:, :], m2[:, :], ACT.Exp, scale=spv[:, 10:11], bias=spv[:, 10:11])\
                        .then_inc(S["lru_a"], 1)
                    act.wait_ge(S["lru_m"], m + 1)
                    A.activation(m4[:, :], m4[:, :], ACT.Ln, scale=-1.0).then_inc(S["lru_l"], 1)
                    act.wait_ge(S["lru_l"], m + 1)
                    A.activation(m4[:, :], m4[:, :], ACT.Exp, scale=0.5).then_inc(S["lru_mult"], 1)
                if F_:
                    gelu1(f, 1)
                if A_:
                    square("1", a, a1, a2)
                if F_:
                    gelu1(f, 2)
                if A_:
                    rstd_ln("1", a, 3, a4)
                    rstd_exp("1", a, a4)
                if F_:
                    gelu1(f, 3)
                if M_:
                    square("3", m, m1, m2)
                if F_:
                    gelu2(f, 0)
                if M_:
                    rstd_ln("3", m, 1, m3)
                    rstd_exp("3", m, m3)
                if F_:
                    gelu2(f, 1)
                if A_:
                    act.wait_ge(S["tk3"], a + 1)
                    A.activation(gw[:, :, 0], gw[:, :, 1], ACT.Tanh, scale=0.5).then_inc(S["th_done"], 1)
                if F_:
                    gelu2(f, 2)
                    gelu2(f, 3)

            schedule(act, dense, tails)

        @block.gpsimd
        def _(pool):
            for name in START:
                pool.sem_inc(S[name], 1)
            pool.wait_ge(S["cst_in"], 16)
            pool.wait_ge(S["conv_in"], 32)
            G.tensor_tensor(wtap[:, :, :, :], rep(wqkv[:, :, :].rearrange("p m (o n) -> p m o n", o=1), 2, TAPS),
                            conv[:, :, :, :], ALU.mult).then_inc(S["wtap_f"], 1)
            pool.wait_ge(S["wtap_hi"], 1)
            G.tensor_tensor(wtapl[:, :, :, :], wtap[:, :, :, :], f32(wtaph[:, :, :, :]), ALU.subtract)\
                .then_inc(S["wtap_done"], 1)
            with pool.Fori(0, NT) as t:
                for g in range(2):
                    pool.wait_ge(*after("qn_done", t + 1))
                    pool.wait_ge(*after("gram_done", 2 * t + g))
                    G.tensor_tensor(spread[:, :, :, :], rep(pk[:, g * 8:(g + 1) * 8, SK:SK + 1, :], 2, NH),
                                    heads(8), ALU.mult).then_inc(S["kexp_done"], 1)
                pool.wait_ge(S["ws_hi"], t + 1)
                cs = bass.ds(t * WCH, WCH)
                G.tensor_tensor(wfl[:, cs], ws[:, :], f32(wfh[:, cs]), ALU.subtract).then_inc(S["ws_lo"], 1)
            pool.wait_ge(S["kkt_read"], 8)
            pool.wait_ge(S["tinit"], 2)
            for j in range(C - 1):
                n, k = C - 1 - j, j + 1
                a = rep(apm[:, j, 3:4, j + 1:C].rearrange("p h (i o) -> p h i o", o=1), 3, k)
                r = rep(tpm[:, 3:4, j:j + 1, 0:k], 2, n)
                m = tmpg[:, 0:n * k].rearrange("p (h i k) -> p h i k", h=1, i=n)
                if j:
                    pool.wait_ge(S["tg_step"], j)
                G.tensor_tensor(m, a, r, ALU.mult).then_inc(S["tg_mul"], 1)
                pool.wait_ge(S["tg_mul"], j + 1)
                o = tpm[:, 3:4, j + 1:C, 0:k]
                G.tensor_tensor(o, o, m, ALU.subtract).then_inc(S["tg_step"], 1)
            pool.wait_ge(S["wm_hi"], 1)
            G.tensor_tensor(wml[:, 0:WM // 2], stg[:, 0:WM // 2], f32(wmh[:, 0:WM // 2]), ALU.subtract)\
                .then_inc(S["wm_lo"], 1)
            pool.wait_ge(S["tt_stored"], 16)

            def dense(m, a, l):
                for e in range(E):
                    if a is not None and e % 2 == 0:
                        n = e // 2
                        pool.wait_ge(S["tb_in"], 16 * a + 16)
                        pool.wait_ge(*after("m2_done", CN * a + n))
                        G.tensor_tensor(texp[:, :, :, :], rep(tb[:, :, n:n + 1, :], 2, NH), heads(B), ALU.mult)\
                            .then_inc(S["texp_ready"], 1)
                    if m is not None:
                        k = E * m + e
                        pool.wait_ge(S["hi1"], k + 1)
                        s = (e % 2) * HC + 1
                        G.tensor_tensor(fal[:, s, :], hf[:, 1, :], f32(fah[:, s, :]), ALU.subtract)\
                            .then_inc(S["lo1"], 1)
                        if e:
                            pool.wait_ge(*after("yg_ready", k))
                            if e == 1:
                                pool.wait_ge(*after("y2", m))
                            else:
                                pool.wait_ge(*after("acc_ready", (E - 1) * m + e - 1))
                            G.tensor_tensor(acc[:, :], (x1 if e == 1 else acc)[:, :], yg[:, (e - 1) % 2, :], ALU.add)\
                                .then_inc(S["acc_ready"], 1)

            def tails(f, m, a):
                if f is None:
                    return
                for o in range(FC):
                    pool.wait_ge(S["h1_hi"], FC * f + o + 1)
                    G.tensor_tensor(fbl[:, o, :], hf[:, o % 2, :], f32(fbh[:, o, :]), ALU.subtract)\
                        .then_inc(S["fb_ready"], 1)
                for o in range(FC):
                    pool.wait_ge(S["h2_hi"], FC * f + o + 1)
                    G.tensor_tensor(fal[:, o, :], hf[:, o % 2, :], f32(fah[:, o, :]), ALU.subtract)\
                        .then_inc(S["f2_ready"], 1)

            schedule(pool, dense, tails)

        @block.vector
        def _(dve):
            tt, ts, stt = V.tensor_tensor, V.tensor_scalar, V.scalar_tensor_tensor
            dve.wait_ge(S["cst_in"], 16)
            V.tensor_copy(sel[0:40, :], cst[0:40, C_SEL:C_SEL + E])
            V.memset(f32(gtT[:, :]), 0.0)
            V.memset(sexp[:, :, :, :], 0.0)
            V.memset(hst[:, :], 0.0).then_inc(S["s_zero"], 1)
            dve.wait_ge(S["w_in"], 32)
            n_sp = [0]
            ap = vec[:, V_AP:V_AP + 1]

            def sp_op(i):
                i.then_inc(S["sp_step"], 1)
                n_sp[0] += 1
                dve.wait_ge(S["sp_step"], n_sp[0])

            col = lambda k: spv[:, k:k + 1]
            stt(col(0), ap, -1.0, ap, ALU.mult, ALU.max).then_inc(S["sp_step"], 1)
            n_sp[0] = 2
            dve.wait_ge(S["sp_step"], 2)
            sp_op(ts(col(2), col(1), 2.0, None, ALU.add))
            sp_op(V.reciprocal(col(3), col(2)))
            sp_op(tt(col(4), col(1), col(3), ALU.mult))
            sp_op(tt(col(5), col(4), col(4), ALU.mult))
            sp_op(ts(col(6), col(5), 1.0 / 17, 1.0 / 15, ALU.mult, ALU.add))
            for k in (13, 11, 9, 7, 5, 3, 1):
                sp_op(tt(col(7), col(6), col(5), ALU.mult))
                sp_op(ts(col(6), col(7), 1.0 / k, None, ALU.add))
            sp_op(tt(col(7), col(6), col(4), ALU.mult))
            sp_op(ts(col(8), ap, 0.0, None, ALU.max))
            sp_op(stt(col(9), col(7), 2.0, col(8), ALU.mult, ALU.add))
            sp_op(ts(col(10), col(9), -4.0, None, ALU.mult))
            sp_op(ts(col(11), col(9), -8.0, None, ALU.mult))

            def split_x(t):
                dve.wait_ge(S["x_in"], 16 * t + 16)
                dve.wait_ge(*after("qkv_proj", 3 * t))
                V.tensor_copy(xth[:, :, :], xt[:, :, :]).then_inc(S["xt_hi"], 1)
                dve.wait_ge(S["xt_hi"], t + 1)
                tt(xtl[:, :, :], xt[:, :, :], f32(xth[:, :, :]), ALU.subtract).then_inc(S["xt_ready"], 1)

            def stage1(t):
                dve.wait_ge(*after("pk_stored", 16 * t))
                dve.wait_ge(*after("gram_done", 2 * t))
                src = [t3, t4]
                for m in range(2):
                    dve.wait_ge(*after("rs_act", 2 * t + m + 1))
                    tt(pk[:, :, SK + m, :], by_chunk(src[m][:, :]), by_chunk(hf[:, m, :]), ALU.mult)\
                        .then_inc(S["kq_done"], 1)
                dve.wait_ge(*after("kq_done", 2 * t + 1))
                V.transpose(pk[:, :, SKT, :], pk[:, :, SK, :]).then_inc(S["qn_done"], 1)
                dve.wait_ge(*after("qkv_act", 3 * t + 3))
                V.transpose(pk[:, :, SVT, :], by_chunk(t5[:, :])).then_inc(S["kv_tok"], 1)
                V.tensor_copy(pk[:, :, SV, :], by_chunk(t5[:, :])).then_inc(S["v_done"], 1)
                dve.wait_ge(*after("bt_ready", t + 1))
                V.transpose(yg[:, 0, :], gb[:, 0, :]).then_inc(S["beta_tmp"], 1)
                dve.wait_ge(*after("beta_tmp", t + 1))
                ts(beta_tok[:, bass.ds(t * CT, CT)], yg[:, 0, 0:W:C], 0.5, 0.5, ALU.mult, ALU.add)\
                    .then_inc(S["beta_tok_done"], 1)
                dve.wait_ge(S["beta_tok_done"], t + 1)
                for g in range(2):
                    bk = bank[6 + g][:, :].rearrange("p (c s i) -> p c s i", c=8, s=2)
                    dve.wait_ge(*after("gram_done", 2 * t + g + 1))
                    tt(pk[:, g * 8:(g + 1) * 8, SATT, :], bk[:, :, 1, :],
                       rep(causal.rearrange("p (o i) -> p o i", o=1), 1, 8), ALU.mult)
                    tt(kkc[:, bass.ds(t * CT + g * 8, 8), :], bk[:, :, 0, :],
                       rep(beta_tok[:, bass.ds(t * CT + g * 8, 8)].rearrange("p (c o) -> p c o", o=1), 2, C),
                       ALU.mult).then_inc(S["gram_read"], 1)

            split_x(0)
            with dve.Fori(0, NT - 1) as t:
                split_x(t + 1)
                stage1(t)
            stage1(NT - 1)
            dve.wait_ge(S["wtap_done"], 1)
            V.memset(big[:, 1, :], 0.0).then_inc(S["tinit"], 1)
            dve.wait_ge(S["tinit"], 1)
            for h in range(NH):
                i = V.memset(big[:, 1, h * C:C * NH * C:NH * C + 1], 1.0)
            i.then_inc(S["tinit"], 1)
            dve.wait_ge(S["kkt_read"], 8)
            dve.wait_ge(S["tinit"], 2)
            for j in range(C - 1):
                n, k = C - 1 - j, j + 1
                a = rep(apm[:, j, 0:3, j + 1:C].rearrange("p h (i o) -> p h i o", o=1), 3, k)
                r = rep(tpm[:, 0:3, j:j + 1, 0:k], 2, n)
                m = tmpv[:, 0:3 * n * k].rearrange("p (h i k) -> p h i k", h=3, i=n)
                if j:
                    dve.wait_ge(S["tv_step"], j)
                tt(m, a, r, ALU.mult).then_inc(S["tv_mul"], 1)
                dve.wait_ge(S["tv_mul"], j + 1)
                o = tpm[:, 0:3, j + 1:C, 0:k]
                tt(o, o, m, ALU.subtract).then_inc(S["tv_step"], 1)
            for g in range(8):
                dve.wait_ge(S["tt_done"], g + 1)
                tt(kkc[:, :, 4 * g:4 * g + 4].rearrange("p c i -> p i c"),
                   bank[g % 2][:, :].rearrange("p (i c) -> p i c", i=4),
                   rep(beta_tok[:, :].rearrange("p (o c) -> p o c", o=1), 1, 4), ALU.mult).then_inc(S["tt_read"], 1)
            dve.wait_ge(S["wm_hi"], 2)
            tt(wml[:, WM // 2:], stg[:, WM // 2:], f32(wmh[:, WM // 2:]), ALU.subtract).then_inc(S["wm_lo"], 1)
            dve.wait_ge(S["tt_stored"], 16)

            def centre(n, t, buf, bk):
                dve.wait_ge(S["mu" + n], t + 1)
                tt(buf[:, :], buf[:, :], bank[bk][:, :], ALU.subtract).then_inc(S["d" + n], 1)

            def scale(n, t, buf, rs, out):
                dve.wait_ge(*after("rs" + n, 2 * t + 2) if n in "34" else (S["rs" + n], 2 * t + 2))
                return tt(out[:, :], buf[:, :], rs[:, :], ALU.mult)

            def delta_spread(t, n):
                k = CN * t + n
                dve.wait_ge(*after("m2_done", k + 1))
                dve.wait_ge(*after("os_done", k))
                tt(spread[:, :, :, :], rep(bank[0][:, 0:256].rearrange("p (s o c) -> p s o c", s=8, o=1), 2, NH),
                   heads(8), ALU.mult).then_inc(S["wu_ready"], 1)

            def delta_qp(t, n):
                k = CN * t + n
                dve.wait_ge(S["m4_done"], k + 1)
                bk = bank[1][:, 0:256].rearrange("p (b s c) -> p b s c", b=B, s=2)
                tt(qpc[:, :, 0, :], pk[:, n:CT:CN, SQ, :], bk[:, :, 0, :], ALU.subtract).then_inc(S["qp_step"], 1)
                tt(qpc[:, :, 1, :], rep(eye.rearrange("p (o c) -> p o c", o=1), 1, B), bk[:, :, 1, :],
                   ALU.subtract).then_inc(S["qp_step"], 1)

            def delta_out(t, n):
                k = CN * t + n
                dve.wait_ge(*after("os_done", k + 1))
                ob = bank[2][:, 0:256].rearrange("p (b s c) -> p b s c", b=B, s=2)
                for h in range(NH):
                    i = V.transpose(sexp[32 * h:32 * h + 32, :, h, :], ob[32 * h:32 * h + 32, :, 1, :])
                i.then_inc(S["s_ready"], 1)
                V.tensor_copy(oT[:, :].rearrange("p (b n c) -> p b n c", b=B, n=CN)[:, :, n, :], ob[:, :, 0, :])\
                    .then_inc(S["o_copied"], 1)

            def gated(m, e):
                k = E * m + e
                dve.wait_ge(*after("dn_done", k + 1))
                dve.wait_ge(*after("gb_ready", k + 1))
                dve.wait_ge(*after("acc_ready", (E - 1) * m + max(e - 1, 0)))
                tt(yg[:, e % 2, :], bank[6][:, :], gb[:, e % 2, :], ALU.mult).then_inc(S["yg_ready"], 1)

            def dense(m, a, l):
                if m is None and l is not None:
                    centre("4", l, f1, 3)
                    scale("4", l, f1, f3, f1).then_inc(S["x4"], 1)
                for e in range(E):
                    if m is not None:
                        k = E * m + e
                        s = (e % 2) * HC
                        dve.wait_ge(*after("gelu_done", 3 * k + 2))
                        dve.wait_ge(*after("dn_done", E * m + max(e - 1, 0)))
                        tt(fal[:, s, :], hf[:, 0, :], f32(fah[:, s, :]), ALU.subtract).then_inc(S["lo0"], 1)
                        dve.wait_ge(*after("gelu_done", 3 * k + 3))
                        V.tensor_copy(fah[:, s + 1, :], hf[:, 1, :]).then_inc(S["hi1"], 1)
                    if a is not None and e % 2 == 0:
                        delta_spread(a, e // 2)
                    if m is not None and e:
                        gated(m, e - 1)
                    if a is not None:
                        (delta_out if e % 2 else delta_qp)(a, e // 2)
                    if m is not None and l is not None and e == 2:
                        centre("4", l, f1, 3)
                    if m is not None and l is not None and e == 5:
                        scale("4", l, f1, f3, f1).then_inc(S["x4"], 1)

            def tails(f, m, a):
                F_, M_, A_ = f is not None, m is not None, a is not None

                def glu(c):
                    k = FC * f + c
                    dve.wait_ge(*after("g_act", k + 1))
                    dve.wait_ge(S["u_done"], k + 1)
                    if c == 0:
                        dve.wait_ge(*after("lo1", E * (f + 2 if M_ else NT)))
                    stt(hf[:, c % 2, :], bank[5 + 2 * (c % 2)][:, :], vec[:, V_S2 + c:V_S2 + c + 1],
                        gb[:, c % 2, :], ALU.mult, ALU.mult).then_inc(S["glu_f"], 1)
                    dve.wait_ge(*after("glu_f", k + 1))
                    V.tensor_copy(fah[:, c, :], hf[:, c % 2, :]).then_inc(S["glu_hi"], 1)
                    dve.wait_ge(S["glu_hi"], k + 1)
                    tt(fal[:, c, :], hf[:, c % 2, :], f32(fah[:, c, :]), ALU.subtract).then_inc(S["fa_ready"], 1)

                def hi(o, acted, done, dst, used, n):
                    dve.wait_ge(S[acted], FC * f + o + 1)
                    dve.wait_ge(*after(used, n))
                    V.tensor_copy(dst[:, o, :], hf[:, o % 2, :]).then_inc(S[done], 1)

                def hi1(o):
                    if F_:
                        hi(o, "h1_act", "h1_hi", fbh, "h2_done", FC * f)

                def hi2(o):
                    if F_:
                        hi(o, "h2_act", "h2_hi", fah, "h1_done", FC * f + FC)

                if A_:
                    vT = pk[:, :, SV, :]
                    dve.wait_ge(*after("o_copied", CN * a + CN))
                    tt(by_chunk(a3[:, :]), by_chunk(oT[:, :]), vT, ALU.subtract).then_inc(S["mix_o"], 1)
                    dve.wait_ge(*after("mix_act", a + 1))
                    dve.wait_ge(S["mix_o"], 2 * a + 1)
                    stt(a3[:, :], a4[:, :], 1.0, a3[:, :], ALU.add, ALU.mult).then_inc(S["mix_o"], 1)
                    dve.wait_ge(S["mix_o"], 2 * a + 2)
                    stt(by_chunk(a1[:, :]), by_chunk(a3[:, :]), 0.5, vT, ALU.mult, ALU.add).then_inc(S["o_ready"], 1)
                if M_:
                    gated(m, E - 1)
                    dve.wait_ge(*after("acc_ready", (E - 1) * (m + 1)))
                    dve.wait_ge(*after("yg_ready", E * (m + 1)))
                    tt(m1[:, :], acc[:, :], yg[:, (E - 1) % 2, :], ALU.add).then_inc(S["y2"], 1)
                if F_:
                    glu(0)
                if M_:
                    centre("2", m, m1, 0)
                if F_:
                    glu(1)
                    glu(2)
                    glu(3)
                if A_:
                    dve.wait_ge(S["ors_done"], 2 * a + 2)
                    stt(a3[:, :], a1[:, :], vec[:, V_NORM:V_NORM + 1], a5[:, :], ALU.mult, ALU.mult)\
                        .then_inc(S["og_done"], 1)
                if M_:
                    scale("2", m, m1, m3, x2).then_inc(S["x2"], 1)
                hi1(0)
                if A_:
                    dve.wait_ge(S["wo_done"], a + 1)
                    tt(by_seq(a1[:, :]), by_seq(bank[3][:, :]), xv, ALU.add).then_inc(S["y1"], 1)
                if M_:
                    dve.wait_ge(S["lru_t"], 2 * m + 1)
                    stt(m1[:, :], m1[:, :], 1.0, x2[:, :], ALU.add, ALU.mult).then_inc(S["lru_gx"], 1)
                    dve.wait_ge(S["lru_a"], 2 * m + 1)
                    ts(m4[:, :], m4[:, :], 1.0, -1e-19, ALU.subtract, ALU.min).then_inc(S["lru_m"], 1)
                    dve.wait_ge(S["lru_mult"], m + 1)
                    dve.wait_ge(S["lru_gx"], m + 1)
                    stt(m1[:, :], m1[:, :], 0.5, m4[:, :], ALU.mult, ALU.mult).then_inc(S["lru_b"], 1)
                    dve.wait_ge(S["lru_b"], m + 1)
                    dve.wait_ge(*after("hst_ready", m))
                    for b in range(B):
                        c = slice(b * TOK, (b + 1) * TOK)
                        i = V.tensor_tensor_scan(m2[:, c], m3[:, c], m1[:, c], hst[:, b:b + 1], ALU.mult, ALU.add)
                    i.then_inc(S["lru_scan"], 1)
                    dve.wait_ge(S["lru_scan"], m + 1)
                    V.tensor_copy(hst[:, :], m2[:, TOK - 1:W:TOK]).then_inc(S["hst_ready"], 1)
                    tt(m1[:, :], m2[:, :], x2[:, :], ALU.add).then_inc(S["y3"], 1)
                hi1(1)
                if A_:
                    centre("1", a, a1, 2)
                hi1(2)
                if A_:
                    dve.wait_ge(*after("gelu_done", 3 * E * a))
                    scale("1", a, a1, a4, x1).then_inc(S["x1_hi"], 1)
                    dve.wait_ge(S["x1_hi"], 2 * a + 1)
                    V.tensor_copy(x1h[:, :], x1[:, :]).then_inc(S["x1_hi"], 1)
                    dve.wait_ge(S["x1_hi"], 2 * a + 2)
                    tt(x1l[:, :], x1[:, :], f32(x1h[:, :]), ALU.subtract).then_inc(S["x1"], 1)
                hi1(3)
                if M_:
                    centre("3", m, m1, 0)
                hi2(0)
                if A_:
                    dve.wait_ge(S["r_done"], a + 1)
                    V.tensor_copy(lg[:, :, :], bank[2][:, 0:B * E].rearrange("p (b e) -> p b e", b=B))\
                        .then_inc(S["lg_ready"], 1)
                    dve.wait_ge(*after("lg_ready", a + 1))
                    V.memset(mf[:, :, :], 0.0)
                    for b in range(B):
                        i = V.max(mx[:, b, :], lg[:, b, :])
                    i.then_inc(S["tk1"], 1)
                    dve.wait_ge(S["tk1"], a + 1)
                    tt(gw[:, :, 1], mx[:, :, 0], mx[:, :, 1], ALU.subtract).then_inc(S["tk3"], 1)
                    for b in range(B):
                        i = V.max_index(mi[:, b, :], mx[:, b, :], lg[:, b, :])
                    i.then_inc(S["tk2"], 1)
                    dve.wait_ge(S["tk2"], a + 1)
                    V.tensor_copy(mf[:, :, :], mi[:, :, 0:2]).then_inc(S["tk4"], 1)
                    dve.wait_ge(S["tk4"], a + 1)
                    for s in range(2):
                        i = tt(gt2[:, :, s, :], rep(iota[:, :].rearrange("p (o e) -> p o e", o=1), 1, B),
                               rep(mf[:, :, s:s + 1], 2, E), ALU.is_equal)
                    i.then_inc(S["tk5"], 1)
                hi2(1)
                if A_:
                    dve.wait_ge(S["th_done"], a + 1)
                    ts(gw[:, :, 1], gw[:, :, 0], -0.5, 0.5, ALU.mult, ALU.add).then_inc(S["tk6"], 1)
                    dve.wait_ge(S["tk6"], 2 * a + 1)
                    ts(gw[:, :, 0], gw[:, :, 0], 0.5, 0.5, ALU.mult, ALU.add).then_inc(S["tk6"], 1)
                    dve.wait_ge(S["tk6"], 2 * a + 2)
                    dve.wait_ge(S["tk5"], a + 1)
                    for s in range(2):
                        i = tt(gt2[:, :, s, :], gt2[:, :, s, :], rep(gw[:, :, s:s + 1], 2, E), ALU.mult)
                    i.then_inc(S["tk7"], 1)
                    dve.wait_ge(S["tk7"], a + 1)
                    tt(gate[:, :, :], gt2[:, :, 0, :], gt2[:, :, 1, :], ALU.add).then_inc(S["gate_ready"], 1)
                hi2(2)
                hi2(3)
                if A_:
                    dve.wait_ge(S["gtp_done"], a + 1)
                    V.tensor_copy(gtT[0:E, :], bank[3][0:E, :]).then_inc(S["gt_hi"], 1)
                    dve.wait_ge(S["gt_hi"], a + 1)
                    tt(gtT[32:32 + E, :], bank[3][0:E, :], f32(gtT[0:E, :]), ALU.subtract).then_inc(S["gt_ready"], 1)
                if F_:
                    dve.wait_ge(*after("w3_done", f + 1))
                    dve.wait_ge(*after("out_stored", 16 * f))
                    stt(f1[:, :], bank[4][:, :], vec[:, V_S3:V_S3 + 1], x3[:, :], ALU.mult, ALU.add)\
                        .then_inc(S["y4"], 1)
                if M_:
                    if F_:
                        dve.wait_ge(*after("y4", f + 1))
                    scale("3", m, m1, m3, x3).then_inc(S["x3_hi"], 1)
                    dve.wait_ge(S["x3_hi"], 2 * m + 1)
                    V.tensor_copy(x3h[:, :], x3[:, :]).then_inc(S["x3_hi"], 1)
                    dve.wait_ge(S["x3_hi"], 2 * m + 2)
                    tt(x3l[:, :], x3[:, :], f32(x3h[:, :]), ALU.subtract).then_inc(S["x3_ready"], 1)

            schedule(dve, dense, tails)


def _layout(a):
    f = lambda n: np.asarray(a[n], dtype=np.float32)
    T = lambda m: np.ascontiguousarray(m.T)
    x = f("L0_attn_hidden_states")
    xp = np.pad(x, ((0, 0), (HALO, 0), (0, 0)))
    xh = np.stack([xp[b, t * TOK:t * TOK + TOK + HALO].T for t in list(range(NT)) + [NT - 1] for b in range(B)], axis=1)
    order = ("k", "q", "v")
    wqkv = np.stack([f(f"L0_attn_W{m}").T for m in order], axis=1)
    conv = np.stack([np.broadcast_to(f(f"L0_attn_conv_{m}").T[None], (128, TAPS, 128)) for m in order], axis=1)
    rep = lambda m: np.repeat(m, DK, axis=0).T

    def blocks(w):
        out = np.zeros((128, 128), np.float32)
        s = w.shape[1]
        for h in range(w.shape[0]):
            out[h * s:(h + 1) * s, h * s:(h + 1) * s] = w[h]
        return out

    wsm = np.stack([rep(f("L0_attn_Wb")), rep(f("L0_attn_Wmix")), f("L0_attn_Wo").T,
                    blocks(f("L1_attn_w_in")), blocks(f("L1_attn_w_a"))], axis=1)
    p = np.arange(128)
    cst = np.zeros((128, N_CONST), np.float32)
    cst[:, C_ID:C_ID + 128] = np.eye(128)
    cst[:, C_MEAN:C_MEAN + 128] = 1.0 / D
    cst[:, C_HEAD:C_HEAD + 128] = (p[:, None] // DK) == (p[None] // DK)
    cst[:, C_CAUSAL:C_CAUSAL + 32] = np.arange(32)[None] >= (p[:, None] % 32)
    cst[:, C_EYE:C_EYE + 32] = np.arange(32)[None] == (p[:, None] % 32)
    for e in range(E):
        cst[[e, 32 + e], C_SEL + e] = 1.0
    vec = np.zeros((128, N_VEC), np.float32)
    cols = lambda v: v.reshape(-1, 128).T
    vec[:, V_S1:V_S1 + FC] = cols(f("L1_ffn_w1_s"))
    vec[:, V_S2:V_S2 + FC] = cols(f("L1_ffn_w2_s"))
    vec[:, V_HS1:V_HS1 + FC] = cols(f("L1_ffn_h1_s"))
    vec[:, V_HS2:V_HS2 + FC] = cols(f("L1_ffn_h2_s"))
    vec[:, V_S3:V_S3 + 1] = cols(f("L1_ffn_w3_s"))
    vec[:, V_NORM] = np.tile(f("L0_attn_norm_w"), NH)
    vec[:, V_AP] = f("L1_attn_a_param")
    vec[:, V_EPS] = LN_EPS
    vec[:, V_L2E] = L2_EPS
    w1 = f("L0_ffn_w1").transpose(2, 0, 1).reshape(128, E * HID)
    w2 = f("L0_ffn_w2").reshape(E, 128, HC, 128).transpose(3, 0, 2, 1).reshape(128, E * HC * 128)
    kc = lambda w: w.T.reshape(FC, 128, -1).transpose(1, 0, 2)
    ins = dict(xh=xh, wqkv=wqkv, conv=conv, wsm=wsm, cst=cst, vec=vec, wr=f("L0_ffn_router_w").T, wm=np.concatenate([w1, w2], axis=1),
               wf=np.concatenate([m.reshape(128, -1) for m in (
                   f("L1_ffn_w1_w").T, f("L1_ffn_w2_w").T, kc(f("L1_ffn_h1_w")), kc(f("L1_ffn_h2_w")),
                   kc(f("L1_ffn_w3_w")))], axis=1), iota=np.broadcast_to(np.arange(E, dtype=np.float32), (128, E)))
    return {n: np.ascontiguousarray(v) for n, v in ins.items()}


def program(nc, ins):
    io = {n: nc.dram_tensor(f"in_{n}", v.shape, F32, kind="ExternalInput").ap() for n, v in ins.items()}
    io["out"] = nc.dram_tensor("out_0", (128, NT * W), F32, kind="ExternalOutput").ap()
    io["pack"] = nc.dram_tensor("pack", (128, NC, NPACK - 1, C), F32, kind="Internal").ap()
    io["tt"] = nc.dram_tensor("tt", (128, NC, C), F32, kind="Internal").ap()
    build(nc, io)


def kernel(**inputs):
    import concourse.bacc as bacc
    from concourse.bass_utils import run_bass_kernel_spmd

    ins = _layout(inputs)
    nc = bacc.Bacc("TRN2", target_bir_lowering=False, num_devices=1)
    program(nc, ins)
    r = run_bass_kernel_spmd(nc, [{f"in_{n}": v for n, v in ins.items()}], core_ids=[0])
    out = r.results[0]["out_0"]
    return out.reshape(128, NT, B, TOK).transpose(2, 1, 3, 0).reshape(B, L, D)
```

```python
from contextlib import ExitStack

import numpy as np
import concourse.bass as bass
import concourse.mybir as mybir
from concourse.alu_op_type import AluOpType as ALU

F32 = mybir.dt.float32
F32R = mybir.dt.float32r
U32 = mybir.dt.uint32
ACT = mybir.ActivationFunctionType
AX = mybir.AxisListType

B, L, D = 4, 1024, 128
NH, DK, C = 4, 32, 32
TOK = 128
NT = L // TOK
W = B * TOK
CN = TOK // C
CT = B * CN
NC = NT * CT
TAPS = 4
HALO = TAPS - 1
E, HID = 8, 256
HC = HID // 128
FF = 512
FC = FF // 128
LN_EPS, RMS_EPS, L2_EPS = 1e-5, 1e-5, 1e-6
WF = 2 * FF + 2 * FC * FF + FC * 128
WM = 2 * E * HID
WCH = WF // NT
SK, SQ, SV, SATT, SKT, SVT = range(6)
NPACK = 6
C_ID, C_MEAN, C_HEAD, C_CAUSAL, C_EYE, C_SEL = 0, 128, 256, 384, 416, 448
N_CONST = C_SEL + E
V_S1, V_S2, V_HS1, V_HS2, V_S3, V_NORM, V_AP = 0, 4, 8, 12, 16, 17, 18
V_EPS, V_L2E, N_VEC = 19, 20, 21


def build(nc, io):
    ctx = ExitStack()
    with ctx:
        top = [(nc.sbuf_base + 63) // 64 * 64]

        def cols(shape):
            n = 4
            for d in shape[1:]:
                n *= d
            return (n + 31) // 32 * 32

        def over(name, shape, dt, at):
            return nc.alloc_sbuf_tensor_at(name, shape, dt, offset=at)

        def sb(name, shape, dt=F32):
            at = top[0]
            top[0] += cols(shape)
            return over(name, shape, dt, at)

        def ps(name):
            return ctx.enter_context(nc.psum_tensor(name, [128, 512], F32))

        def sem(name):
            return ctx.enter_context(nc.semaphore(name))

        cst = sb("cst", [128, N_CONST])
        vec = sb("vec", [128, N_VEC])
        ident = cst[:, C_ID:C_ID + 128]
        mean_w = cst[:, C_MEAN:C_MEAN + 128]
        head_w = cst[:, C_HEAD:C_HEAD + 128]
        causal = cst[:, C_CAUSAL:C_CAUSAL + 32]
        eye = cst[:, C_EYE:C_EYE + 32]
        sel = sb("sel", [40, E], F32R)
        wsm = sb("wsm", [128, 5, 128])
        wr = sb("wr", [128, E])
        beta_tok = sb("beta_tok", [128, NC])
        lg = sb("lg", [128, B, E]); mx = sb("mx", [128, B, 8]); mi = sb("mi", [128, B, 8], U32)
        mf = sb("mf", [128, B, 2]); gw = sb("gw", [128, B, 2]); gt2 = sb("gt2", [128, B, 2, E])
        gate = sb("gate", [128, B, E]); iota = sb("iota", [128, E])
        hst = sb("hst", [128, B])
        spv = sb("spv", [128, 12])
        gtT = sb("gtT", [64, W], F32R)
        at_x = top[0]
        x1 = sb("x1", [128, W]); x1h = sb("x1h", [128, W], F32R); x1l = sb("x1l", [128, W], F32R)
        x2 = sb("x2", [128, W])
        x3 = sb("x3", [128, W]); x3h = sb("x3h", [128, W], F32R); x3l = sb("x3l", [128, W], F32R)
        acc = sb("acc", [128, W])
        gb = sb("gb", [128, 2, W]); yg = sb("yg", [128, 2, W]); hf = sb("hf", [128, 2, W])
        a1, a2, a3, a4, a5, oT = (sb(n, [128, W]) for n in ("a1", "a2", "a3", "a4", "a5", "oT"))
        temps = top[0]
        m1, m2, m3, m4 = (sb(n, [128, W]) for n in ("m1", "m2", "m3", "m4"))
        f1, f2, f3 = (sb(n, [128, W]) for n in ("f1", "f2", "f3"))
        pk = sb("pk", [128, CT, NPACK, C])
        xt = sb("xt", [128, B, TOK + HALO])
        xv = xt[:, :, HALO:HALO + TOK]
        xth = sb("xth", [128, B, TOK + HALO], F32R); xtl = sb("xtl", [128, B, TOK + HALO], F32R)
        tb = sb("tb", [128, B, CN, C])
        at_texp = top[0]
        texp = sb("texp", [128, 2, B, NH, C])
        spread = sb("spread", [128, 8, NH, C])
        sexp = sb("sexp", [128, B, NH, DK])
        qpc = sb("qpc", [128, B, 2, C])
        ws = sb("ws", [128, WCH])
        at_fa = top[0]
        fah = sb("fah", [128, FC, W], F32R); fal = sb("fal", [128, FC, W], F32R)
        at_fb = top[0]
        fbh = sb("fbh", [128, FC, W], F32R); fbl = sb("fbl", [128, FC, W], F32R)
        at_wm = top[0]
        wmh = sb("wmh", [128, WM], F32R); wml = sb("wml", [128, WM], F32R)
        wfh = sb("wfh", [128, WF], F32R); wfl = sb("wfl", [128, WF], F32R)
        assert top[0] <= nc.sbuf_usable_end, top[0]
        wqkv = over("wqkv", [128, 3, 128], F32, temps)
        conv = over("conv", [128, 3, TAPS, 128], F32, temps + 2048)
        tmpv = over("tmpv", [128, 768], F32, temps)
        tmpg = over("tmpg", [128, 256], F32, temps + 4096)
        wtap = over("wtap", [128, 3, TAPS, 128], F32, at_wm)
        wtaph = over("wtaph", [128, 3, TAPS, 128], F32R, at_fa)
        wtapl = over("wtapl", [128, 3, TAPS, 128], F32R, at_fa + 6144)
        stg = over("stg", [128, WM], F32, at_x)
        kkc = over("kkc", [128, NC, C], F32, at_fb)
        ttc = over("ttc", [128, NC, C], F32, at_fa)
        opa, opt = over("opa", [128, NH * C * C], F32, at_fa), over("opt", [128, NH * C * C], F32, at_fb)
        apm = opa[:, :].rearrange("p (j h i) -> p j h i", j=C, h=NH)
        tpr = opt[:, :].rearrange("p (i n) -> p i n", i=C)
        tpm = opt[:, :].rearrange("p (i h j) -> p h i j", h=NH, i=C)
        bank = [ps(f"bank{i}") for i in range(8)]
        i1 = at_wm + 6144
        xsh = [xth, over("xth1", [128, B, TOK + HALO], F32R, i1)]
        xsl = [xtl, over("xtl1", [128, B, TOK + HALO], F32R, i1 + 2112)]
        pks = [pk, over("pk1", [128, CT, NPACK, C], F32, i1 + 4224)]
        act_kqv = [[a3, a4, a5], [over(n, [128, W], F32, i1 + 16512 + 2048 * i) for i, n in enumerate(("k1", "q1", "v1"))]]
        squ = [[a1, a2], [f1, f2]]
        rnorm = [[hf[:, 0, :], hf[:, 1, :]], [acc[:, :], f3[:, :]]]
        kspread = [spread, over("spread1", [128, 8, NH, C], F32, at_texp)]

        O_G, O_U, O_H1, O_H2, O_W3 = 0, FF, 2 * FF, 2 * FF + FC * FF, 2 * FF + 2 * FC * FF
        O_UP, O_DN = 0, E * HID

        names = """w_in cst_in conv_in x_in pk_stored pk_loaded tb_in fw_in ws_in ws_hi ws_lo wm_in wm_hi wm_lo tt_stored
            wtap_f wtap_hi wtap_done xt_hi xt_ready
            beta_proj qkv_proj qkv_act sq_done ss_done rs_ln rs_act kq_done qn_done kv_tok kexp_done gram_done
            bt_ready beta_tmp beta_tok_done gram_read v_done
            kkt_done kkt_read tinit tv_mul tv_step tg_mul tg_step tt_done tt_read s_zero sp_step
            texp_ready m2_done wu_ready m4_done qp_step os_done s_ready o_copied
            mixl_done mix_act mix_o o_ready osq_done oss_done ors_done og_done wo_done x1_hi
            r_done lg_ready tk1 tk2 tk3 tk4 tk5 th_done tk6 tk7 gate_ready gtp_done gt_hi gt_ready
            gbp_done gb_ready up_done gelu_done hi1 lo0 lo1 dn_done yg_ready acc_ready
            lru_proj lru_t lru_a lru_m lru_l lru_mult lru_gx lru_b lru_scan hst_ready x3_hi x3_ready
            g_done u_done g_act glu_f glu_hi fa_ready h1_done h1_act h1_hi fb_ready h2_done h2_act h2_hi f2_ready
            w3_done out_stored""".split()
        S = {n: sem(n) for n in names}
        for n in "1234":
            for k in ("y", "mu", "d", "sq", "var", "rs", "x"):
                S[k + n] = sem(f"ln{n}_{k}")
        START = """beta_proj qkv_proj qkv_act sq_done ss_done rs_ln rs_act kq_done qn_done gram_done bt_ready beta_tmp
            gram_read v_done kexp_done ws_lo m2_done wu_ready qp_step os_done s_ready o_copied x1 y2 y4
            dn_done lo0 lo1 gelu_done yg_ready acc_ready gb_ready w3_done gt_ready rs3 d3 d1 lg_ready mix_act
            hst_ready out_stored pk_stored fa_ready h1_done h2_done fb_ready x4 o_ready y1 rs4 d4 x3_ready
            g_act glu_f""".split()

        CREDIT = {n: 1 for n in START}
        CREDIT.update(qn_done=2, kq_done=3, gram_read=3, gram_done=3, ss_done=3, v_done=2, pk_stored=17, qkv_proj=4,
                      qkv_act=3)

        def after(name, n):
            return S[name], n + CREDIT.get(name, 0)

        block = ctx.enter_context(nc.Block())
        V, A, P, G = nc.vector, nc.scalar, nc.tensor, nc.gpsimd

        def rep(ap, axis, n):
            shape = list(ap.shape)
            shape[axis] = n
            return ap.broadcast_to(shape)

        def heads(n):
            return rep(cst[:, C_HEAD:C_HEAD + 128].rearrange("p (o h c) -> p o h c", o=1, h=NH), 1, n)

        def f32(ap):
            return ap.bitcast(F32)

        def by_seq(ap):
            return ap.rearrange("p (b n) -> p b n", b=B)

        LN_EXP = "natural_log_exp_and_others"

        def by_chunk(ap):
            return ap.rearrange("p (c i) -> p c i", c=CT)

        def tiles_of_stage1(eng, body):
            with eng.Fori(0, NT // 2 - 1) as u:
                for s in range(2):
                    body(u * 2 + s, s)
            for t in (NT - 2, NT - 1):
                body(t, t % 2)

        def schedule(eng, dense, tails):
            dense(None, 0, None)
            tails(None, None, 0, None)
            dense(0, 1, None)
            tails(None, 0, 1, None)
            dense(1, 2, None)
            tails(0, 1, 2, None)
            dense(2, 3, 0)
            with eng.Fori(2, NT - 2) as t:
                tails(t - 1, t, t + 1, t - 2)
                dense(t + 1, t + 2, t - 1)
            tails(NT - 3, NT - 2, NT - 1, NT - 4)
            dense(NT - 1, None, NT - 3)
            tails(NT - 2, NT - 1, None, NT - 3)
            dense(None, None, NT - 2)
            tails(NT - 1, None, None, NT - 2)
            dense(None, None, NT - 1)
            tails(None, None, None, NT - 1)

        @block.sync
        def _(sp):
            def load_x(t):
                sp.dma_start(xt[:, :, :], io["xh"][:, bass.ds(t * B, B), :]).then_inc(S["x_in"], 16)

            def load_tb(t):
                sp.dma_start(tb[:, :, :, :].rearrange("p b n c -> p (b n) c"),
                             io["tt"][:, bass.ds(t * CT, CT), :]).then_inc(S["tb_in"], 16)

            def load_tile(t):
                sp.wait_ge(*after("o_ready", t))
                sp.dma_start(pk[:, :, 1:, :], io["pack"][:, bass.ds(t * CT, CT), :, :]).then_inc(S["pk_loaded"], 16)
                load_tb(t)
                sp.wait_ge(*after("y1", t))
                load_x(t)

            def store_out(t):
                sp.wait_ge(*after("x4", t + 1))
                sp.dma_start(io["out"][:, bass.ds(t * W, W)], f1[:, :]).then_inc(S["out_stored"], 16)

            sp.dma_start(wqkv[:, :, :], io["wqkv"]).then_inc(S["conv_in"], 16)
            sp.dma_start(conv[:, :, :, :], io["conv"]).then_inc(S["conv_in"], 16)
            load_x(0)
            sp.dma_start(wsm[:, :, :], io["wsm"]).then_inc(S["w_in"], 16)
            sp.dma_start(vec[:, :], io["vec"]).then_inc(S["w_in"], 16)
            sp.dma_start(cst[:, :], io["cst"]).then_inc(S["cst_in"], 16)
            sp.dma_start(wr[:, :], io["wr"]).then_inc(S["fw_in"], 16)
            sp.dma_start(iota[:, :], io["iota"]).then_inc(S["fw_in"], 16)

            def load_ws(t):
                sp.wait_ge(*after("ws_lo", t))
                sp.dma_start(ws[:, :], io["wf"][:, bass.ds(t * WCH, WCH)]).then_inc(S["ws_in"], 16)

            def next_x(t):
                sp.wait_ge(*after("qkv_proj", 3 * (t - 1) + 1))
                load_x(t)

            def stage1(t, s):
                if not isinstance(t, int) or t + 1 < NT:
                    load_ws(t + 1)
                if not isinstance(t, int) or t + 2 < NT:
                    next_x(t + 2)
                sp.wait_ge(*after("gram_read", 2 * t + 2))
                sp.wait_ge(*after("pk_stored", 16 * t))
                sp.dma_start(io["pack"][:, bass.ds(t * CT, CT), :, :], pks[s][:, :, 1:, :]).then_inc(S["pk_stored"], 16)

            load_ws(0)
            next_x(1)
            tiles_of_stage1(sp, stage1)
            sp.wait_ge(*after("kq_done", 2 * NT))
            sp.dma_start(stg[:, :], io["wm"]).then_inc(S["wm_in"], 16)
            sp.wait_ge(*after("qkv_proj", 3 * NT))
            load_x(0)
            sp.wait_ge(*after("pk_stored", 16 * NT))
            sp.dma_start(pk[:, :, 1:, :], io["pack"][:, 0:CT, :, :]).then_inc(S["pk_loaded"], 16)
            sp.wait_ge(S["tt_read"], 8)
            sp.dma_start(io["tt"], ttc[:, :, :]).then_inc(S["tt_stored"], 16)
            sp.wait_ge(S["tt_stored"], 16)

            def dense(m, a, f):
                pass

            def tails(f, m, a, l):
                if a is not None and (not isinstance(a, int) or a < NT - 1):
                    load_tile(a + 1)
                if l is not None:
                    store_out(l)

            schedule(sp, dense, tails)
            sp.wait_ge(*after("out_stored", 16 * NT))

        @block.tensor
        def _(pe):
            def mm(out, lhsT, rhs, start=True, stop=True, skip=False):
                return P.matmul(out, lhsT, rhs, start=start, stop=stop, skip_group_check=skip)

            def mm3(out, wh, wl, xh, xl, start=True, stop=True):
                mm(out, wh, xl, start=start, stop=False)
                mm(out, wl, xh, start=False, stop=False)
                return mm(out, wh, xh, start=False, stop=stop)

            def flat(ap):
                return ap.rearrange("p h c -> p (h c)")

            def project(t, s):
                pe.wait_ge(S["x_in"], 16 * t + 16)
                pe.wait_ge(*after("bt_ready", t))
                mm(by_seq(bank[3][:, :]), wsm[:, 0, :], xv).then_inc(S["beta_proj"], 1)
                pe.wait_ge(S["xt_ready"], t + 1)
                for m in range(3):
                    pe.wait_ge(*after("qkv_act", 3 * (t - 1) + m + 1))
                    for k in range(TAPS):
                        i = mm3(by_seq(bank[m][:, :]), wtaph[:, m, k, :], wtapl[:, m, k, :],
                                xsh[s][:, :, k:k + TOK], xsl[s][:, :, k:k + TOK], start=k == 0, stop=k == TAPS - 1)
                    i.then_inc(S["qkv_proj"], 1)

            def squares(t, s):
                for m in range(2):
                    pe.wait_ge(*after("sq_done", 2 * t + m + 1))
                    pe.wait_ge(*after("rs_ln", 2 * t))
                    mm(bank[4 + m][:, :], head_w, squ[s][m][:, :]).then_inc(S["ss_done"], 1)

            def gram(t, s):
                for g in range(2):
                    pe.wait_ge(*after("qn_done", t + 1))
                    pe.wait_ge(*after("kexp_done", 2 * t + g + 1))
                    pe.wait_ge(*after("gram_read", 2 * t))
                    for c in range(8):
                        i = mm(bank[6 + g][:, c * 64:(c + 1) * 64], flat(kspread[g][:, c, :, :]),
                               flat(pks[s][:, g * 8 + c, SK:SQ + 1, :]))
                    i.then_inc(S["gram_done"], 1)

            pe.wait_ge(S["w_in"], 32)
            pe.wait_ge(S["wtap_done"], 1)

            def stage1(t, s):
                squares(t, s)
                if not isinstance(t, int) or t + 1 < NT:
                    project(t + 1, 1 - s)
                gram(t, s)

            project(0, 0)
            pe.wait_ge(S["cst_in"], 16)
            tiles_of_stage1(pe, stage1)
            pe.wait_ge(*after("gram_read", 2 * NT))
            for g in range(8):
                if g >= 2:
                    pe.wait_ge(S["kkt_read"], g - 1)
                for j in range(4):
                    i = P.transpose(bank[g % 2][:, j * 128:(j + 1) * 128], kkc[:, :, 4 * g + j], ident)
                i.then_inc(S["kkt_done"], 1)
            pe.wait_ge(S["tv_step"], C - 1)
            pe.wait_ge(S["tg_step"], C - 1)
            pe.wait_ge(S["kkt_read"], 8)
            for g in range(8):
                if g >= 2:
                    pe.wait_ge(S["tt_read"], g - 1)
                for j in range(4):
                    i = P.transpose(bank[g % 2][:, j * 128:(j + 1) * 128], tpr[:, 4 * g + j, :], ident)
                i.then_inc(S["tt_done"], 1)
            pe.wait_ge(S["tt_read"], 8)
            pe.wait_ge(S["s_zero"], 1)
            pe.wait_ge(S["fw_in"], 32)
            pe.wait_ge(S["wm_lo"], 1)
            pe.wait_ge(*after("ws_lo", NT))

            def mean_product(n, t, src, bk):
                pe.wait_ge(*after("y" + n, t + 1))
                mm(bank[bk][:, :], mean_w, src[:, :]).then_inc(S["mu" + n], 1)

            def var_product(n, t, src, bk):
                pe.wait_ge(S["sq" + n], t + 1)
                mm(bank[bk][:, :], mean_w, src[:, :]).then_inc(S["var" + n], 1)

            def delta_wu(t, n):
                pe.wait_ge(S["texp_ready"], CN * t + n + 1)
                pe.wait_ge(S["pk_loaded"], 16 * t + 16)
                pe.wait_ge(*after("wu_ready", CN * t + n))
                for b in range(B):
                    i = mm(bank[0][:, b * 64:(b + 1) * 64], flat(texp[:, n % 2, b, :, :]),
                           flat(pk[:, b * CN + n, SKT:SVT + 1, :]))
                i.then_inc(S["m2_done"], 1)

            def delta_attn(t, n):
                k = CN * t + n
                pe.wait_ge(*after("wu_ready", k + 1))
                pe.wait_ge(*after("qp_step", 2 * k))
                for b in range(B):
                    i = mm(bank[1][:, b * 64:(b + 1) * 64], flat(spread[:, 2 * b, :, :]),
                           flat(pk[:, b * CN + n, SATT:SKT + 1, :]))
                i.then_inc(S["m4_done"], 1)
                pe.wait_ge(*after("o_copied", k))
                for b in range(B):
                    mm(bank[2][:, b * 64:(b + 1) * 64], flat(spread[:, 2 * b + 1, :, :]),
                       flat(pk[:, b * CN + n, SATT:SKT + 1, :]), start=b == 0, stop=False, skip=True)

            def delta_state(t, n):
                k = CN * t + n
                pe.wait_ge(*after("qp_step", 2 * k + 2))
                pe.wait_ge(*after("s_ready", k))
                for b in range(B):
                    i = mm(bank[2][:, b * 64:(b + 1) * 64], flat(sexp[:, b, :, :]),
                           flat(qpc[:, b, :, :]), start=False, stop=b == B - 1, skip=True)
                i.then_inc(S["os_done"], 1)

            def up(t, e):
                pe.wait_ge(*after("x1", t + 1))
                for c in range(HC):
                    pe.wait_ge(*after("gelu_done", 3 * (E * t + e) - 1 + c if e else 3 * E * t))
                    o = O_UP + e * HID + c * 128
                    mm3(bank[4 + c][:, :], wmh[:, o:o + 128], wml[:, o:o + 128], x1h[:, :], x1l[:, :])\
                        .then_inc(S["up_done"], 1)

            def gate_rows(t, e):
                pe.wait_ge(*after("gt_ready", t + 1))
                pe.wait_ge(*after("gb_ready", E * t + e))
                mm(bank[7][:, :], sel[0:40, e:e + 1].broadcast_to([40, 128]), gtT[0:40, :]).then_inc(S["gbp_done"], 1)

            def down(t, e):
                pe.wait_ge(*after("lo0", E * t + e + 1))
                pe.wait_ge(*after("yg_ready", E * t + e))
                for c in range(HC):
                    if c == 1:
                        pe.wait_ge(*after("lo1", E * t + e + 1))
                    o, s = O_DN + (e * HC + c) * 128, (e % 2) * HC + c
                    i = mm3(bank[6][:, :], wmh[:, o:o + 128], wml[:, o:o + 128], fbh[:, s, :], fbl[:, s, :],
                            start=c == 0, stop=c == HC - 1)
                i.then_inc(S["dn_done"], 1)

            def dense(m, a, f):
                if a is not None:
                    pe.wait_ge(*after("lg_ready", a))
                    delta_wu(a, 0)
                for e in range(E):
                    if m is not None:
                        up(m, e)
                        gate_rows(m, e)
                    if e == 0 and f is not None:
                        output_product(f)
                    if a is not None:
                        (delta_state if e % 2 else delta_attn)(a, e // 2)
                    if f is not None and e == 1:
                        mean_product("4", f, f1, 3)
                    if a is not None and e == 4:
                        pe.wait_ge(S["x_in"], 16 * NT + 16 * a + 16)
                        if f is not None:
                            pe.wait_ge(*after("d4", f + 1))
                        mm(by_seq(bank[3][:, :]), wsm[:, 1, :], xv).then_inc(S["mixl_done"], 1)
                    if m is not None and e:
                        down(m, e - 1)
                    if a is not None and e % 2 and e < E - 1:
                        delta_wu(a, e // 2 + 1)
                    if f is not None and e == E - 1:
                        if a is not None:
                            pe.wait_ge(*after("mix_act", a + 1))
                        var_product("4", f, f2, 3)
                if m is not None:
                    down(m, E - 1)

            def output_product(f):
                for c in range(FC):
                    pe.wait_ge(S["f2_ready"], FC * f + c + 1)
                    w = O_W3 + c * 128
                    i = mm3(bank[6][:, :], wfh[:, w:w + 128], wfl[:, w:w + 128], fah[:, c, :], fal[:, c, :],
                            start=c == 0, stop=c == FC - 1)
                i.then_inc(S["w3_done"], 1)

            def glu(f, c):
                o = 4 + 2 * (c % 2)
                pe.wait_ge(*after("g_act", FC * f + max(c - 1, 0)))
                g, u = O_G + c * 128, O_U + c * 128
                mm3(bank[o][:, :], wfh[:, g:g + 128], wfl[:, g:g + 128], x3h[:, :], x3l[:, :]).then_inc(S["g_done"], 1)
                pe.wait_ge(*after("glu_f", FC * f + max(c - 1, 0)))
                mm3(bank[o + 1][:, :], wfh[:, u:u + 128], wfl[:, u:u + 128], x3h[:, :], x3l[:, :]).then_inc(S["u_done"], 1)

            def hidden(f, o, base, xh, xl, ready, done, chunks=range(FC)):
                for c, p in [(c, p) for c in chunks for p in (o, o + 1)]:
                    if o == 0 and p == 0:
                        pe.wait_ge(*after(ready, FC * f + c + 1))
                    if base == O_H2 and c == 0:
                        pe.wait_ge(S["h1_act"], FC * f + p + 1)
                    w = base + c * FF + p * 128
                    i = mm3(bank[4 + p][:, :], wfh[:, w:w + 128], wfl[:, w:w + 128], xh[:, c, :], xl[:, c, :],
                            start=c == 0, stop=c == FC - 1)
                    if c == FC - 1:
                        i.then_inc(S[done], 1)

            def tails(f, m, a, l):
                if f is not None:
                    last = f + 2 if m is not None else NT
                    pe.wait_ge(*after("x3_ready", f + 1))
                    pe.wait_ge(*after("gelu_done", 3 * E * last))
                    glu(f, 0)
                if f is not None:
                    pe.wait_ge(*after("y4", f))
                    pe.wait_ge(*after("gb_ready", E * last))
                    pe.wait_ge(*after("yg_ready", E * last))
                    glu(f, 1)
                if m is not None:
                    mean_product("2", m, m1, 0)
                if a is not None:
                    pe.wait_ge(S["osq_done"], a + 1)
                    pe.wait_ge(*after("o_copied", CN * a + CN))
                    mm(bank[2][:, :], head_w, a2[:, :]).then_inc(S["oss_done"], 1)
                if f is not None:
                    glu(f, 2)
                if m is not None:
                    var_product("2", m, m2, 1)
                if f is not None:
                    glu(f, 3)
                    pe.wait_ge(*after("g_act", FC * f + FC - 1))
                    pe.wait_ge(*after("glu_f", FC * f + FC - 1))
                    hidden(f, 0, O_H1, fah, fal, "fa_ready", "h1_done")
                    pe.wait_ge(*after("glu_f", FC * f + FC))
                if a is not None:
                    pe.wait_ge(S["og_done"], a + 1)
                    if l is not None:
                        pe.wait_ge(*after("rs4", 2 * l + 1))
                    mm(bank[3][:, :], wsm[:, 2, :], a3[:, :]).then_inc(S["wo_done"], 1)
                if m is not None:
                    pe.wait_ge(S["x2"], m + 1)
                    mm(bank[0][:, :], wsm[:, 3, :], x2[:, :]).then_inc(S["lru_proj"], 1)
                    mm(bank[1][:, :], wsm[:, 4, :], x2[:, :]).then_inc(S["lru_proj"], 1)
                if a is not None:
                    pe.wait_ge(S["ors_done"], 2 * a + 2)
                    mean_product("1", a, a1, 2)
                if f is not None:
                    hidden(f, 2, O_H1, fah, fal, "fa_ready", "h1_done")
                if a is not None:
                    var_product("1", a, a2, 3)
                if f is not None:
                    hidden(f, 0, O_H2, fbh, fbl, "fb_ready", "h2_done", range(2))
                if m is not None:
                    pe.wait_ge(S["lru_t"], 2 * m + 2)
                    mean_product("3", m, m1, 0)
                if a is not None:
                    pe.wait_ge(*after("x1", a + 1))
                    for b in range(B):
                        i = mm(bank[2][:, b * E:(b + 1) * E], x1[:, b * TOK:(b + 1) * TOK], wr[:, :])
                    i.then_inc(S["r_done"], 1)
                if f is not None:
                    hidden(f, 0, O_H2, fbh, fbl, "fb_ready", "h2_done", range(2, FC))
                if m is not None:
                    var_product("3", m, m2, 1)
                if f is not None:
                    hidden(f, 2, O_H2, fbh, fbl, "fb_ready", "h2_done")
                if a is not None:
                    pe.wait_ge(S["gate_ready"], a + 1)
                    for b in range(B):
                        i = mm(bank[3][0:E, b * TOK:(b + 1) * TOK], gate[:, b, :], ident)
                    i.then_inc(S["gtp_done"], 1)
                if f is not None:
                    pe.wait_ge(S["h2_act"], FC * f + FC)
                if m is not None:
                    pe.wait_ge(*after("d3", m + 1))
                    pe.wait_ge(*after("rs3", 2 * m + 1))

            schedule(pe, dense, tails)

        @block.scalar
        def _(act):
            eps = vec[:, V_EPS:V_EPS + 1]
            l2e = vec[:, V_L2E:V_L2E + 1]
            act.wait_ge(S["wtap_f"], 1)
            A.activation(wtaph[:, :, :, :], wtap[:, :, :, :], ACT.Copy).then_inc(S["wtap_hi"], 1)

            def stage1(t, s):
                for m in range(3):
                    dst = act_kqv[s][m]
                    act.wait_ge(*after("qkv_proj", 3 * t + m + 1))
                    act.wait_ge(*(after("kq_done", 2 * (t - 1)) if m < 2 else after("v_done", t - 1)))
                    A.activation(dst[:, :], bank[m][:, :], ACT.Silu).then_inc(S["qkv_act"], 1)
                    if m < 2:
                        act.wait_ge(*after("qkv_act", 3 * t + m + 1))
                        act.wait_ge(*after("ss_done", 2 * (t - 1)))
                        A.activation(squ[s][m][:, :], dst[:, :], ACT.Square).then_inc(S["sq_done"], 1)
                act.wait_ge(*after("beta_proj", t + 1))
                act.wait_ge(*after("beta_tmp", t))
                A.activation(gb[:, 0, :], bank[3][:, :], ACT.Tanh, scale=0.5).then_inc(S["bt_ready"], 1)
                for m in range(2):
                    act.wait_ge(*after("ss_done", 2 * t + m + 1))
                    act.wait_ge(*after("kq_done", 2 * (t - 1)))
                    A.activation(rnorm[s][m], bank[4 + m][:, :], ACT.Ln, bias=l2e).then_inc(S["rs_ln"], 1)
                for m in range(2):
                    act.wait_ge(*after("rs_ln", 2 * t + m + 1))
                    A.activation(rnorm[s][m], rnorm[s][m], ACT.Exp, scale=-0.5).then_inc(S["rs_act"], 1)
                act.wait_ge(S["ws_in"], 16 * t + 16)
                A.activation(wfh[:, bass.ds(t * WCH, WCH)], ws[:, :], ACT.Copy).then_inc(S["ws_hi"], 1)

            act.wait_ge(S["w_in"], 32)
            tiles_of_stage1(act, stage1)
            act.wait_ge(S["sp_step"], 1)
            A.activation(spv[:, 1:2], spv[:, 0:1], ACT.Exp, scale=-1.0).then_inc(S["sp_step"], 1)
            for g in range(8):
                act.wait_ge(S["kkt_done"], g + 1)
                A.activation(apm[:, 4 * g:4 * g + 4, :, :].rearrange("p j h i -> p (j h i)"), bank[g % 2][:, :],
                             ACT.Copy).then_inc(S["kkt_read"], 1)
            act.wait_ge(S["wm_in"], 16)
            act.wait_ge(*after("pk_stored", 16 * NT))
            act.wait_ge(*after("v_done", NT))
            for g in range(2):
                c = slice(g * WM // 2, (g + 1) * WM // 2)
                A.activation(wmh[:, c], stg[:, c], ACT.Copy).then_inc(S["wm_hi"], 1)

            def square(n, t, src, dst):
                act.wait_ge(*after("d" + n, t + 1) if n in "134" else (S["d" + n], t + 1))
                A.activation(dst[:, :], src[:, :], ACT.Square).then_inc(S["sq" + n], 1)

            def rstd_ln(n, t, bk, dst):
                act.wait_ge(S["var" + n], t + 1)
                A.activation(dst[:, :], bank[bk][:, :], ACT.Ln, bias=eps).then_inc(S["rs" + n], 1)

            def rstd_exp(n, t, dst):
                act.wait_ge(*after("rs" + n, 2 * t + 1) if n in "34" else (S["rs" + n], 2 * t + 1))
                A.activation(dst[:, :], dst[:, :], ACT.Exp, scale=-0.5).then_inc(S["rs" + n], 1)

            def dense(m, a, f):
                for e in range(E):
                    if m is not None:
                        k = E * m + e
                        s = (e % 2) * HC
                        act.wait_ge(S["up_done"], HC * k + 1)
                        act.wait_ge(*after("lo0", k))
                        if e == 0 and f is not None:
                            act.wait_ge(S["f2_ready"], FC * f + 3)
                        A.activation(hf[:, 0, :], bank[4][:, :], ACT.Gelu).then_inc(S["gelu_done"], 1)
                        act.wait_ge(*after("dn_done", E * m + max(e - 1, 0)))
                        A.activation(fbh[:, s, :], bank[4][:, :], ACT.Gelu).then_inc(S["gelu_done"], 1)
                        act.wait_ge(S["up_done"], HC * k + 2)
                        act.wait_ge(*after("lo1", k))
                        if e == 0 and f is not None:
                            act.wait_ge(S["f2_ready"], FC * f + 4)
                        A.activation(hf[:, 1, :], bank[5][:, :], ACT.Gelu).then_inc(S["gelu_done"], 1)
                        act.wait_ge(S["gbp_done"], k + 1)
                        act.wait_ge(*after("yg_ready", E * m + max(e - 1, 0)))
                        A.activation(gb[:, e % 2, :], bank[7][:, :], ACT.Copy).then_inc(S["gb_ready"], 1)
                    if a is not None and e == 5:
                        act.wait_ge(S["mixl_done"], a + 1)
                        act.wait_ge(*after("x1", a))
                        A.activation(a4[:, :], bank[3][:, :], ACT.Tanh, scale=0.5).then_inc(S["mix_act"], 1)
                    if f is not None and e == 3:
                        square("4", f, f1, f2)

            def silu(f, c):
                act.wait_ge(S["g_done"], FC * f + c + 1)
                act.wait_ge(*after("glu_f", FC * f + max(c - 1, 0)))
                A.activation(gb[:, c % 2, :], bank[4 + 2 * (c % 2)][:, :], ACT.Silu,
                             scale=vec[:, V_S1 + c:V_S1 + c + 1]).then_inc(S["g_act"], 1)

            def gelu(f, o, done, acted, v, free, n):
                act.wait_ge(S[done], FC * f + o + 1 + (1 if done in START else 0))
                act.wait_ge(*after(free, n))
                A.activation(hf[:, o % 2, :], bank[4 + o][:, :], ACT.Gelu, scale=vec[:, v + o:v + o + 1])\
                    .then_inc(S[acted], 1)

            def gelu1(f, o):
                if o < 2:
                    gelu(f, o, "h1_done", "h1_act", V_HS1, "fa_ready", FC * f + 3 + o)
                else:
                    gelu(f, o, "h1_done", "h1_act", V_HS1, "fb_ready", FC * f + o - 1)

            def gelu2(f, o):
                if o < 2:
                    gelu(f, o, "h2_done", "h2_act", V_HS2, "fb_ready", FC * f + 3 + o)
                else:
                    gelu(f, o, "h2_done", "h2_act", V_HS2, "f2_ready", FC * f + o - 1)

            def tails(f, m, a, l):
                F_, M_, A_, L_ = f is not None, m is not None, a is not None, l is not None
                if F_:
                    act.wait_ge(*after("yg_ready", E * (f + 2 if M_ else NT)))
                    silu(f, 0)
                if A_:
                    act.wait_ge(*after("o_ready", a + 1))
                    A.activation(a2[:, :], a1[:, :], ACT.Square).then_inc(S["osq_done"], 1)
                if F_:
                    silu(f, 1)
                if M_:
                    square("2", m, m1, m2)
                if F_:
                    silu(f, 2)
                    silu(f, 3)
                if A_:
                    act.wait_ge(S["oss_done"], a + 1)
                    A.activation(a5[:, :], bank[2][:, :], ACT.Ln, scale=1.0 / DK, bias=eps).then_inc(S["ors_done"], 1)
                if L_:
                    rstd_ln("4", l, 3, f3)
                if M_:
                    rstd_ln("2", m, 1, m3)
                if A_:
                    act.wait_ge(S["ors_done"], 2 * a + 1)
                    A.activation(a5[:, :], a5[:, :], ACT.Exp, scale=-0.5).then_inc(S["ors_done"], 1)
                if M_:
                    rstd_exp("2", m, m3)
                if L_:
                    rstd_exp("4", l, f3)
                if F_:
                    gelu1(f, 0)
                    gelu1(f, 1)
                if M_:
                    act.wait_ge(S["x2"], m + 1)
                    act.wait_ge(S["lru_proj"], 2 * m + 1)
                    A.activation(m1[:, :], bank[0][:, :], ACT.Tanh, scale=0.5).then_inc(S["lru_t"], 1)
                    act.wait_ge(S["lru_proj"], 2 * m + 2)
                    A.activation(m2[:, :], bank[1][:, :], ACT.Tanh, scale=0.5).then_inc(S["lru_t"], 1)
                if A_:
                    square("1", a, a1, a2)
                if A_ or M_:
                    A.preload_act_table_set(LN_EXP)
                if M_:
                    act.wait_ge(S["lru_t"], 2 * m + 2)
                    A.activation(m4[:, :], m2[:, :], ACT.Exp, scale=spv[:, 11:12], bias=spv[:, 11:12])\
                        .then_inc(S["lru_a"], 1)
                    A.activation(m3[:, :], m2[:, :], ACT.Exp, scale=spv[:, 10:11], bias=spv[:, 10:11])\
                        .then_inc(S["lru_a"], 1)
                    act.wait_ge(S["lru_m"], m + 1)
                    A.activation(m4[:, :], m4[:, :], ACT.Ln, scale=-1.0).then_inc(S["lru_l"], 1)
                    act.wait_ge(S["lru_l"], m + 1)
                    A.activation(m4[:, :], m4[:, :], ACT.Exp, scale=0.5).then_inc(S["lru_mult"], 1)
                if A_:
                    rstd_ln("1", a, 3, a4)
                    rstd_exp("1", a, a4)
                if F_:
                    gelu1(f, 2)
                    gelu1(f, 3)
                if M_:
                    square("3", m, m1, m2)
                if F_:
                    gelu2(f, 0)
                    gelu2(f, 1)
                if A_:
                    act.wait_ge(S["tk3"], a + 1)
                    A.activation(gw[:, :, 0], gw[:, :, 1], ACT.Tanh, scale=0.5).then_inc(S["th_done"], 1)
                if M_:
                    A.preload_act_table_set(LN_EXP)
                    rstd_ln("3", m, 1, m3)
                    rstd_exp("3", m, m3)
                if F_:
                    gelu2(f, 2)
                    gelu2(f, 3)

            schedule(act, dense, tails)

        @block.gpsimd
        def _(pool):
            for name, n in CREDIT.items():
                pool.sem_inc(S[name], n)
            pool.wait_ge(S["cst_in"], 16)

            def stage1(t, s):
                for g in range(2):
                    pool.wait_ge(*after("kq_done", 2 * t + 1))
                    pool.wait_ge(*after("gram_done", 2 * t + g - 1))
                    G.tensor_tensor(kspread[g][:, :, :, :], rep(pks[s][:, g * 8:(g + 1) * 8, SK:SK + 1, :], 2, NH),
                                    heads(8), ALU.mult).then_inc(S["kexp_done"], 1)
                pool.wait_ge(S["ws_hi"], t + 1)
                cs = bass.ds(t * WCH, WCH)
                G.tensor_tensor(wfl[:, cs], ws[:, :], f32(wfh[:, cs]), ALU.subtract).then_inc(S["ws_lo"], 1)

            tiles_of_stage1(pool, stage1)
            pool.wait_ge(S["kkt_read"], 8)
            pool.wait_ge(S["tinit"], 2)
            for j in range(C - 1):
                n, k = C - 1 - j, j + 1
                a = rep(apm[:, j, 3:4, j + 1:C].rearrange("p h (i o) -> p h i o", o=1), 3, k)
                r = rep(tpm[:, 3:4, j:j + 1, 0:k], 2, n)
                m = tmpg[:, 0:n * k].rearrange("p (h i k) -> p h i k", h=1, i=n)
                if j:
                    pool.wait_ge(S["tg_step"], j)
                G.tensor_tensor(m, a, r, ALU.mult).then_inc(S["tg_mul"], 1)
                pool.wait_ge(S["tg_mul"], j + 1)
                o = tpm[:, 3:4, j + 1:C, 0:k]
                G.tensor_tensor(o, o, m, ALU.subtract).then_inc(S["tg_step"], 1)
            pool.wait_ge(S["wm_hi"], 2)
            G.tensor_tensor(wml[:, :], stg[:, :], f32(wmh[:, :]), ALU.subtract).then_inc(S["wm_lo"], 1)

            def t_spread(a, n):
                if isinstance(a, int) and a == 0:
                    pool.wait_ge(S["tt_read"], 8)
                    src = ttc[:, 0:CT, :].rearrange("p (b n) c -> p b n c", b=B)
                else:
                    pool.wait_ge(S["tb_in"], 16 * a)
                    src = tb
                pool.wait_ge(*after("m2_done", CN * a + max(n - 1, 0)))
                G.tensor_tensor(texp[:, n % 2, :, :, :], rep(src[:, :, n:n + 1, :], 2, NH), heads(B), ALU.mult)\
                    .then_inc(S["texp_ready"], 1)

            def dense(m, a, f):
                for e in range(E):
                    if m is not None:
                        k = E * m + e
                        pool.wait_ge(S["hi1"], k + 1)
                        s = (e % 2) * HC + 1
                        G.tensor_tensor(fbl[:, s, :], hf[:, 1, :], f32(fbh[:, s, :]), ALU.subtract)\
                            .then_inc(S["lo1"], 1)
                        if e:
                            pool.wait_ge(*after("yg_ready", k))
                            if e == 1:
                                pool.wait_ge(*after("y2", m))
                            else:
                                pool.wait_ge(*after("acc_ready", (E - 1) * m + e - 1))
                            G.tensor_tensor(acc[:, :], (x1 if e == 1 else acc)[:, :], yg[:, (e - 1) % 2, :], ALU.add)\
                                .then_inc(S["acc_ready"], 1)
                    if a is not None and e in (1, 3):
                        t_spread(a, e // 2 + 2)

            def tails(f, m, a, l):
                if f is not None:
                    for c in range(FC):
                        pool.wait_ge(S["glu_hi"], FC * f + c + 1)
                        G.tensor_tensor(fal[:, c, :], hf[:, c % 2, :], f32(fah[:, c, :]), ALU.subtract)\
                            .then_inc(S["fa_ready"], 1)
                    for o in range(FC):
                        pool.wait_ge(S["h1_hi"], FC * f + o + 1)
                        G.tensor_tensor(fbl[:, o, :], hf[:, o % 2, :], f32(fbh[:, o, :]), ALU.subtract)\
                            .then_inc(S["fb_ready"], 1)
                if a is not None and (not isinstance(a, int) or a < NT - 1):
                    t_spread(a + 1, 0)
                    t_spread(a + 1, 1)
                if f is not None:
                    for o in range(FC):
                        pool.wait_ge(S["h2_hi"], FC * f + o + 1)
                        G.tensor_tensor(fal[:, o, :], hf[:, o % 2, :], f32(fah[:, o, :]), ALU.subtract)\
                            .then_inc(S["f2_ready"], 1)

            t_spread(0, 0)
            t_spread(0, 1)
            schedule(pool, dense, tails)

        @block.vector
        def _(dve):
            tt, ts, stt = V.tensor_tensor, V.tensor_scalar, V.scalar_tensor_tensor
            dve.wait_ge(S["conv_in"], 32)
            tt(wtap[:, :, :, :], rep(wqkv[:, :, :].rearrange("p m (o n) -> p m o n", o=1), 2, TAPS),
               conv[:, :, :, :], ALU.mult).then_inc(S["wtap_f"], 1)
            dve.wait_ge(S["wtap_hi"], 1)
            tt(wtapl[:, :, :, :], wtap[:, :, :, :], f32(wtaph[:, :, :, :]), ALU.subtract).then_inc(S["wtap_done"], 1)

            def split_x(t, s):
                dve.wait_ge(S["x_in"], 16 * t + 16)
                dve.wait_ge(*after("qkv_proj", 3 * (t - 1)))
                V.tensor_copy(xsh[s][:, :, :], xt[:, :, :]).then_inc(S["xt_hi"], 1)
                dve.wait_ge(S["xt_hi"], t + 1)
                tt(xsl[s][:, :, :], xt[:, :, :], f32(xsh[s][:, :, :]), ALU.subtract).then_inc(S["xt_ready"], 1)

            def stage1(t, s):
                p = pks[s]
                k, q, v = act_kqv[s]
                dve.wait_ge(*after("pk_stored", 16 * (t - 1)))
                dve.wait_ge(*after("gram_done", 2 * (t - 1)))
                for m, src in enumerate((k, q)):
                    dve.wait_ge(*after("rs_act", 2 * t + m + 1))
                    tt(p[:, :, SK + m, :], by_chunk(src[:, :]), by_chunk(rnorm[s][m]), ALU.mult)\
                        .then_inc(S["kq_done"], 1)
                dve.wait_ge(*after("kq_done", 2 * t + 1))
                V.transpose(p[:, :, SKT, :], p[:, :, SK, :]).then_inc(S["qn_done"], 1)
                dve.wait_ge(*after("qkv_act", 3 * t + 3))
                V.transpose(p[:, :, SVT, :], by_chunk(v[:, :])).then_inc(S["kv_tok"], 1)
                V.tensor_copy(p[:, :, SV, :], by_chunk(v[:, :])).then_inc(S["v_done"], 1)
                dve.wait_ge(*after("bt_ready", t + 1))
                V.transpose(yg[:, 0, :], gb[:, 0, :]).then_inc(S["beta_tmp"], 1)
                dve.wait_ge(*after("beta_tmp", t + 1))
                ts(beta_tok[:, bass.ds(t * CT, CT)], yg[:, 0, 0:W:C], 0.5, 0.5, ALU.mult, ALU.add)\
                    .then_inc(S["beta_tok_done"], 1)
                if not isinstance(t, int) or t + 2 < NT:
                    split_x(t + 2, s)
                dve.wait_ge(S["beta_tok_done"], t + 1)
                for g in range(2):
                    bk = bank[6 + g][:, :].rearrange("p (c s i) -> p c s i", c=8, s=2)
                    dve.wait_ge(*after("gram_done", 2 * t + g + 1))
                    tt(p[:, g * 8:(g + 1) * 8, SATT, :], bk[:, :, 1, :],
                       rep(causal.rearrange("p (o i) -> p o i", o=1), 1, 8), ALU.mult)
                    tt(kkc[:, bass.ds(t * CT + g * 8, 8), :], bk[:, :, 0, :],
                       rep(beta_tok[:, bass.ds(t * CT + g * 8, 8)].rearrange("p (c o) -> p c o", o=1), 2, C),
                       ALU.mult).then_inc(S["gram_read"], 1)

            split_x(0, 0)
            split_x(1, 1)
            dve.wait_ge(S["cst_in"], 16)
            V.tensor_copy(sel[0:40, :], cst[0:40, C_SEL:C_SEL + E])
            V.memset(f32(gtT[:, :]), 0.0)
            V.memset(sexp[:, :, :, :], 0.0)
            V.memset(hst[:, :], 0.0).then_inc(S["s_zero"], 1)
            tiles_of_stage1(dve, stage1)
            dve.wait_ge(S["w_in"], 32)
            n_sp = [0]
            ap = vec[:, V_AP:V_AP + 1]

            def sp_op(i):
                i.then_inc(S["sp_step"], 1)
                n_sp[0] += 1
                dve.wait_ge(S["sp_step"], n_sp[0])

            col = lambda k: spv[:, k:k + 1]
            stt(col(0), ap, -1.0, ap, ALU.mult, ALU.max).then_inc(S["sp_step"], 1)
            n_sp[0] = 2
            dve.wait_ge(S["sp_step"], 2)
            sp_op(ts(col(2), col(1), 2.0, None, ALU.add))
            sp_op(V.reciprocal(col(3), col(2)))
            sp_op(tt(col(4), col(1), col(3), ALU.mult))
            sp_op(tt(col(5), col(4), col(4), ALU.mult))
            sp_op(ts(col(6), col(5), 1.0 / 17, 1.0 / 15, ALU.mult, ALU.add))
            for k in (13, 11, 9, 7, 5, 3, 1):
                sp_op(tt(col(7), col(6), col(5), ALU.mult))
                sp_op(ts(col(6), col(7), 1.0 / k, None, ALU.add))
            sp_op(tt(col(7), col(6), col(4), ALU.mult))
            sp_op(ts(col(8), ap, 0.0, None, ALU.max))
            sp_op(stt(col(9), col(7), 2.0, col(8), ALU.mult, ALU.add))
            sp_op(ts(col(10), col(9), -4.0, None, ALU.mult))
            sp_op(ts(col(11), col(9), -8.0, None, ALU.mult))

            dve.wait_ge(S["kkt_done"], 8)
            V.memset(opt[:, :], 0.0).then_inc(S["tinit"], 1)
            dve.wait_ge(S["tinit"], 1)
            for h in range(NH):
                i = V.memset(opt[:, h * C:C * NH * C:NH * C + 1], 1.0)
            i.then_inc(S["tinit"], 1)
            dve.wait_ge(S["kkt_read"], 8)
            dve.wait_ge(S["tinit"], 2)
            for j in range(C - 1):
                n, k = C - 1 - j, j + 1
                a = rep(apm[:, j, 0:3, j + 1:C].rearrange("p h (i o) -> p h i o", o=1), 3, k)
                r = rep(tpm[:, 0:3, j:j + 1, 0:k], 2, n)
                m = tmpv[:, 0:3 * n * k].rearrange("p (h i k) -> p h i k", h=3, i=n)
                if j:
                    dve.wait_ge(S["tv_step"], j)
                tt(m, a, r, ALU.mult).then_inc(S["tv_mul"], 1)
                dve.wait_ge(S["tv_mul"], j + 1)
                o = tpm[:, 0:3, j + 1:C, 0:k]
                tt(o, o, m, ALU.subtract).then_inc(S["tv_step"], 1)
            for g in range(8):
                dve.wait_ge(S["tt_done"], g + 1)
                tt(ttc[:, :, 4 * g:4 * g + 4].rearrange("p c i -> p i c"),
                   bank[g % 2][:, :].rearrange("p (i c) -> p i c", i=4),
                   rep(beta_tok[:, :].rearrange("p (o c) -> p o c", o=1), 1, 4), ALU.mult).then_inc(S["tt_read"], 1)
            def centre(n, t, buf, bk):
                dve.wait_ge(S["mu" + n], t + 1)
                tt(buf[:, :], buf[:, :], bank[bk][:, :], ALU.subtract).then_inc(S["d" + n], 1)

            def scale(n, t, buf, rs, out):
                dve.wait_ge(*after("rs" + n, 2 * t + 2) if n in "34" else (S["rs" + n], 2 * t + 2))
                return tt(out[:, :], buf[:, :], rs[:, :], ALU.mult)

            def delta_spread(t, n):
                k = CN * t + n
                dve.wait_ge(*after("m2_done", k + 1))
                dve.wait_ge(*after("os_done", k))
                tt(spread[:, :, :, :], rep(bank[0][:, 0:256].rearrange("p (s o c) -> p s o c", s=8, o=1), 2, NH),
                   heads(8), ALU.mult).then_inc(S["wu_ready"], 1)

            def delta_qp(t, n):
                k = CN * t + n
                dve.wait_ge(S["m4_done"], k + 1)
                bk = bank[1][:, 0:256].rearrange("p (b s c) -> p b s c", b=B, s=2)
                tt(qpc[:, :, 0, :], pk[:, n:CT:CN, SQ, :], bk[:, :, 0, :], ALU.subtract).then_inc(S["qp_step"], 1)
                tt(qpc[:, :, 1, :], rep(eye.rearrange("p (o c) -> p o c", o=1), 1, B), bk[:, :, 1, :],
                   ALU.subtract).then_inc(S["qp_step"], 1)

            def delta_out(t, n):
                k = CN * t + n
                dve.wait_ge(*after("os_done", k + 1))
                ob = bank[2][:, 0:256].rearrange("p (b s c) -> p b s c", b=B, s=2)
                for h in range(NH):
                    i = V.transpose(sexp[32 * h:32 * h + 32, :, h, :], ob[32 * h:32 * h + 32, :, 1, :])
                i.then_inc(S["s_ready"], 1)
                V.tensor_copy(oT[:, :].rearrange("p (b n c) -> p b n c", b=B, n=CN)[:, :, n, :], ob[:, :, 0, :])\
                    .then_inc(S["o_copied"], 1)

            def gated(m, e):
                k = E * m + e
                dve.wait_ge(*after("dn_done", k + 1))
                dve.wait_ge(*after("gb_ready", k + 1))
                dve.wait_ge(*after("acc_ready", (E - 1) * m + max(e - 1, 0)))
                tt(yg[:, e % 2, :], bank[6][:, :], gb[:, e % 2, :], ALU.mult).then_inc(S["yg_ready"], 1)

            def dense(m, a, f):
                if a is not None:
                    delta_spread(a, 0)
                for e in range(E):
                    if m is not None:
                        k = E * m + e
                        s = (e % 2) * HC
                        dve.wait_ge(*after("gelu_done", 3 * k + 2))
                        dve.wait_ge(*after("dn_done", E * m + max(e - 1, 0)))
                        tt(fbl[:, s, :], hf[:, 0, :], f32(fbh[:, s, :]), ALU.subtract).then_inc(S["lo0"], 1)
                        dve.wait_ge(*after("gelu_done", 3 * k + 3))
                        V.tensor_copy(fbh[:, s + 1, :], hf[:, 1, :]).then_inc(S["hi1"], 1)
                    if a is not None:
                        (delta_out if e % 2 else delta_qp)(a, e // 2)
                    if e == 0 and f is not None:
                        dve.wait_ge(*after("w3_done", f + 1))
                        dve.wait_ge(*after("out_stored", 16 * f))
                        stt(f1[:, :], bank[6][:, :], vec[:, V_S3:V_S3 + 1], x3[:, :], ALU.mult, ALU.add)\
                            .then_inc(S["y4"], 1)
                    if e == 0:
                        x = m - 1 if m is not None else f + 1 if f is not None else NT
                        if not isinstance(x, int) or 0 <= x < NT:
                            if f is not None:
                                dve.wait_ge(*after("y4", f + 1))
                            scale("3", x, m1, m3, x3).then_inc(S["x3_hi"], 1)
                            dve.wait_ge(S["x3_hi"], 2 * x + 1)
                            V.tensor_copy(x3h[:, :], x3[:, :]).then_inc(S["x3_hi"], 1)
                            dve.wait_ge(S["x3_hi"], 2 * x + 2)
                            tt(x3l[:, :], x3[:, :], f32(x3h[:, :]), ALU.subtract).then_inc(S["x3_ready"], 1)
                    if e == 2 and f is not None:
                        centre("4", f, f1, 3)
                    if m is not None and e:
                        gated(m, e - 1)
                    if a is not None and e % 2 and e < E - 1:
                        delta_spread(a, e // 2 + 1)
                if a is not None:
                    vT = pk[:, :, SV, :]
                    dve.wait_ge(*after("o_copied", CN * a + CN))
                    tt(by_chunk(a3[:, :]), by_chunk(oT[:, :]), vT, ALU.subtract).then_inc(S["mix_o"], 1)
                    dve.wait_ge(*after("mix_act", a + 1))
                    dve.wait_ge(S["mix_o"], 2 * a + 1)
                    stt(a3[:, :], a4[:, :], 1.0, a3[:, :], ALU.add, ALU.mult).then_inc(S["mix_o"], 1)
                    dve.wait_ge(S["mix_o"], 2 * a + 2)
                    stt(by_chunk(a1[:, :]), by_chunk(a3[:, :]), 0.5, vT, ALU.mult, ALU.add).then_inc(S["o_ready"], 1)
                if m is not None:
                    gated(m, E - 1)
                    dve.wait_ge(*after("acc_ready", (E - 1) * (m + 1)))
                    dve.wait_ge(*after("yg_ready", E * (m + 1)))
                    tt(m1[:, :], acc[:, :], yg[:, (E - 1) % 2, :], ALU.add).then_inc(S["y2"], 1)

            def tails(f, m, a, l):
                F_, M_, A_, L_ = f is not None, m is not None, a is not None, l is not None

                def glu(c):
                    k = FC * f + c
                    dve.wait_ge(*after("g_act", k + 1))
                    dve.wait_ge(S["u_done"], k + 1)
                    if c == 0:
                        dve.wait_ge(*after("lo1", E * (f + 2 if M_ else NT)))
                    dve.wait_ge(*after("fa_ready", FC * f + max(c - 1, 0)))
                    stt(hf[:, c % 2, :], bank[5 + 2 * (c % 2)][:, :], vec[:, V_S2 + c:V_S2 + c + 1],
                        gb[:, c % 2, :], ALU.mult, ALU.mult).then_inc(S["glu_f"], 1)
                    dve.wait_ge(*after("glu_f", k + 1))
                    V.tensor_copy(fah[:, c, :], hf[:, c % 2, :]).then_inc(S["glu_hi"], 1)

                def hi(o, acted, done, dst, used, n):
                    dve.wait_ge(S[acted], FC * f + o + 1)
                    dve.wait_ge(*after(used, n))
                    V.tensor_copy(dst[:, o, :], hf[:, o % 2, :]).then_inc(S[done], 1)

                def hi1(o):
                    if F_:
                        hi(o, "h1_act", "h1_hi", fbh, "h2_done", FC * f)

                def hi2(o):
                    if F_:
                        hi(o, "h2_act", "h2_hi", fah, "h1_done", FC * f + FC)

                if F_:
                    glu(0)
                if M_:
                    centre("2", m, m1, 0)
                if F_:
                    glu(1)
                    glu(2)
                    glu(3)
                if A_:
                    dve.wait_ge(S["ors_done"], 2 * a + 2)
                    stt(a3[:, :], a1[:, :], vec[:, V_NORM:V_NORM + 1], a5[:, :], ALU.mult, ALU.mult)\
                        .then_inc(S["og_done"], 1)
                if M_:
                    scale("2", m, m1, m3, x2).then_inc(S["x2"], 1)
                if L_:
                    scale("4", l, f1, f3, f1).then_inc(S["x4"], 1)
                hi1(0)
                hi1(1)
                if A_:
                    dve.wait_ge(S["wo_done"], a + 1)
                    tt(by_seq(a1[:, :]), by_seq(bank[3][:, :]), xv, ALU.add).then_inc(S["y1"], 1)
                    centre("1", a, a1, 2)
                if M_:
                    dve.wait_ge(S["lru_t"], 2 * m + 1)
                    stt(m1[:, :], m1[:, :], 1.0, x2[:, :], ALU.add, ALU.mult).then_inc(S["lru_gx"], 1)
                    dve.wait_ge(S["lru_a"], 2 * m + 1)
                    ts(m4[:, :], m4[:, :], 1.0, -1e-19, ALU.subtract, ALU.min).then_inc(S["lru_m"], 1)
                    dve.wait_ge(S["lru_mult"], m + 1)
                    dve.wait_ge(S["lru_gx"], m + 1)
                    stt(m1[:, :], m1[:, :], 0.5, m4[:, :], ALU.mult, ALU.mult).then_inc(S["lru_b"], 1)
                    dve.wait_ge(S["lru_b"], m + 1)
                    dve.wait_ge(*after("hst_ready", m))
                    for b in range(B):
                        c = slice(b * TOK, (b + 1) * TOK)
                        i = V.tensor_tensor_scan(m2[:, c], m3[:, c], m1[:, c], hst[:, b:b + 1], ALU.mult, ALU.add)
                    i.then_inc(S["lru_scan"], 1)
                    dve.wait_ge(S["lru_scan"], m + 1)
                    V.tensor_copy(hst[:, :], m2[:, TOK - 1:W:TOK]).then_inc(S["hst_ready"], 1)
                    tt(m1[:, :], m2[:, :], x2[:, :], ALU.add).then_inc(S["y3"], 1)
                if A_:
                    dve.wait_ge(*after("gelu_done", 3 * E * a))
                    scale("1", a, a1, a4, x1).then_inc(S["x1_hi"], 1)
                    dve.wait_ge(S["x1_hi"], 2 * a + 1)
                    V.tensor_copy(x1h[:, :], x1[:, :]).then_inc(S["x1_hi"], 1)
                    dve.wait_ge(S["x1_hi"], 2 * a + 2)
                    tt(x1l[:, :], x1[:, :], f32(x1h[:, :]), ALU.subtract).then_inc(S["x1"], 1)
                hi1(2)
                if M_:
                    centre("3", m, m1, 0)
                hi1(3)
                if A_:
                    dve.wait_ge(S["r_done"], a + 1)
                    V.tensor_copy(lg[:, :, :], bank[2][:, 0:B * E].rearrange("p (b e) -> p b e", b=B))\
                        .then_inc(S["lg_ready"], 1)
                    dve.wait_ge(*after("lg_ready", a + 1))
                    V.memset(mf[:, :, :], 0.0)
                    for b in range(B):
                        i = V.max(mx[:, b, :], lg[:, b, :])
                    i.then_inc(S["tk1"], 1)
                    dve.wait_ge(S["tk1"], a + 1)
                    tt(gw[:, :, 1], mx[:, :, 0], mx[:, :, 1], ALU.subtract).then_inc(S["tk3"], 1)
                    for b in range(B):
                        i = V.max_index(mi[:, b, :], mx[:, b, :], lg[:, b, :])
                    i.then_inc(S["tk2"], 1)
                    dve.wait_ge(S["tk2"], a + 1)
                    V.tensor_copy(mf[:, :, :], mi[:, :, 0:2]).then_inc(S["tk4"], 1)
                    dve.wait_ge(S["tk4"], a + 1)
                    for s in range(2):
                        i = tt(gt2[:, :, s, :], rep(iota[:, :].rearrange("p (o e) -> p o e", o=1), 1, B),
                               rep(mf[:, :, s:s + 1], 2, E), ALU.is_equal)
                    i.then_inc(S["tk5"], 1)
                hi2(0)
                hi2(1)
                if A_:
                    dve.wait_ge(S["th_done"], a + 1)
                    ts(gw[:, :, 1], gw[:, :, 0], -0.5, 0.5, ALU.mult, ALU.add).then_inc(S["tk6"], 1)
                    dve.wait_ge(S["tk6"], 2 * a + 1)
                    ts(gw[:, :, 0], gw[:, :, 0], 0.5, 0.5, ALU.mult, ALU.add).then_inc(S["tk6"], 1)
                    dve.wait_ge(S["tk6"], 2 * a + 2)
                    dve.wait_ge(S["tk5"], a + 1)
                    for s in range(2):
                        i = tt(gt2[:, :, s, :], gt2[:, :, s, :], rep(gw[:, :, s:s + 1], 2, E), ALU.mult)
                    i.then_inc(S["tk7"], 1)
                    dve.wait_ge(S["tk7"], a + 1)
                    tt(gate[:, :, :], gt2[:, :, 0, :], gt2[:, :, 1, :], ALU.add).then_inc(S["gate_ready"], 1)
                hi2(2)
                hi2(3)
                if A_:
                    dve.wait_ge(S["gtp_done"], a + 1)
                    V.tensor_copy(gtT[0:E, :], bank[3][0:E, :]).then_inc(S["gt_hi"], 1)
                    dve.wait_ge(S["gt_hi"], a + 1)
                    tt(gtT[32:32 + E, :], bank[3][0:E, :], f32(gtT[0:E, :]), ALU.subtract).then_inc(S["gt_ready"], 1)

            schedule(dve, dense, tails)


def _layout(a):
    f = lambda n: np.asarray(a[n], dtype=np.float32)
    T = lambda m: np.ascontiguousarray(m.T)
    x = f("L0_attn_hidden_states")
    xp = np.pad(x, ((0, 0), (HALO, 0), (0, 0)))
    xh = np.stack([xp[b, t * TOK:t * TOK + TOK + HALO].T for t in range(NT) for b in range(B)], axis=1)
    order = ("k", "q", "v")
    wqkv = np.stack([f(f"L0_attn_W{m}").T for m in order], axis=1)
    conv = np.stack([np.broadcast_to(f(f"L0_attn_conv_{m}").T[None], (128, TAPS, 128)) for m in order], axis=1)
    rep = lambda m: np.repeat(m, DK, axis=0).T

    def blocks(w):
        out = np.zeros((128, 128), np.float32)
        s = w.shape[1]
        for h in range(w.shape[0]):
            out[h * s:(h + 1) * s, h * s:(h + 1) * s] = w[h]
        return out

    wsm = np.stack([rep(f("L0_attn_Wb")), rep(f("L0_attn_Wmix")), f("L0_attn_Wo").T,
                    blocks(f("L1_attn_w_in")), blocks(f("L1_attn_w_a"))], axis=1)
    p = np.arange(128)
    cst = np.zeros((128, N_CONST), np.float32)
    cst[:, C_ID:C_ID + 128] = np.eye(128)
    cst[:, C_MEAN:C_MEAN + 128] = 1.0 / D
    cst[:, C_HEAD:C_HEAD + 128] = (p[:, None] // DK) == (p[None] // DK)
    cst[:, C_CAUSAL:C_CAUSAL + 32] = np.arange(32)[None] >= (p[:, None] % 32)
    cst[:, C_EYE:C_EYE + 32] = np.arange(32)[None] == (p[:, None] % 32)
    for e in range(E):
        cst[[e, 32 + e], C_SEL + e] = 1.0
    vec = np.zeros((128, N_VEC), np.float32)
    cols = lambda v: v.reshape(-1, 128).T
    vec[:, V_S1:V_S1 + FC] = cols(f("L1_ffn_w1_s"))
    vec[:, V_S2:V_S2 + FC] = cols(f("L1_ffn_w2_s"))
    vec[:, V_HS1:V_HS1 + FC] = cols(f("L1_ffn_h1_s"))
    vec[:, V_HS2:V_HS2 + FC] = cols(f("L1_ffn_h2_s"))
    vec[:, V_S3:V_S3 + 1] = cols(f("L1_ffn_w3_s"))
    vec[:, V_NORM] = np.tile(f("L0_attn_norm_w"), NH)
    vec[:, V_AP] = f("L1_attn_a_param")
    vec[:, V_EPS] = LN_EPS
    vec[:, V_L2E] = L2_EPS
    w1 = f("L0_ffn_w1").transpose(2, 0, 1).reshape(128, E * HID)
    w2 = f("L0_ffn_w2").reshape(E, 128, HC, 128).transpose(3, 0, 2, 1).reshape(128, E * HC * 128)
    kc = lambda w: w.T.reshape(FC, 128, -1).transpose(1, 0, 2)
    ins = dict(xh=xh, wqkv=wqkv, conv=conv, wsm=wsm, cst=cst, vec=vec, wr=f("L0_ffn_router_w").T, wm=np.concatenate([w1, w2], axis=1),
               wf=np.concatenate([m.reshape(128, -1) for m in (
                   f("L1_ffn_w1_w").T, f("L1_ffn_w2_w").T, kc(f("L1_ffn_h1_w")), kc(f("L1_ffn_h2_w")),
                   kc(f("L1_ffn_w3_w")))], axis=1), iota=np.broadcast_to(np.arange(E, dtype=np.float32), (128, E)))
    return {n: np.ascontiguousarray(v) for n, v in ins.items()}


def program(nc, ins):
    io = {n: nc.dram_tensor(f"in_{n}", v.shape, F32, kind="ExternalInput").ap() for n, v in ins.items()}
    io["out"] = nc.dram_tensor("out_0", (128, NT * W), F32, kind="ExternalOutput").ap()
    io["pack"] = nc.dram_tensor("pack", (128, NC, NPACK - 1, C), F32, kind="Internal").ap()
    io["tt"] = nc.dram_tensor("tt", (128, NC, C), F32, kind="Internal").ap()
    build(nc, io)


def kernel(**inputs):
    import concourse.bacc as bacc
    from concourse.bass_utils import run_bass_kernel_spmd

    ins = _layout(inputs)
    nc = bacc.Bacc("TRN2", target_bir_lowering=False, num_devices=1)
    program(nc, ins)
    r = run_bass_kernel_spmd(nc, [{f"in_{n}": v for n, v in ins.items()}], core_ids=[0])
    out = r.results[0]["out_0"]
    return out.reshape(128, NT, B, TOK).transpose(2, 1, 3, 0).reshape(B, L, D)
```
